# Optimizing a Trainium2 kernel written in Bass

```python
import numpy as np
import jax
import jax.numpy as jnp

def _softmax(x, axis=-1):
    return jax.nn.softmax(x, axis=axis)

def _gelu(x):
    return jax.nn.gelu(x, approximate=True)

def _silu(x):
    return jax.nn.silu(x)

def _sigmoid(x):
    return jax.nn.sigmoid(x)

def _layernorm(x, axis=-1, eps=1e-05):
    m = jnp.mean(x, axis=axis, keepdims=True)
    v = jnp.var(x, axis=axis, keepdims=True)
    return (x - m) / jnp.sqrt(v + eps)

def _scatter_add(tgt, idx, src, axis=0):
    return tgt.at[idx].add(src)

def _segment_sum(src, seg, n):
    return jax.ops.segment_sum(src, seg, n)
kernel_name = 'mk_adaln_d1_jaxref_r8_d476bd'

def setup_inputs(seed: int=0):
    np.random.seed(seed)
    _w = jnp.asarray

    def _L0_attn_setup():
        import jax, jax.numpy as jnp
        import numpy as np
        B, N, DIM = (2, 256, 128)
        H, DH = (16, 64)
        EPS = 1e-12

        def _l2norm(t):
            n = jnp.sqrt(jnp.sum(t * t, axis=-1, keepdims=True))
            return t / jnp.maximum(n, EPS)
        key = jax.random.key(seed)
        ks = jax.random.split(key, 8)
        inner = H * DH
        s = 0.02
        return {'x': jax.random.normal(ks[0], (B, N, DIM), dtype=jnp.float32), 'Wq': jax.random.normal(ks[1], (inner, DIM), dtype=jnp.float32) * s, 'Wk': jax.random.normal(ks[2], (inner, DIM), dtype=jnp.float32) * s, 'Wv': jax.random.normal(ks[3], (inner, DIM), dtype=jnp.float32) * s, 'Wo': jax.random.normal(ks[4], (DIM, inner), dtype=jnp.float32) * s, 'bo': jnp.zeros((DIM,), dtype=jnp.float32), 'q_scale': jnp.ones((H, 1, DH), dtype=jnp.float32), 'k_scale': jnp.ones((H, 1, DH), dtype=jnp.float32)}
    _L0_attn_in = _L0_attn_setup()

    def _L0_ffn_setup():
        import jax, jax.numpy as jnp
        import numpy as np
        import math
        B, T, C = (4, 256, 128)
        E, K = (8, 2)
        EH, SH = (256, 512)
        CAP_FACTOR = 1.25
        SCALING = 1.0
        FC_MULT = 1.0

        def _capacity(N, k):
            avg = math.ceil(N * k / E)
            return max(int(math.ceil(avg * CAP_FACTOR)), 1)
        key = jax.random.key(seed)
        ks = jax.random.split(key, 6)
        sd = 0.02
        return {'x': jax.random.normal(ks[0], (B, T, C), jnp.float32), 'proj_w': jax.random.normal(ks[1], (E, C), jnp.float32) * sd, 'proj_b': jnp.zeros((E,), jnp.float32), 'expert_bias': jnp.zeros((E,), jnp.float32), 'fc1_w': jax.random.normal(ks[2], (E, EH, C), jnp.float32) * sd, 'fc1_b': jnp.zeros((E, EH), jnp.float32), 'fc2_w': jax.random.normal(ks[3], (E, C, EH), jnp.float32) * sd, 'fc2_b': jnp.zeros((E, C), jnp.float32), 'sh1_w': jax.random.normal(ks[4], (SH, C), jnp.float32) * sd, 'sh1_b': jnp.zeros((SH,), jnp.float32), 'sh2_w': jax.random.normal(ks[5], (C, SH), jnp.float32) * sd, 'sh2_b': jnp.zeros((C,), jnp.float32)}
    _L0_ffn_in = _L0_ffn_setup()
    _L0_c = _w((lambda *s: np.random.randn(*s).astype(np.float32) * 0.05)(8, 128))
    _L0_wmod = _w((lambda *s: np.random.randn(*s).astype(np.float32) * 0.05)(128, 6 * 128) * 128 ** (-0.5))
    _d = {'L0_attn_x': _L0_attn_in['x'], 'L0_attn_Wq': _L0_attn_in['Wq'], 'L0_attn_Wk': _L0_attn_in['Wk'], 'L0_attn_Wv': _L0_attn_in['Wv'], 'L0_attn_Wo': _L0_attn_in['Wo'], 'L0_attn_bo': _L0_attn_in['bo'], 'L0_attn_q_scale': _L0_attn_in['q_scale'], 'L0_attn_k_scale': _L0_attn_in['k_scale'], 'L0_ffn_proj_w': _L0_ffn_in['proj_w'], 'L0_ffn_proj_b': _L0_ffn_in['proj_b'], 'L0_ffn_expert_bias': _L0_ffn_in['expert_bias'], 'L0_ffn_fc1_w': _L0_ffn_in['fc1_w'], 'L0_ffn_fc1_b': _L0_ffn_in['fc1_b'], 'L0_ffn_fc2_w': _L0_ffn_in['fc2_w'], 'L0_ffn_fc2_b': _L0_ffn_in['fc2_b'], 'L0_ffn_sh1_w': _L0_ffn_in['sh1_w'], 'L0_ffn_sh1_b': _L0_ffn_in['sh1_b'], 'L0_ffn_sh2_w': _L0_ffn_in['sh2_w'], 'L0_ffn_sh2_b': _L0_ffn_in['sh2_b'], 'L0_c': _L0_c, 'L0_wmod': _L0_wmod}
    _x0 = _d['L0_attn_x']
    _d['L0_attn_x'] = jax.random.normal(jax.random.fold_in(jax.random.key(seed), 1), (8, 512, 128), dtype=_x0.dtype)
    del _x0
    return _d

def reference(L0_attn_x, L0_attn_Wq, L0_attn_Wk, L0_attn_Wv, L0_attn_Wo, L0_attn_bo, L0_attn_q_scale, L0_attn_k_scale, L0_ffn_proj_w, L0_ffn_proj_b, L0_ffn_expert_bias, L0_ffn_fc1_w, L0_ffn_fc1_b, L0_ffn_fc2_w, L0_ffn_fc2_b, L0_ffn_sh1_w, L0_ffn_sh1_b, L0_ffn_sh2_w, L0_ffn_sh2_b, L0_c, L0_wmod):

    def _L0_attn_ref(x, Wq, Wk, Wv, Wo, bo, q_scale, k_scale):
        import jax, jax.numpy as jnp
        import numpy as np
        B, N, DIM = (2, 256, 128)
        H, DH = (16, 64)
        EPS = 1e-12

        def _l2norm(t):
            n = jnp.sqrt(jnp.sum(t * t, axis=-1, keepdims=True))
            return t / jnp.maximum(n, EPS)
        b, n, _ = x.shape
        q = jnp.einsum('bnd,ed->bne', x, Wq).reshape(b, n, H, DH).transpose(0, 2, 1, 3)
        k = jnp.einsum('bnd,ed->bne', x, Wk).reshape(b, n, H, DH).transpose(0, 2, 1, 3)
        v = jnp.einsum('bnd,ed->bne', x, Wv).reshape(b, n, H, DH).transpose(0, 2, 1, 3)
        q = _l2norm(q) * q_scale
        k = _l2norm(k) * k_scale
        attn = jnp.einsum('bhid,bhjd->bhij', q, k) * DH ** (-0.5)
        attn = jax.nn.softmax(attn, axis=-1)
        out = jnp.einsum('bhij,bhjd->bhid', attn, v)
        out = out.transpose(0, 2, 1, 3).reshape(b, n, H * DH)
        return jnp.einsum('bne,de->bnd', out, Wo) + bo

    def _L0_ffn_ref(x, proj_w, proj_b, expert_bias, fc1_w, fc1_b, fc2_w, fc2_b, sh1_w, sh1_b, sh2_w, sh2_b):
        import jax, jax.numpy as jnp
        import numpy as np
        import math
        B, T, C = (4, 256, 128)
        E, K = (8, 2)
        EH, SH = (256, 512)
        CAP_FACTOR = 1.25
        SCALING = 1.0
        FC_MULT = 1.0

        def _capacity(N, k):
            avg = math.ceil(N * k / E)
            return max(int(math.ceil(avg * CAP_FACTOR)), 1)
        Bx, Tx, Cx = x.shape
        N = Bx * Tx
        xf = x.reshape(N, Cx)
        z = xf @ proj_w.T + proj_b
        s = jax.nn.sigmoid(z) + expert_bias
        logits = jnp.log(jnp.clip(s, 1e-12)) * SCALING
        probs = jax.nn.softmax(logits, axis=-1)
        topk_w, topk_idx = jax.lax.top_k(probs, K)
        topk_w = topk_w / jnp.clip(topk_w.sum(-1, keepdims=True), 1e-12)
        pair_e = topk_idx.reshape(-1)
        pair_w = topk_w.reshape(-1)
        pair_tok = jnp.repeat(jnp.arange(N), K)
        cap = _capacity(N, K)
        assigned = pair_e[None, :] == jnp.arange(E)[:, None]
        wmat = jnp.where(assigned, pair_w[None, :], -jnp.inf)
        kept_w, kept_pair = jax.lax.top_k(wmat, cap)
        valid = kept_w > -jnp.inf
        kept_w = jnp.where(valid, kept_w, 0.0)
        kept_tok = pair_tok[kept_pair]
        xe = xf[kept_tok]
        h = jax.nn.gelu(jnp.einsum('ecd,ehd->ech', xe, fc1_w) + fc1_b[:, None, :], approximate=False)
        oe = jnp.einsum('ech,edh->ecd', h, fc2_w) + fc2_b[:, None, :]
        contrib = oe * kept_w[..., None]
        y = jnp.zeros((N, Cx), x.dtype).at[kept_tok.reshape(-1)].add(contrib.reshape(-1, Cx))
        sh = jax.nn.gelu(xf @ sh1_w.T + sh1_b, approximate=False) @ sh2_w.T + sh2_b
        return ((sh + y) * FC_MULT).reshape(Bx, Tx, Cx)
    x = L0_attn_x
    mod = (_silu(L0_c) @ L0_wmod).reshape(L0_c.shape[0], 6, 1, -1)
    sa, ca, ga, sb, cb, gb = (mod[:, 0], mod[:, 1], mod[:, 2], mod[:, 3], mod[:, 4], mod[:, 5])
    ga = (2 * (ga >= 0) - 1) * jnp.maximum(jnp.abs(ga), 0.25)
    gb = (2 * (gb >= 0) - 1) * jnp.maximum(jnp.abs(gb), 0.25)
    h = _layernorm(x, axis=-1) * (1 + ca) + sa
    x = x + ga * _L0_attn_ref(h, L0_attn_Wq, L0_attn_Wk, L0_attn_Wv, L0_attn_Wo, L0_attn_bo, L0_attn_q_scale, L0_attn_k_scale)
    h = _layernorm(x, axis=-1) * (1 + cb) + sb
    x = x + gb * _L0_ffn_ref(h, L0_ffn_proj_w, L0_ffn_proj_b, L0_ffn_expert_bias, L0_ffn_fc1_w, L0_ffn_fc1_b, L0_ffn_fc2_w, L0_ffn_fc2_b, L0_ffn_sh1_w, L0_ffn_sh1_b, L0_ffn_sh2_w, L0_ffn_sh2_b)
    return x

_drawn_inputs = setup_inputs


def setup_inputs(seed=0):
    import zlib

    import numpy as np

    out = dict(_drawn_inputs(seed))
    spreads = {'L0_attn_bo': (0.0, 0.322),
     'L0_attn_q_scale': (1.0, 0.6),
     'L0_attn_k_scale': (1.0, 0.6),
     'L0_ffn_proj_b': (0.0, 0.8),
     'L0_ffn_expert_bias': (0.0, 0.482),
     'L0_ffn_fc1_b': (0.0, 0.8),
     'L0_ffn_fc2_b': (0.0, 0.632),
     'L0_ffn_sh1_b': (0.0, 0.8),
     'L0_ffn_sh2_b': (0.0, 0.362)}
    factors = {'L0_attn_Wq': 8.0,
     'L0_attn_Wk': 8.0,
     'L0_attn_Wv': 8.0,
     'L0_attn_Wo': 8.0,
     'L0_ffn_proj_w': 4.628,
     'L0_ffn_fc1_w': 8.0,
     'L0_ffn_fc2_w': 8.0,
     'L0_ffn_sh1_w': 4.223,
     'L0_ffn_sh2_w': 3.836}
    for name, (base, spread) in spreads.items():
        noise = np.random.default_rng([zlib.crc32(name.encode()), seed]).standard_normal(out[name].shape)
        drawn = base * np.exp(spread * noise) if base else spread * noise
        out[name] = jnp.asarray(drawn.astype(out[name].dtype))
    for name, factor in factors.items():
        out[name] = (out[name] * factor).astype(out[name].dtype)
    return out
```

```python
from contextlib import ExitStack

import concourse.bass as bass
from concourse import mybir

P = 128
ALU = mybir.AluOpType
ACT = mybir.ActivationFunctionType
AX = mybir.AxisListType
F32 = mybir.dt.float32
F32R = mybir.dt.float32r
I32 = mybir.dt.int32
U32 = mybir.dt.uint32

LN_EPS = 1e-5
NORM_EPS = 1e-12
CLIP = 1e-12
MIN_GATE = 0.25
EXPERTS_PER_TOKEN = 2
CAP_NUM, CAP_DEN = 5, 4
RSQRT_MAGIC = float(0x5F3759DF)

SA, CA, GA, SB, CB, GB, GA_BO, GB_B2 = range(8)

QL, KL, KH, QH = range(4)
ST_Q, ST_K, ST_KX = range(3)


def after(engine, semaphore, value):
    if not (isinstance(value, int) and value <= 0):
        engine.wait_ge(semaphore, value)


def rsqrt_guess(nc, out, half, x, done):
    nc.vector.tensor_scalar(half, x, -0.5, None, ALU.mult)
    nc.vector.tensor_scalar(out.bitcast(I32), x.bitcast(I32), -0.5, RSQRT_MAGIC, ALU.mult, ALU.add).then_inc(done, 1)


def rsqrt_newton(nc, pool, out, half, tmp, c15, step, done):
    for k in range(3):
        if k:
            pool.wait_ge(step, done + 4 * k)
        nc.gpsimd.tensor_tensor(tmp, out, out, ALU.mult).then_inc(step, 1)
        pool.wait_ge(step, done + 4 * k + 1)
        nc.gpsimd.tensor_tensor(tmp, tmp, half, ALU.mult).then_inc(step, 1)
        pool.wait_ge(step, done + 4 * k + 2)
        nc.gpsimd.tensor_tensor(tmp, tmp, c15, ALU.add).then_inc(step, 1)
        pool.wait_ge(step, done + 4 * k + 3)
        nc.gpsimd.tensor_tensor(out, out, tmp, ALU.mult).then_inc(step, 1)


NEWTON_OPS = 12



def adaln_attention_moe(nc, x, Wq, Wk, Wv, Wo, bo, q_scale, k_scale, proj_w, proj_b, expert_bias,
                        fc1_w, fc1_b, fc2_w, fc2_b, sh1_w, sh1_b, sh2_w, sh2_b, c, wmod, out):
    B, N, C = x.shape
    H, DH = q_scale.shape[0], q_scale.shape[2]
    E, EH = fc1_b.shape
    SH = sh1_b.shape[0]
    NT = N // P
    HP = H // 2
    TT = B * NT
    T = B * N
    CAP = -(-(-(-T * EXPERTS_PER_TOKEN // E)) * CAP_NUM // CAP_DEN)
    S_TILES = 2 * NT
    assert C == P and DH == 64 and N == 512 and HP % 4 == 0 and EH == 2 * P and SH % P == 0

    x_tok = x.rearrange("b (t p) c -> p (b t) c", p=P)
    out_tok = out.rearrange("b (t p) c -> b p t c", p=P)

    with ExitStack() as whole:
        whole.enter_context(nc.allow_non_contiguous_dma(reason="a few small vectors go on partitions"))

        def alloc(scope):
            def sb(name, shape, dt=F32):
                return scope.enter_context(nc.sbuf_tensor(name, shape, dt))

            def pb(name, shape=(P, 512)):
                return scope.enter_context(nc.psum_tensor(name, list(shape), F32))

            def sem(name):
                return scope.enter_context(nc.semaphore(name))
            return sb, pb, sem

        sb, pb, sem = alloc(whole)
        x1_all = sb("x1_all", [P, TT, C])
        h2_all = sb("h2_all", [P, T])
        z_all = sb("z_all", [P, TT, E])
        ident = sb("ident", [P, P])
        modT = sb("modT", [P, 8, B])
        projT = sb("projT", [P, E])
        projb_row = sb("projb_row", [P, E])
        sh2b_col = sb("sh2b_col", [P, 1])
        bank = [pb(f"bank{i}") for i in range(8)]

        with ExitStack() as scope:
            sb, pb, sem = alloc(scope)
            wqkv_h = sb("wqkv_h", [P, 3, H * DH], F32R)
            wqkv_l = sb("wqkv_l", [P, 3, H * DH], F32R)
            wo_h = sb("wo_h", [P, HP, C], F32R)
            wo_l = sb("wo_l", [P, HP, C], F32R)
            qk_scale = sb("qk_scale", [P, HP])

            with ExitStack() as scope0:
                sb, pb, sem = alloc(scope0)
                raw = sb("raw", [P, 3, HP, C])
                raw_o = sb("raw_o", [P, H * DH])
                wmod_sb = sb("wmod_sb", [P, 6 * C])
                cT = sb("cT", [P, B])
                eT = sb("eT", [P, B])
                siluT = sb("siluT", [P, B])
                mod_sb = sb("mod_sb", [P, 6 * B])
                clampT = sb("clampT", [P, 2, B])
                signT = sb("signT", [P, 2, B])
                bo_col = sb("bo_col", [P, 1])
                ks_col = sb("ks_col", [P, HP])
                qs_col = sb("qs_col", [P, HP])
                s_w = [sem(f"s_w{i}") for i in range(4)]
                s_mod_in = sem("s_mod_in")
                s_small = sem("s_small")
                s_ident = sem("s_ident")
                s_wt = sem("s_wt")
                s_wh = sem("s_wh")
                s_wl = sem("s_wl")
                s_exp = sem("s_exp")
                s_silu = sem("s_silu")
                s_mod = sem("s_mod")
                s_mc = sem("s_mc")
                s_x = sem("s_x")

                with nc.Block() as block:
                    @block.sync
                    def _(sp):
                        for n, w in enumerate((Wq, Wk, Wv)):
                            sp.dma_start(raw[:, n], w.rearrange("(r p) c -> p r c", p=P)).then_inc(s_w[n], 16)
                        sp.dma_start(raw_o[:], Wo).then_inc(s_w[3], 16)
                        sp.dma_start(x1_all[:], x_tok).then_inc(s_x, 16)
                        sp.wait_ge(s_x, 16)

                    @block.gpsimd
                    def _(pool):
                        nc.gpsimd.memset(ident[:], 0.0).then_inc(s_ident, 1)
                        pool.wait_ge(s_ident, 1)
                        nc.gpsimd.affine_select(out=ident[:], in_=ident[:], compare_op=ALU.not_equal, fill=1.0,
                                                base=0, pattern=[[-1, P]], channel_multiplier=1).then_inc(s_ident, 1)

                    @block.tensor
                    def _(pe):
                        pe.wait_ge(s_ident, 2)
                        for n in range(4):
                            pe.wait_ge(s_w[n], 16)
                            for half in range(2):
                                for r in range(4):
                                    chunk = 4 * half + r
                                    src = raw[:, n, chunk] if n < 3 else raw_o[:, chunk * P:(chunk + 1) * P]
                                    last = nc.tensor.transpose(bank[2 * n + half][:, r * P:(r + 1) * P], src, ident[:])
                                last.then_inc(s_wt, 1)
                        pe.wait_ge(s_silu, 3)
                        pe.wait_ge(s_wl, 1)
                        for v in range(6):
                            last = nc.tensor.matmul(bank[0][:, v * B:(v + 1) * B], wmod_sb[:, v * C:(v + 1) * C],
                                                    siluT[:], start=True, stop=True)
                        last.then_inc(s_mod, 1)

                    def weight_part(parts, n, half):
                        w = parts[0] if n < 3 else parts[1]
                        flat = w[:, n] if n < 3 else w[:].rearrange("p h c -> p (h c)")
                        return flat[:, half * 512:(half + 1) * 512]

                    @block.scalar
                    def _(act):
                        act.dma_start(cT[:], c.rearrange("b c -> c b")).then_inc(s_mod_in, 16)
                        act.dma_start(wmod_sb[:], wmod).then_inc(s_mod_in, 16)
                        act.dma_start(bo_col[:], bo.rearrange("(c o) -> c o", o=1)).then_inc(s_small, 16)
                        act.dma_start(sh2b_col[:], sh2_b.rearrange("(c o) -> c o", o=1)).then_inc(s_small, 16)
                        for h in range(2):
                            act.dma_start(qs_col[h * DH:(h + 1) * DH, :],
                                          q_scale.rearrange("(hp two) o d -> two d (hp o)", two=2)[h]).then_inc(s_small, 16)
                            act.dma_start(ks_col[h * DH:(h + 1) * DH, :],
                                          k_scale.rearrange("(hp two) o d -> two d (hp o)", two=2)[h]).then_inc(s_small, 16)
                        act.dma_start(projT[:], proj_w.rearrange("e c -> c e")).then_inc(s_small, 16)
                        act.dma_start(projb_row[:], proj_b.partition_broadcast(P)).then_inc(s_small, 16)
                        act.wait_ge(s_mod_in, 32)
                        nc.scalar.activation(eT[:], cT[:], ACT.Exp, scale=-1.0).then_inc(s_exp, 1)
                        for j in range(8):
                            act.wait_ge(s_wt, j + 1)
                            nc.scalar.activation(weight_part((wqkv_h, wo_h), j // 2, j % 2), bank[j][:],
                                                 ACT.Copy).then_inc(s_wh, 1)

                    @block.vector
                    def _(dve):
                        dve.wait_ge(s_exp, 1)
                        nc.vector.tensor_scalar(eT[:], eT[:], 1.0, None, ALU.add).then_inc(s_silu, 1)
                        dve.wait_ge(s_silu, 1)
                        nc.vector.reciprocal(eT[:], eT[:]).then_inc(s_silu, 1)
                        dve.wait_ge(s_silu, 2)
                        nc.vector.tensor_tensor(siluT[:], eT[:], cT[:], ALU.mult).then_inc(s_silu, 1)
                        for j in range(8):
                            dve.wait_ge(s_wh, j + 1)
                            nc.vector.tensor_tensor(weight_part((wqkv_l, wo_l), j // 2, j % 2), bank[j][:],
                                                    weight_part((wqkv_h, wo_h), j // 2, j % 2).bitcast(F32),
                                                    ALU.subtract).then_inc(s_wl, 1)
                        dve.wait_ge(s_small, 8 * 16)
                        nc.vector.scalar_tensor_tensor(out=qk_scale[:], in0=qs_col[:], scalar=float(DH) ** -0.5,
                                                       in1=ks_col[:], op0=ALU.mult, op1=ALU.mult)
                        dve.wait_ge(s_mod, 1)
                        nc.vector.tensor_copy(mod_sb[:], bank[0][:, 0:6 * B]).then_inc(s_mc, 1)
                        dve.wait_ge(s_mc, 1)
                        for v in (SA, SB):
                            nc.vector.tensor_copy(modT[:, v], mod_sb[:, v * B:(v + 1) * B])
                        for v in (CA, CB):
                            nc.vector.tensor_scalar(modT[:, v], mod_sb[:, v * B:(v + 1) * B], 1.0, None, ALU.add)
                        for k, v in enumerate((GA, GB)):
                            nc.vector.tensor_scalar(signT[:, k], mod_sb[:, v * B:(v + 1) * B], 0.0, 2.0,
                                                    ALU.is_ge, ALU.mult).then_inc(s_mc, 1)
                            nc.vector.scalar_tensor_tensor(out=clampT[:, k], in0=mod_sb[:, v * B:(v + 1) * B],
                                                           scalar=-1.0, in1=mod_sb[:, v * B:(v + 1) * B],
                                                           op0=ALU.mult, op1=ALU.max).then_inc(s_mc, 1)
                        dve.wait_ge(s_mc, 5)
                        nc.vector.tensor_scalar(clampT[:], clampT[:], MIN_GATE, None, ALU.max).then_inc(s_mc, 1)
                        dve.wait_ge(s_mc, 6)
                        for k, v in enumerate((GA, GB)):
                            nc.vector.scalar_tensor_tensor(out=modT[:, v], in0=signT[:, k], scalar=-1.0,
                                                           in1=clampT[:, k], op0=ALU.add, op1=ALU.mult).then_inc(s_mc, 1)
                        dve.wait_ge(s_mc, 8)
                        nc.vector.tensor_scalar(modT[:, GA_BO], modT[:, GA], bo_col[:], None, ALU.mult)
                        nc.vector.tensor_scalar(modT[:, GB_B2], modT[:, GB], sh2b_col[:], None, ALU.mult)

            sb, pb, sem = alloc(scope)
            hT_h = sb("hT_h", [P, N], F32R)
            hT_l = sb("hT_l", [P, N], F32R)
            qk_tok = sb("qk_tok", [P, 2, NT, 2 * P])
            v_tok = sb("v_tok", [P, 4, NT, P])
            sq = sb("sq", [P, NT, 2 * P])
            ss = sb("ss", [P, NT * 4])
            rn = sb("rn", [P, NT * 4])
            rn_t = sb("rn_t", [P, NT * 4])
            ss_half = sb("ss_half", [P, NT * 4])
            consts1 = sb("consts1", [P, 2])
            c15, c1 = consts1[:, 0:1], consts1[:, 1:2]
            var_half = sb("var_half", [P, NT])
            parts = sb("parts", [P, 4, N], F32R)
            stack = sb("stack", [P, 2, 2, 3, N], F32R)
            probs = sb("probs", [P, 4, N])
            probsT = sb("probsT", [P, 2, 2, NT, N])
            neg_max = sb("neg_max", [P, S_TILES])
            row_sum = sb("row_sum", [P, 2, S_TILES])
            inv_sum = sb("inv_sum", [P, 2, S_TILES])
            inv_wide = sb("inv_wide", [P, NT, 2, DH])
            inv_row = sb("inv_row", [P, N])
            oT = sb("oT", [P, N])
            oT_h = sb("oT_h", [P, HP, N], F32R)
            oT_l = sb("oT_l", [P, HP, N], F32R)
            m_out = sb("m_out", [P, N])
            h_ln = sb("h_ln", [P, NT, C])
            stats = sb("stats", [P, NT, 6])
            mean_var = sb("mean_var", [P, NT, 2])
            var_eps = sb("var_eps", [P, NT])
            rstd = sb("rstd", [P, NT])
            rstd_t = sb("rstd_t", [P, NT])
            mod1 = sb("mod1", [P, 2])
            mod2 = sb("mod2", [P, 4])

            S_BANK, T_BANK, O_BANK, PJ_BANK = bank[0:3], bank[3:5], bank[5], bank[6]
            XT_BANK = M_BANK = bank[7]

            hT_ready = sem("hT_ready")
            pj_ready = sem("pj_ready")
            pj_copied = sem("pj_copied")
            v_copied = sem("v_copied")
            sq_done = sem("sq_done")
            ss_done = sem("ss_done")
            ss_max = sem("ss_max")
            rn_guess = sem("rn_guess")
            ln_guess = sem("ln_guess")
            s_const = sem("s_const")
            rn_step = sem("rn_step")
            qn_done = sem("qn_done")
            qt_ready = sem("qt_ready")
            qh_done = sem("qh_done")
            ql_done = sem("ql_done")
            kt_ready = sem("kt_ready")
            kh_done = sem("kh_done")
            kl_done = sem("kl_done")
            stack_a = sem("stack_a")
            stack_b = sem("stack_b")
            s_ready = sem("s_ready")
            max_done = sem("max_done")
            p_done = sem("p_done")
            t_ready = sem("t_ready")
            t_dve = sem("t_dve")
            t_act = sem("t_act")
            inv_done = sem("inv_done")
            wide_done = sem("wide_done")
            r_ready = sem("r_ready")
            r_copied = sem("r_copied")
            av_done = sem("av_done")
            o_done = sem("o_done")
            oh_done = sem("oh_done")
            ol_done = sem("ol_done")
            mod1_done = sem("mod1_done")
            st1_done = sem("st1_done")
            ve_done = sem("ve_done")
            ln_step = sem("ln_step")
            hln_done = sem("hln_done")
            hlnT_ready = sem("hlnT_ready")
            h1_done = sem("h1_done")
            h1h_done = sem("h1h_done")
            y_ready = sem("y_ready")
            y_done = sem("y_done")
            yT_ready = sem("yT_ready")
            mod2_done = sem("mod2_done")
            x1_done = sem("x1_done")
            h2_done = sem("h2_done")
            h2_kept = sem("h2_kept")
            z_ready = sem("z_ready")
            z_done = sem("z_done")

            QT_AT, KT_AT = 1, 3
            Y_SLOT, Y_STEPS = 1, (5, 6)
            YT_AT, H2T_AT, Z_AT, H1T_AT = (2, 0), (3, 6), (4, 0), (4, 6)

            LAST = B - 1
            P_LAG = 3

            def over_batches(engine, batch):
                batch(0)
                with engine.Fori(1, LAST) as b:
                    batch(b)
                batch(LAST)

            def is_const(b, value):
                return isinstance(b, int) and b == value

            with nc.Block() as block:

                @block.sync
                def _(sp):
                    def stacks(u, hp):
                        sp.wait_ge(kl_done, u + 1)
                        for head in range(2):
                            own, other = (0, DH) if head == 0 else (DH, 0)
                            src = parts[own:own + DH]
                            dst = stack[:, hp % 2, head]
                            there = (stack_a, stack_b)[head]
                            sp.dma_start(dst[own:own + DH].bitcast(F32), src[:, QH:QL:-1].bitcast(F32)).then_inc(there, 16)
                            sp.dma_start(dst[other:other + DH].bitcast(F32), src[:, QL:QH].bitcast(F32)).then_inc(there, 16)

                    def batch(b):
                        for hp in range(HP):
                            stacks(HP * b + hp, hp)

                    over_batches(sp, batch)

                @block.tensor
                def _(pe):
                    def project(u, hp, wb, t):
                        if t == 0:
                            pe.wait_ge(hT_ready, wb + 1)
                            after(pe, r_copied, u - 3)
                            after(pe, v_copied, NT * u)
                        else:
                            pe.wait_ge(v_copied, NT * u + t)
                        o = PJ_BANK[:, 0:3 * P].rearrange("p (n c) -> p n c", n=3)
                        cols = slice(hp * P, (hp + 1) * P)
                        toks = slice(t * P, (t + 1) * P)
                        nc.tensor.matmul(o, hT_h[:, toks], wqkv_h[:, :, cols], start=True, stop=False)
                        nc.tensor.matmul(o, hT_h[:, toks], wqkv_l[:, :, cols], start=False, stop=False)
                        nc.tensor.matmul(o, hT_l[:, toks], wqkv_h[:, :, cols], start=False,
                                         stop=True).then_inc(pj_ready, 1)

                    def transpose_q(u, hp, *free):
                        pe.wait_ge(qn_done, u + 1)
                        for semaphore, value in free:
                            after(pe, semaphore, value)
                        for t in range(NT):
                            last = nc.tensor.transpose(XT_BANK[:, t * P:(t + 1) * P], qk_tok[:, hp % 2, t, 0:P], ident[:])
                        last.then_inc(qt_ready, 1)

                    def transpose_k(u, hp):
                        pe.wait_ge(ql_done, u + 1)
                        for t in range(NT):
                            last = nc.tensor.transpose(XT_BANK[:, t * P:(t + 1) * P], qk_tok[:, hp % 2, t, P:2 * P], ident[:])
                        last.then_inc(kt_ready, 1)

                    def scores(u, hp, i):
                        g = S_TILES * u + i
                        if i == 0:
                            pe.wait_ge(stack_a, 32 * (u + 1))
                        if i == NT:
                            pe.wait_ge(stack_b, 32 * (u + 1))
                        after(pe, p_done, g - (2 if i >= 3 else 4 if i == 2 else 1))
                        head, t = i // NT, i % NT
                        st = stack[:, hp % 2, head]
                        q = st[:, ST_Q, t * P:(t + 1) * P]
                        nc.tensor.matmul(S_BANK[i % 3][:], q, st[:, ST_K], start=True, stop=False)
                        nc.tensor.matmul(S_BANK[i % 3][:], q, st[:, ST_KX], start=False, stop=True).then_inc(s_ready, 1)

                    def transpose_probs(u, i):
                        pe.wait_ge(p_done, S_TILES * u + i + 1)
                        semaphore, count = {0: (t_dve, -1), 1: (t_dve, 0), 2: (t_dve, 1), 7: (t_dve, 2)}.get(i, (t_act, i - 2))
                        after(pe, semaphore, 4 * u + count)
                        for j in range(NT):
                            last = nc.tensor.transpose(T_BANK[i % 2][:, j * P:(j + 1) * P],
                                                       probs[:, i % 4, j * P:(j + 1) * P], ident[:])
                        last.then_inc(t_ready, 1)

                    def inverse_rows(u, hp, pj):
                        pe.wait_ge(wide_done, u + 1)
                        pe.wait_ge(v_copied, pj)
                        after(pe, r_copied, u)
                        for t in range(NT):
                            last = nc.tensor.transpose(PJ_BANK[:, t * P:(t + 1) * P],
                                                       inv_wide[:, t].rearrange("p h d -> p (h d)"), ident[:])
                        last.then_inc(r_ready, 1)

                    def weigh_values(u, hp, j):
                        if j == 0:
                            pe.wait_ge(t_dve, 4 * (u + 1))
                            pe.wait_ge(t_act, 4 * (u + 1))
                            after(pe, o_done, u)
                        for head in range(2):
                            rows = slice(head * DH, (head + 1) * DH)
                            last = nc.tensor.matmul(O_BANK[rows, :], v_tok[:, hp % 4, j, rows],
                                                    probsT[:, hp % 2, head, j], start=(j == 0), stop=(j == NT - 1),
                                                    skip_group_check=True)
                        if j == NT - 1:
                            last.then_inc(av_done, 1)

                    def project_out(b, u, half):
                        if half == 0:
                            pe.wait_ge(ol_done, HP * (b + 1))
                            after(pe, kl_done, u)
                        for hp in range(half * HP // 2, (half + 1) * HP // 2):
                            nc.tensor.matmul(M_BANK[:], wo_h[:, hp], oT_h[:, hp], start=(hp == 0), stop=False)
                            nc.tensor.matmul(M_BANK[:], wo_l[:, hp], oT_h[:, hp], start=False, stop=False)
                            last = nc.tensor.matmul(M_BANK[:], wo_h[:, hp], oT_l[:, hp], start=False, stop=(hp == HP - 1))
                        if half == 1:
                            last.then_inc(y_ready, 1)

                    def transpose_y(b):
                        pe.wait_ge(y_done, b + 1)
                        for t in range(NT):
                            last = nc.tensor.transpose(M_BANK[:, t * P:(t + 1) * P], m_out[:, t * P:(t + 1) * P], ident[:])
                        last.then_inc(yT_ready, 1)

                    def transpose_ln(count, *free):
                        pe.wait_ge(hln_done, count)
                        for semaphore, value in free:
                            after(pe, semaphore, value)
                        for t in range(NT):
                            last = nc.tensor.transpose(M_BANK[:, t * P:(t + 1) * P], h_ln[:, t], ident[:])
                        last.then_inc(hlnT_ready, 1)

                    def router(b, u):
                        pe.wait_ge(h2_done, b + 1)
                        after(pe, kl_done, u)
                        for t in range(NT):
                            last = nc.tensor.matmul(M_BANK[:, t * E:(t + 1) * E], m_out[:, t * P:(t + 1) * P], projT[:],
                                                    start=True, stop=True)
                        last.then_inc(z_ready, 1)

                    def slot(b, hp, main=True, tail=True):
                        u = HP * b + hp
                        front_a = main and not (is_const(b, LAST) and hp + 2 >= HP)
                        front_b = main and not (is_const(b, LAST) and hp + 1 >= HP)
                        for i in range(S_TILES):
                            if main:
                                scores(u, hp, i)
                            if tail and i < P_LAG:
                                transpose_probs(u - 1, S_TILES - P_LAG + i)
                            if main and i >= P_LAG:
                                transpose_probs(u, i - P_LAG)
                            if front_a and i < NT:
                                project(u + 2, (hp + 2) % HP, b + (hp + 2) // HP, i)
                            if not is_const(b, 0) and main:
                                if (hp, i) == YT_AT:
                                    transpose_y(b - 1)
                                if (hp, i) == Z_AT:
                                    router(b - 1, u + 1)
                            if front_b and i == QT_AT:
                                side = {2: (x1_done, b), 4: (z_done, b), 5: (h1_done, b + 2)}
                                if is_const(b, LAST):
                                    side.pop(5)
                                transpose_q(u + 1, hp + 1, side.get(hp, (kl_done, u + 1)), (kl_done, u + 1))
                            if front_b and i == KT_AT:
                                transpose_k(u + 1, hp + 1)
                            if tail and i in (4, 6):
                                weigh_values(u - 1, hp - 1, i - 4)
                                weigh_values(u - 1, hp - 1, i - 3)
                            if tail and i == 5:
                                pj = NT * (u + 3) if front_a else NT * HP * B
                                inverse_rows(u - 1, hp - 1, pj)
                            if not is_const(b, 0) and main:
                                if hp == Y_SLOT and i in Y_STEPS:
                                    project_out(b - 1, u + 2, Y_STEPS.index(i))
                                if (hp, i) == H2T_AT:
                                    transpose_ln(2 * b + 1, (kl_done, u + 2))
                            if not is_const(b, LAST) and (hp, i) == H1T_AT and main:
                                transpose_ln(2 * b + 2, (kl_done, u + 2))

                    def batch(b):
                        for hp in range(HP):
                            slot(b, hp, tail=not (is_const(b, 0) and hp == 0))

                    transpose_ln(1)
                    for hp in range(2):
                        for t in range(NT):
                            project(hp, hp, 0, t)
                    transpose_q(0, 0, (h1_done, 1))
                    transpose_k(0, 0)
                    over_batches(pe, batch)
                    slot(B, 0, main=False)
                    for half in range(2):
                        project_out(LAST, HP * B, half)
                    transpose_y(LAST)
                    transpose_ln(2 * B, (x1_done, B))
                    router(LAST, 0)

                @block.scalar
                def _(act):
                    def copy_projection(u, hp, t):
                        act.wait_ge(pj_ready, NT * u + t + 1)
                        if t == 0:
                            after(act, av_done, u - 3)
                        nc.scalar.activation(qk_tok[:, hp % 2, t], PJ_BANK[:, 0:2 * P], ACT.Copy).then_inc(pj_copied, 1)
                        nc.scalar.activation(v_tok[:, hp % 4, t], PJ_BANK[:, 2 * P:3 * P], ACT.Copy).then_inc(v_copied, 1)

                    def square_projection(u, hp, t):
                        act.wait_ge(pj_copied, NT * u + t + 1)
                        if t == 0:
                            after(act, ss_done, 2 * u)
                        nc.scalar.activation(sq[:, t], qk_tok[:, hp % 2, t], ACT.Square).then_inc(sq_done, 1)

                    def high_q(u, hp):
                        act.wait_ge(qt_ready, u + 1)
                        after(act, stack_a, 32 * u)
                        after(act, stack_b, 32 * u)
                        nc.scalar.activation(parts[:, QH], XT_BANK[:], ACT.Copy,
                                             scale=qk_scale[:, hp % HP:hp % HP + 1]).then_inc(qh_done, 1)

                    def high_k(u):
                        act.wait_ge(kt_ready, u + 1)
                        nc.scalar.activation(parts[:, KH], XT_BANK[:], ACT.Copy).then_inc(kh_done, 1)

                    def exponentials(u, hp, i):
                        g = S_TILES * u + i
                        act.wait_ge(max_done, g + 1)
                        after(act, t_ready, g - 3)
                        if i == 0:
                            after(act, inv_done, u - 1)
                        nc.scalar.activation(probs[:, i % 4], S_BANK[i % 3][:], ACT.Exp, bias=neg_max[:, i:i + 1],
                                             accum_out=row_sum[:, hp % 2, i:i + 1]).then_inc(p_done, 1)

                    def copy_transposed(u, hp, i):
                        act.wait_ge(t_ready, S_TILES * u + i + 1)
                        if i == 1:
                            after(act, av_done, u - 1)
                        head, t = i // NT, i % NT
                        nc.scalar.activation(probsT[:, hp % 2, head, :, t * P:(t + 1) * P],
                                             T_BANK[i % 2][:].rearrange("p (j q) -> p j q", j=NT),
                                             ACT.Copy).then_inc(t_act, 1)

                    def copy_inverse(u):
                        act.wait_ge(r_ready, u + 1)
                        after(act, o_done, u)
                        nc.scalar.activation(inv_row[:], PJ_BANK[:], ACT.Copy).then_inc(r_copied, 1)

                    def modulate1(b):
                        act.wait_ge(hlnT_ready, 2 * b if not isinstance(b, int) else max(2 * b, 1))
                        act.wait_ge(mod1_done, b + 1)
                        nc.scalar.activation(m_out[:], M_BANK[:], ACT.Identity, scale=mod1[:, 0:1],
                                             bias=mod1[:, 1:2]).then_inc(h1_done, 1)

                    def gate_y(b):
                        act.wait_ge(y_ready, b + 1)
                        act.wait_ge(mod2_done, b + 1)
                        act.wait_ge(hT_ready, b + 2 if not is_const(b, LAST) else LAST + 1)
                        nc.scalar.activation(m_out[:], M_BANK[:], ACT.Identity, scale=mod2[:, 0:1],
                                             bias=mod2[:, 1:2]).then_inc(y_done, 1)

                    def modulate2(b, count):
                        act.wait_ge(hlnT_ready, count)
                        nc.scalar.activation(m_out[:], M_BANK[:], ACT.Identity, scale=mod2[:, 2:3],
                                             bias=mod2[:, 3:4]).then_inc(h2_done, 1)

                    def keep_h2(b):
                        act.wait_ge(h2_done, b + 1)
                        nc.scalar.activation(h2_all[:, bass.ts(b, N)], m_out[:], ACT.Copy).then_inc(h2_kept, 1)

                    def slot(b, hp, main=True, tail=True):
                        u = HP * b + hp
                        front_a = main and not (is_const(b, LAST) and hp + 2 >= HP)
                        front_b = main and not (is_const(b, LAST) and hp + 1 >= HP)
                        for i in range(S_TILES):
                            if not is_const(b, 0) and main:
                                if (hp, i) == (Y_SLOT, Y_STEPS[-1] + 1):
                                    gate_y(b - 1)
                                if (hp, i) == (H2T_AT[0], H2T_AT[1] + 1):
                                    modulate2(b - 1, 2 * b + 1)
                            if front_a and i < NT:
                                copy_projection(u + 2, hp + 2, i)
                            if front_b and i == KT_AT + 1:
                                high_k(u + 1)
                            if main and i > P_LAG:
                                copy_transposed(u, hp, i - P_LAG)
                            if front_a and i < NT:
                                square_projection(u + 2, hp + 2, i)
                            if main:
                                exponentials(u, hp, i)
                            if front_b and i == QT_AT:
                                high_q(u + 1, hp + 1)
                            if tail and i == 6:
                                copy_inverse(u - 1)
                            if not is_const(b, 0) and main and (hp, i) == (H2T_AT[0], H2T_AT[1] + 1):
                                keep_h2(b - 1)
                            if not is_const(b, LAST) and (hp, i) == (H1T_AT[0], H1T_AT[1] + 1) and main:
                                modulate1(b + 1)

                    def batch(b):
                        for hp in range(HP):
                            slot(b, hp, tail=not (is_const(b, 0) and hp == 0))

                    modulate1(0)
                    for hp in range(2):
                        for t in range(NT):
                            copy_projection(hp, hp, t)
                            square_projection(hp, hp, t)
                    high_q(0, 0)
                    high_k(0)
                    over_batches(act, batch)
                    slot(B, 0, main=False)
                    gate_y(LAST)
                    modulate2(LAST, 2 * B)
                    keep_h2(LAST)

                @block.vector
                def _(dve):
                    def sum_squares(u, half):
                        dve.wait_ge(sq_done, NT * u + 2 * half + 2)
                        if half == 0:
                            after(dve, qn_done, u)
                        nc.vector.reduce_sum(ss[:, 8 * half:8 * half + 8],
                                             sq[:, 2 * half:2 * half + 2].rearrange("p t (n d) -> p (t n) d", d=DH),
                                             AX.X).then_inc(ss_done, 1)

                    def guard_squares(u):
                        dve.wait_ge(ss_done, 2 * u + 2)
                        nc.vector.tensor_scalar(ss[:], ss[:], NORM_EPS ** 2, None, ALU.max).then_inc(ss_max, 1)

                    def guess_norms(u):
                        dve.wait_ge(ss_max, u + 1)
                        rsqrt_guess(nc, rn[:], ss_half[:], ss[:], rn_guess)

                    def low_q(u, hp):
                        dve.wait_ge(qh_done, u + 1)
                        nc.vector.scalar_tensor_tensor(out=parts[:, QL], in0=XT_BANK[:],
                                                       scalar=qk_scale[:, hp % HP:hp % HP + 1],
                                                       in1=parts[:, QH].bitcast(F32), op0=ALU.mult,
                                                       op1=ALU.subtract).then_inc(ql_done, 1)

                    def low_k(u):
                        dve.wait_ge(kh_done, u + 1)
                        nc.vector.tensor_tensor(parts[:, KL], XT_BANK[:], parts[:, KH].bitcast(F32),
                                                ALU.subtract).then_inc(kl_done, 1)

                    def row_max(u, i):
                        dve.wait_ge(s_ready, S_TILES * u + i + 1)
                        nc.vector.reduce_max(neg_max[:, i:i + 1], S_BANK[i % 3][:], AX.X, negate=True).then_inc(max_done, 1)

                    def copy_transposed(u, hp, i):
                        dve.wait_ge(t_ready, S_TILES * u + i + 1)
                        if i == 0:
                            after(dve, av_done, u - 1)
                        head, t = i // NT, i % NT
                        nc.vector.tensor_copy(probsT[:, hp % 2, head, :, t * P:(t + 1) * P],
                                              T_BANK[i % 2][:].rearrange("p (j q) -> p j q", j=NT)).then_inc(t_dve, 1)

                    def invert_sums(u, hp):
                        dve.wait_ge(p_done, S_TILES * (u + 1))
                        after(dve, wide_done, u - 1)
                        nc.vector.reciprocal(inv_sum[:, hp % 2], row_sum[:, hp % 2]).then_inc(inv_done, 1)

                    def normalise(u):
                        dve.wait_ge(av_done, u + 1)
                        dve.wait_ge(r_copied, u + 1)
                        after(dve, ol_done, u)
                        nc.vector.tensor_tensor(oT[:], O_BANK[:], inv_row[:], ALU.mult).then_inc(o_done, 1)

                    def high_o(u, hp, b):
                        dve.wait_ge(o_done, u + 1)
                        after(dve, y_ready, b)
                        nc.vector.tensor_copy(oT_h[:, hp % HP], oT[:]).then_inc(oh_done, 1)

                    def tile_of(b, t):
                        return x1_all[:, bass.ds(b * NT + t, 1)].rearrange("p o c -> p (o c)")

                    def tile_stats(b, count):
                        for t in range(NT):
                            nc.vector.bn_stats(stats[:, t], tile_of(b, t)).then_inc(st1_done, 1)

                    def stats_there(count):
                        dve.wait_ge(st1_done, (2 * NT) * count + NT)
                        after(dve, hln_done, count)

                    def aggregate(count):
                        for t in range(NT):
                            nc.vector.bn_aggr(mean_var[:, t], stats[:, t]).then_inc(st1_done, 1)
                        dve.wait_ge(st1_done, (2 * NT) * (count + 1))
                        after(dve, ln_step, NEWTON_OPS * count)
                        nc.vector.tensor_scalar(var_eps[:], mean_var[:, :, 1], LN_EPS, None, ALU.add).then_inc(ve_done, 1)

                    def guess_std(count):
                        dve.wait_ge(ve_done, count + 1)
                        rsqrt_guess(nc, rstd[:], var_half[:], var_eps[:], ln_guess)

                    def ln_rows(b, count):
                        dve.wait_ge(ln_step, NEWTON_OPS * (count + 1))
                        after(dve, hlnT_ready, count)
                        for t in range(NT):
                            last = nc.vector.tensor_scalar(
                                h_ln[:, t], tile_of(b, t),
                                mean_var[:, t, 0:1], rstd[:, t:t + 1], ALU.subtract, ALU.mult)
                        last.then_inc(hln_done, 1)

                    def take_mod(dst, cols, b, done, free):
                        after(dve, *free)
                        for k, v in enumerate(cols):
                            last = nc.vector.tensor_copy(dst[:, k:k + 1], modT[:, v, bass.ts(b, 1)])
                        last.then_inc(done, 1)

                    def high_h1(b):
                        dve.wait_ge(h1_done, b + 1)
                        after(dve, pj_ready, NT * HP * b)
                        nc.vector.tensor_copy(hT_h[:], m_out[:]).then_inc(h1h_done, 1)

                    def low_h1(b):
                        dve.wait_ge(h1h_done, b + 1)
                        nc.vector.tensor_tensor(hT_l[:], m_out[:], hT_h[:].bitcast(F32), ALU.subtract).then_inc(hT_ready, 1)

                    def residual(b):
                        dve.wait_ge(yT_ready, b + 1)
                        rows = x1_all[:, bass.ts(b, NT)]
                        nc.vector.tensor_tensor(rows, M_BANK[:].rearrange("p (t c) -> p t c", t=NT), rows,
                                                ALU.add).then_inc(x1_done, 1)

                    def logits(b):
                        dve.wait_ge(z_ready, b + 1)
                        rows = z_all[:, bass.ts(b, NT)]
                        nc.vector.tensor_tensor(rows, M_BANK[:, 0:NT * E].rearrange("p (t e) -> p t e", t=NT),
                                                projb_row[:].unsqueeze(1).to_broadcast([P, NT, E]), ALU.add).then_inc(z_done, 1)

                    def slot(b, hp, main=True, tail=True):
                        u = HP * b + hp
                        front_a = main and not (is_const(b, LAST) and hp + 2 >= HP)
                        front_b = main and not (is_const(b, LAST) and hp + 1 >= HP)
                        for i in range(S_TILES):
                            if main and not is_const(b, 0) and (hp, i) == (2, 5):
                                dve.wait_ge(x1_done, b)
                            if main and not is_const(b, 0) and (hp, i) == (2, 6):
                                stats_there(2 * b)
                            if main and not is_const(b, LAST) and (hp, i) == (3, 7):
                                stats_there(2 * b + 1)
                            if main:
                                row_max(u, i)
                            if tail and i < P_LAG:
                                copy_transposed(u - 1, hp - 1, S_TILES - P_LAG + i)
                            if tail and i == 1:
                                invert_sums(u - 1, hp - 1)
                            if main and i == P_LAG:
                                copy_transposed(u, hp, 0)
                            if front_b and i == QT_AT + 1:
                                low_q(u + 1, hp + 1)
                            if front_b and i == KT_AT + 1:
                                low_k(u + 1)
                            if front_a and i in (3, 4):
                                sum_squares(u + 2, i - 3)
                            if front_a and i == 5:
                                guard_squares(u + 2)
                                guess_norms(u + 2)
                            if tail and i == 7:
                                normalise(u - 1)
                                high_o(u - 1, hp - 1, b if hp > 0 else b - 1)
                            if not is_const(b, 0) and main:
                                if (hp, i) == (0, 5):
                                    take_mod(mod2, (GA, GA_BO, CB, SB), b - 1, mod2_done, (h2_done, b - 1))
                                if (hp, i) == YT_AT:
                                    residual(b - 1)
                                if (hp, i) == (2, 5):
                                    tile_stats(b - 1, 2 * b)
                                if (hp, i) == (2, 6):
                                    aggregate(2 * b)
                                if (hp, i) == (2, 7):
                                    guess_std(2 * b)
                                if (hp, i) == (3, 5):
                                    ln_rows(b - 1, 2 * b)
                                if (hp, i) == Z_AT:
                                    logits(b - 1)
                            if not is_const(b, LAST) and main:
                                nth = 2 * b + 1
                                if (hp, i) == (3, 6):
                                    tile_stats(b + 1, nth)
                                    take_mod(mod1, (CA, SA), b + 1, mod1_done, (h1_done, b + 1))
                                if (hp, i) == (3, 7):
                                    aggregate(nth)
                                if (hp, i) == (4, 0):
                                    guess_std(nth)
                                if (hp, i) == (4, 5):
                                    ln_rows(b + 1, nth)
                                if (hp, i) == (5, 5):
                                    high_h1(b + 1)
                                if (hp, i) == (5, 6):
                                    low_h1(b + 1)

                    def batch(b):
                        for hp in range(HP):
                            slot(b, hp, tail=not (is_const(b, 0) and hp == 0))

                    take_mod(mod1, (CA, SA), 0, mod1_done, (h1_done, 0))
                    tile_stats(0, 0)
                    stats_there(0)
                    aggregate(0)
                    guess_std(0)
                    ln_rows(0, 0)
                    high_h1(0)
                    low_h1(0)
                    for u in range(2):
                        sum_squares(u, 0)
                        sum_squares(u, 1)
                        guard_squares(u)
                        guess_norms(u)
                    low_q(0, 0)
                    low_k(0)
                    over_batches(dve, batch)
                    slot(B, 0, main=False)
                    take_mod(mod2, (GA, GA_BO, CB, SB), LAST, mod2_done, (h2_done, LAST))
                    residual(LAST)
                    dve.wait_ge(x1_done, B)
                    tile_stats(LAST, 2 * B - 1)
                    stats_there(2 * B - 1)
                    aggregate(2 * B - 1)
                    guess_std(2 * B - 1)
                    ln_rows(LAST, 2 * B - 1)
                    logits(LAST)

                @block.gpsimd
                def _(pool):
                    def normalise_qk(u, hp):
                        pool.wait_ge(rn_guess, u + 1)
                        rsqrt_newton(nc, pool, rn[:], ss_half[:], rn_t[:], c15.to_broadcast([P, NT * 4]), rn_step, NEWTON_OPS * u)
                        pool.wait_ge(rn_step, NEWTON_OPS * (u + 1))
                        qk = qk_tok[:, hp % 2].rearrange("p t (n d) -> p (t n) d", d=DH)
                        nc.gpsimd.tensor_tensor(qk, qk, rn[:].unsqueeze(2).to_broadcast([P, NT * 4, DH]),
                                                ALU.mult).then_inc(qn_done, 1)

                    def widen(u, hp):
                        pool.wait_ge(inv_done, u + 1)
                        after(pool, r_ready, u)
                        src = inv_sum[:, hp % 2].rearrange("p (h t) -> p t h", h=2)
                        nc.gpsimd.tensor_tensor(inv_wide[:], src.unsqueeze(3).to_broadcast([P, NT, 2, DH]),
                                                c1.unsqueeze(2).unsqueeze(3).to_broadcast([P, NT, 2, DH]),
                                                ALU.mult).then_inc(wide_done, 1)

                    def low_o(u, hp):
                        pool.wait_ge(oh_done, u + 1)
                        nc.gpsimd.tensor_tensor(oT_l[:, hp % HP], oT[:], oT_h[:, hp % HP].bitcast(F32),
                                                ALU.subtract).then_inc(ol_done, 1)

                    def inverse_std(count):
                        pool.wait_ge(ln_guess, count + 1)
                        rsqrt_newton(nc, pool, rstd[:], var_half[:], rstd_t[:], c15.to_broadcast([P, NT]), ln_step, NEWTON_OPS * count)

                    def slot(b, hp, main=True, tail=True):
                        u = HP * b + hp
                        front_a = main and not (is_const(b, LAST) and hp + 2 >= HP)
                        if tail:
                            widen(u - 1, hp - 1)
                        if not is_const(b, 0) and main and hp == 3:
                            inverse_std(2 * b)
                        if not is_const(b, LAST) and main and hp == 4:
                            inverse_std(2 * b + 1)
                        if front_a:
                            normalise_qk(u + 2, hp + 2)
                        if tail:
                            low_o(u - 1, hp - 1)

                    def batch(b):
                        for hp in range(HP):
                            slot(b, hp, tail=not (is_const(b, 0) and hp == 0))

                    nc.gpsimd.memset(c15, 1.5).then_inc(s_const, 1)
                    nc.gpsimd.memset(c1, 1.0).then_inc(s_const, 1)
                    pool.wait_ge(s_const, 2)
                    inverse_std(0)
                    for u in range(2):
                        normalise_qk(u, u)
                    over_batches(pool, batch)
                    slot(B, 0, main=False)
                    inverse_std(2 * B - 1)

        TILES = SH // P + E * (EH // P)
        SHT = SH // P
        with ExitStack() as scope:
            sb, pb, sem = alloc(scope)
            up_h = sb("up_h", [P, TILES, P], F32R)
            up_l = sb("up_l", [P, TILES, P], F32R)
            down_h = sb("down_h", [P, TILES, P], F32R)
            down_l = sb("down_l", [P, TILES, P], F32R)
            up_bias = sb("up_bias", [P, TILES])
            b2_pad = sb("b2_pad", [P, C])
            h2_h = sb("h2_h", [P, T], F32R)
            h2_l = sb("h2_l", [P, T], F32R)
            gates = sb("gates", [P, TT, E])
            gate_pad = sb("gate_pad", [P, NT, P])

            with ExitStack() as scope2:
                sb, pb, sem = alloc(scope2)
                raw_up = sb("raw_up", [P, TILES, P])
                raw_down = sb("raw_down", [P, TILES, P])
                ebias_row = sb("ebias_row", [P, E])
                s_up = sem("s_up")
                s_down = sem("s_down")
                s_bias = sem("s_bias")
                s_zero = sem("s_zero")
                s_wt = sem("s_wt2")
                s_wh = sem("s_wh2")
                s_wl = sem("s_wl2")
                s_h2h = sem("s_h2h")
                s_h2l = sem("s_h2l")
                s_sig = sem("s_sig")
                rt = sem("rt")
                consts = sem("consts")
                count_in = sem("count_in")
                count_out = sem("count_out")
                thr = sem("thr")
                fin_in = sem("fin_in")
                fin_out = sem("fin_out")

                def rt_tile(name, shape=(P, TT, E), dt=F32):
                    return sb(name, list(shape), dt)

                prob = rt_tile("prob")
                t1 = rt_tile("t1")
                t2 = rt_tile("t2")
                top1 = rt_tile("top1")
                top2 = rt_tile("top2")
                m1 = rt_tile("m1", (P, TT))
                m2 = rt_tile("m2", (P, TT))
                den = rt_tile("den", (P, TT))
                w1 = rt_tile("w1", (P, TT))
                w2 = rt_tile("w2", (P, TT))
                ranked = rt_tile("ranked", (P, E, TT))
                above = rt_tile("above", (P, E, TT))
                equal = rt_tile("equal", (P, E, TT))
                before = rt_tile("before", (P, E, TT))
                not_first = rt_tile("not_first", (P, E, TT))
                rev = rt_tile("rev", (P, E))
                rev_i = rt_tile("rev_i", (P, E), I32)
                ones = rt_tile("ones", (P, P))
                earlier = rt_tile("earlier", (P, P))
                thr_u = rt_tile("thr_u", (P, E), U32)
                cand_u = rt_tile("cand_u", (P, E), U32)
                bit_f = rt_tile("bit_f", (P, E))
                bit_u = rt_tile("bit_u", (P, E), U32)
                inc_u = rt_tile("inc_u", (P, E), U32)
                part_count = rt_tile("part_count", (P, E))
                room = rt_tile("room", (P, E))
                BITS = 30

                def by_expert(tile):
                    return tile[:].rearrange("p t e -> p e t")

                wfull = sb("wfull", [P, 2, 4 * P])

                def weight_group(j):
                    low, high = (up_l, up_h) if j < TILES // 4 else (down_l, down_h)
                    k = 4 * (j % (TILES // 4))
                    flat = [w[:, k:k + 4].rearrange("p r c -> p (r c)") for w in (low, high)]
                    return flat[0], flat[1], wfull[:, j % 2], k

                with nc.Block() as block:
                    @block.sync
                    def _(sp):
                        sp.dma_start(ebias_row[:], expert_bias.partition_broadcast(P)).then_inc(s_bias, 16)
                        sp.dma_start(raw_up[:, 0:SHT], sh1_w.rearrange("(r p) c -> p r c", p=P)).then_inc(s_up, 16)
                        sp.dma_start(raw_up[:, SHT:], fc1_w.rearrange("e (r p) c -> p (e r) c", p=P)).then_inc(s_up, 16)
                        sp.dma_start(raw_down[:, 0:SHT], sh2_w.rearrange("c (r h) -> c r h", h=P)).then_inc(s_down, 16)
                        sp.dma_start(raw_down[:, SHT:].rearrange("p (e r) h -> p e (r h)", e=E),
                                     fc2_w.rearrange("e c h -> c e h")).then_inc(s_down, 16)
                        sp.dma_start(up_bias[:, 0:SHT], sh1_b.rearrange("(r p) -> p r", p=P)).then_inc(s_bias, 16)
                        sp.dma_start(up_bias[:, SHT:], fc1_b.rearrange("e (r p) -> p (e r)", p=P)).then_inc(s_bias, 16)
                        sp.wait_ge(s_zero, 2)
                        sp.dma_start(b2_pad[0:E, :], fc2_b).then_inc(s_bias, 16)
                        sp.wait_ge(s_bias, 64)

                    @block.gpsimd
                    def _(pool):
                        nc.gpsimd.memset(b2_pad[:], 0.0).then_inc(s_zero, 1)
                        nc.gpsimd.memset(gate_pad[:], 0.0).then_inc(s_zero, 1)
                        nc.gpsimd.iota(rev_i[:], pattern=[[-1, E]], base=E, channel_multiplier=0).then_inc(consts, 1)
                        nc.gpsimd.memset(ones[:], 1.0).then_inc(consts, 1)
                        pool.wait_ge(consts, 2)
                        nc.gpsimd.affine_select(out=earlier[:], in_=ones[:], compare_op=ALU.is_gt, fill=0.0,
                                                base=0, pattern=[[1, P]], channel_multiplier=-1).then_inc(consts, 1)
                        for q in range(B):
                            pool.wait_ge(s_h2h, q + 1)
                            cols = slice(q * N, (q + 1) * N)
                            nc.gpsimd.tensor_tensor(h2_l[:, cols], h2_all[:, cols], h2_h[:, cols].bitcast(F32),
                                                    ALU.subtract).then_inc(s_h2l, 1)
                        for j in range(2 * TILES // 4):
                            pool.wait_ge(s_wh, 2 * j + 2)
                            dst, hi, full, cols = weight_group(j)
                            nc.gpsimd.tensor_tensor(dst, full, hi.bitcast(F32), ALU.subtract).then_inc(s_wl, 1)

                    @block.tensor
                    def _(pe):
                        def transpose_weights(j):
                            if j == 0:
                                pe.wait_ge(s_up, 32)
                            if j == TILES // 4:
                                pe.wait_ge(s_down, 32)
                            after(pe, s_wh, 2 * (j - 3))
                            src = raw_up if j < TILES // 4 else raw_down
                            for r in range(4):
                                last = nc.tensor.transpose(bank[j % 4][:, r * P:(r + 1) * P],
                                                           src[:, 4 * (j % (TILES // 4)) + r], ident[:])
                            last.then_inc(s_wt, 1)

                        for j in range(2 * TILES // 4):
                            transpose_weights(j)
                        pe.wait_ge(consts, 3)
                        with pe.Fori(0, BITS) as k:
                            pe.wait_ge(count_in, k + 1)
                            nc.tensor.matmul(bank[7][:, 0:E], ones[:], part_count[:], start=True,
                                             stop=True).then_inc(count_out, 1)
                        pe.wait_ge(fin_in, 1)
                        nc.tensor.matmul(bank[6][:, 0:E], ones[:], part_count[:], start=True, stop=True).then_inc(fin_out, 1)
                        nc.tensor.matmul(bank[5][:, 0:E * TT], ones[:], equal[:].rearrange("p e t -> p (e t)"),
                                         start=True, stop=True).then_inc(fin_out, 1)
                        nc.tensor.matmul(bank[4][:, 0:E * TT], earlier[:], equal[:].rearrange("p e t -> p (e t)"),
                                         start=True, stop=True).then_inc(fin_out, 1)

                    @block.scalar
                    def _(act):
                        nc.scalar.activation(t1[:], z_all[:], ACT.Exp, scale=-1.0).then_inc(s_sig, 1)
                        for q in range(B):
                            cols = slice(q * N, (q + 1) * N)
                            nc.scalar.activation(h2_h[:, cols], h2_all[:, cols], ACT.Copy).then_inc(s_h2h, 1)
                        for j in range(2 * TILES // 4):
                            act.wait_ge(s_wt, j + 1)
                            after(act, s_wl, j - 1)
                            _, hi, full, _ = weight_group(j)
                            nc.scalar.activation(full, bank[j % 4][:], ACT.Copy).then_inc(s_wh, 1)
                            nc.scalar.activation(hi, bank[j % 4][:], ACT.Copy).then_inc(s_wh, 1)

                    @block.vector
                    def _(dve):
                        steps = [0]

                        def link(instruction):
                            steps[0] += 1
                            instruction.then_inc(rt, 1)
                            dve.wait_ge(rt, steps[0])

                        def spread(row):
                            return row[:].unsqueeze(2).to_broadcast([P, TT, E])

                        dve.wait_ge(consts, 3)
                        link(nc.vector.tensor_copy(rev[:], rev_i[:]))
                        rev_all = rev[:].unsqueeze(1).to_broadcast([P, TT, E])
                        dve.wait_ge(s_sig, 1)
                        dve.wait_ge(s_bias, 64)
                        link(nc.vector.tensor_scalar(t1[:], t1[:], 1.0, None, ALU.add))
                        link(nc.vector.reciprocal(t1[:], t1[:]))
                        link(nc.vector.tensor_tensor(t1[:], t1[:], ebias_row[:].unsqueeze(1).to_broadcast([P, TT, E]), ALU.add))
                        link(nc.vector.tensor_scalar(t1[:], t1[:], CLIP, None, ALU.max))
                        link(nc.vector.reduce_max(m1[:], t1[:], AX.X))
                        link(nc.vector.reciprocal(m1[:], m1[:]))
                        link(nc.vector.tensor_tensor(t1[:], t1[:], spread(m1), ALU.mult))
                        link(nc.vector.reduce_sum(m1[:], t1[:], AX.X))
                        link(nc.vector.reciprocal(m1[:], m1[:]))
                        link(nc.vector.tensor_tensor(prob[:], t1[:], spread(m1), ALU.mult))

                        def first_max(values, best, choice):
                            link(nc.vector.reduce_max(best[:], values[:], AX.X))
                            link(nc.vector.tensor_tensor(t2[:], values[:], spread(best), ALU.is_equal))
                            link(nc.vector.tensor_tensor(t2[:], t2[:], rev_all, ALU.mult))
                            link(nc.vector.reduce_max(den[:], t2[:], AX.X))
                            link(nc.vector.tensor_tensor(choice[:], rev_all, spread(den), ALU.is_equal))

                        first_max(prob, m1, top1)
                        link(nc.vector.scalar_tensor_tensor(out=t1[:], in0=top1[:], scalar=-2.0, in1=prob[:],
                                                            op0=ALU.mult, op1=ALU.add))
                        first_max(t1, m2, top2)
                        link(nc.vector.tensor_tensor(den[:], m1[:], m2[:], ALU.add))
                        link(nc.vector.tensor_scalar(den[:], den[:], CLIP, None, ALU.max))
                        link(nc.vector.reciprocal(den[:], den[:]))
                        link(nc.vector.tensor_tensor(w1[:], m1[:], den[:], ALU.mult))
                        link(nc.vector.tensor_tensor(w2[:], m2[:], den[:], ALU.mult))
                        link(nc.vector.tensor_tensor(t1[:], top1[:], spread(w1), ALU.mult))
                        link(nc.vector.tensor_tensor(t2[:], top2[:], spread(w2), ALU.mult))
                        link(nc.vector.tensor_tensor(prob[:], t1[:], t2[:], ALU.add))
                        link(nc.vector.tensor_tensor(t1[:], top1[:], top2[:], ALU.add))
                        link(nc.vector.scalar_tensor_tensor(out=ranked[:], in0=by_expert(t1), scalar=-1.0,
                                                            in1=by_expert(prob), op0=ALU.add, op1=ALU.add))

                        link(nc.vector.memset(thr_u[:], 0))
                        link(nc.vector.memset(bit_f[:], float(2 ** (BITS - 1))))
                        link(nc.vector.tensor_copy(bit_u[:], bit_f[:]))
                        with dve.Fori(0, BITS) as k:
                            nc.vector.tensor_tensor(cand_u[:], thr_u[:], bit_u[:], ALU.bitwise_or).then_inc(thr, 1)
                            dve.wait_ge(thr, 6 * k + 1)
                            nc.vector.tensor_tensor(above[:], ranked[:],
                                                    cand_u[:].bitcast(F32).unsqueeze(2).to_broadcast([P, E, TT]),
                                                    ALU.is_ge).then_inc(thr, 1)
                            dve.wait_ge(thr, 6 * k + 2)
                            nc.vector.reduce_sum(part_count[:], above[:], AX.X).then_inc(count_in, 1)
                            dve.wait_ge(count_out, k + 1)
                            nc.vector.scalar_tensor_tensor(out=inc_u[:], in0=bank[7][:, 0:E], scalar=float(CAP),
                                                           in1=bit_f[:], op0=ALU.is_ge, op1=ALU.mult).then_inc(thr, 1)
                            dve.wait_ge(thr, 6 * k + 3)
                            nc.vector.tensor_tensor(thr_u[:], thr_u[:], inc_u[:], ALU.bitwise_or).then_inc(thr, 1)
                            nc.vector.tensor_scalar(bit_f[:], bit_f[:], 0.5, None, ALU.mult).then_inc(thr, 1)
                            dve.wait_ge(thr, 6 * k + 5)
                            nc.vector.tensor_copy(bit_u[:], bit_f[:]).then_inc(thr, 1)
                            dve.wait_ge(thr, 6 * k + 6)

                        thr_all = thr_u[:].bitcast(F32).unsqueeze(2).to_broadcast([P, E, TT])
                        link(nc.vector.tensor_tensor(above[:], ranked[:], thr_all, ALU.is_gt))
                        link(nc.vector.tensor_tensor(equal[:], ranked[:], thr_all, ALU.is_equal))
                        link(nc.vector.memset(not_first[:], 1.0))
                        link(nc.vector.memset(not_first[:, :, 0:1], 0.0))
                        nc.vector.reduce_sum(part_count[:], above[:], AX.X).then_inc(fin_in, 1)
                        dve.wait_ge(fin_out, 3)
                        link(nc.vector.tensor_scalar(room[:], bank[6][:, 0:E], -1.0, float(CAP), ALU.mult, ALU.add))
                        link(nc.vector.tensor_copy(before[:], bank[5][:, 0:E * TT].rearrange("p (e t) -> p e t", e=E)))
                        link(nc.vector.tensor_tensor_scan(t1[:].rearrange("p t e -> p (t e)"),
                                                          not_first[:].rearrange("p e t -> p (e t)"),
                                                          before[:].rearrange("p e t -> p (e t)"), 0.0, ALU.mult, ALU.add))
                        flat1 = t1[:].rearrange("p t e -> p (t e)").rearrange("p (e t) -> p e t", e=E)
                        link(nc.vector.tensor_tensor(before[:], flat1, before[:], ALU.subtract))
                        link(nc.vector.tensor_tensor(before[:], bank[4][:, 0:E * TT].rearrange("p (e t) -> p e t", e=E),
                                                     before[:], ALU.add))
                        link(nc.vector.tensor_tensor(before[:], before[:], room[:].unsqueeze(2).to_broadcast([P, E, TT]), ALU.is_lt))
                        link(nc.vector.tensor_tensor(before[:], before[:], equal[:], ALU.mult))
                        link(nc.vector.tensor_tensor(above[:], above[:], before[:], ALU.add))
                        link(nc.vector.tensor_tensor(by_expert(gates), above[:], by_expert(prob), ALU.mult))

            sb, pb, sem = alloc(scope)
            LAG = 3
            act_out = sb("act_out", [P, 4, N])
            gated = sb("gated", [P, 4, N])
            hid_h = sb("hid_h", [P, 4, N], F32R)
            hid_l = sb("hid_l", [P, 4, N], F32R)
            gateT = sb("gateT", [P, N])
            yT = sb("yT", [P, N])
            mod3 = sb("mod3", [P, 2])
            H_BANK, W_BANK, Y_BANK, GT_BANK, Z_BANK = bank[0:2], bank[2:4], bank[4], bank[5], bank[6]
            up_ready = sem("up_ready")
            gelu_done = sem("gelu_done")
            gate_ready = sem("gate_ready")
            gated_done = sem("gated_done")
            hi_done = sem("hi_done")
            lo_done = sem("lo_done")
            down_done = sem("down_done")
            pad_done = sem("pad_done")
            gT_ready = sem("gT_ready")
            gT_copied = sem("gT_copied")
            mod3_done = sem("mod3_done")
            yc_done = sem("yc_done")
            z3_ready = sem("z3_ready")
            out_done = sem("out_done")
            stored = sem("stored")
            EXPERT_TILES = TILES - SHT

            def over_all(engine, batch):
                batch(0)
                with engine.Fori(1, B) as b:
                    batch(b)

            def none_before(b):
                return isinstance(b, int) and b == 0

            with nc.Block() as block:
                @block.sync
                def _(sp):
                    with sp.Fori(0, B) as b:
                        sp.wait_ge(out_done, b + 1)
                        sp.dma_start(out_tok[bass.ds(b, 1)].rearrange("o p t c -> p (o t) c"),
                                     x1_all[:, bass.ts(b, NT)]).then_inc(stored, 16)
                    sp.wait_ge(stored, 16 * B)

                @block.tensor
                def _(pe):
                    def up(b, k):
                        n = TILES * b + k
                        after(pe, gelu_done, n - 1)
                        cols = bass.ts(b, N)
                        nc.tensor.matmul(H_BANK[k % 2][:], up_h[:, k], h2_h[:, cols], start=True, stop=False)
                        nc.tensor.matmul(H_BANK[k % 2][:], up_l[:, k], h2_h[:, cols], start=False, stop=False)
                        nc.tensor.matmul(H_BANK[k % 2][:], up_h[:, k], h2_l[:, cols], start=False,
                                         stop=True).then_inc(up_ready, 1)

                    def gate_rows(b, e):
                        if e == 0:
                            pe.wait_ge(pad_done, b + 1)
                        after(pe, gated_done, EXPERT_TILES * b + 2 * (e - 1))
                        for t in range(NT):
                            last = nc.tensor.transpose(W_BANK[e % 2][:, t * P:(t + 1) * P],
                                                       gate_pad[:, t, e:e + 1].to_broadcast([P, P]), ident[:])
                        last.then_inc(gate_ready, 1)

                    def gates_to_experts(b):
                        pe.wait_ge(pad_done, b + 1)
                        after(pe, gT_copied, b)
                        for t in range(NT):
                            last = nc.tensor.transpose(GT_BANK[:, t * P:(t + 1) * P], gate_pad[:, t], ident[:])
                        last.then_inc(gT_ready, 1)

                    def down(b, k):
                        n = TILES * b + k
                        if k == 0:
                            pe.wait_ge(gT_copied, b + 1)
                            after(pe, yc_done, b)
                            nc.tensor.matmul(Y_BANK[:], b2_pad[:], gateT[:], start=True, stop=False)
                        pe.wait_ge(lo_done, n + 1)
                        nc.tensor.matmul(Y_BANK[:], down_h[:, k], hid_h[:, k % 4], start=False, stop=False)
                        nc.tensor.matmul(Y_BANK[:], down_l[:, k], hid_h[:, k % 4], start=False, stop=False)
                        nc.tensor.matmul(Y_BANK[:], down_h[:, k], hid_l[:, k % 4], start=False,
                                         stop=(k == TILES - 1)).then_inc(down_done, 1)

                    def back_to_tokens(b):
                        pe.wait_ge(yc_done, b + 1)
                        after(pe, out_done, b)
                        for t in range(NT):
                            last = nc.tensor.transpose(Z_BANK[:, t * P:(t + 1) * P], yT[:, t * P:(t + 1) * P], ident[:])
                        last.then_inc(z3_ready, 1)

                    def batch(b):
                        for k in range(TILES):
                            up(b, k)
                            if k == 2:
                                gates_to_experts(b)
                            if k >= SHT and (k - SHT) % 2 == 0:
                                gate_rows(b, (k - SHT) // 2)
                            if k >= LAG:
                                down(b, k - LAG)
                            elif not none_before(b):
                                down(b - 1, TILES + k - LAG)
                            if k == 6 and not none_before(b):
                                back_to_tokens(b - 1)

                    over_all(pe, batch)
                    for k in range(TILES - LAG, TILES):
                        down(B - 1, k)
                    back_to_tokens(B - 1)

                @block.scalar
                def _(act):
                    def take_sum(b):
                        act.wait_ge(down_done, TILES * (b + 1))
                        act.wait_ge(mod3_done, b + 1)
                        after(act, z3_ready, b)
                        nc.scalar.activation(yT[:], Y_BANK[:], ACT.Identity, scale=mod3[:, 0:1],
                                             bias=mod3[:, 1:2]).then_inc(yc_done, 1)

                    def batch(b):
                        for k in range(TILES):
                            n = TILES * b + k
                            act.wait_ge(up_ready, n + 1)
                            after(act, lo_done, n - 3)
                            nc.scalar.activation(act_out[:, k % 4], H_BANK[k % 2][:], ACT.Gelu,
                                                 bias=up_bias[:, k:k + 1]).then_inc(gelu_done, 1)
                            if k == 2:
                                act.wait_ge(gT_ready, b + 1)
                                after(act, down_done, TILES * b - 2 * TILES + 1 if isinstance(b, int) else TILES * (b - 1) + 1)
                                nc.scalar.activation(gateT[:], GT_BANK[:], ACT.Copy).then_inc(gT_copied, 1)
                            if k == 3 and not none_before(b):
                                take_sum(b - 1)

                    over_all(act, batch)
                    take_sum(B - 1)

                @block.vector
                def _(dve):
                    def take_gates(b):
                        after(dve, up_ready, TILES * b - 1)
                        nc.vector.tensor_copy(gate_pad[:, :, 0:E], gates[:, bass.ts(b, NT)]).then_inc(pad_done, 1)

                    def take_mod3(b):
                        after(dve, yc_done, b)
                        for j, v in enumerate((GB, GB_B2)):
                            last = nc.vector.tensor_copy(mod3[:, j:j + 1], modT[:, v, bass.ts(b, 1)])
                        last.then_inc(mod3_done, 1)

                    def add_residual(b):
                        dve.wait_ge(z3_ready, b + 1)
                        rows = x1_all[:, bass.ts(b, NT)]
                        nc.vector.tensor_tensor(rows, Z_BANK[:].rearrange("p (t c) -> p t c", t=NT), rows,
                                                ALU.add).then_inc(out_done, 1)

                    def batch(b):
                        take_gates(b)
                        for k in range(TILES):
                            n = TILES * b + k
                            dve.wait_ge(gelu_done, n + 1)
                            source = act_out
                            if k >= SHT:
                                e = (k - SHT) // 2
                                dve.wait_ge(gate_ready, E * b + e + 1)
                                after(dve, lo_done, n - 3)
                                nc.vector.tensor_tensor(gated[:, k % 4], W_BANK[e % 2][:], act_out[:, k % 4],
                                                        ALU.mult).then_inc(gated_done, 1)
                                dve.wait_ge(gated_done, EXPERT_TILES * b + k - SHT + 1)
                                source = gated
                            after(dve, down_done, n - 3)
                            nc.vector.tensor_copy(hid_h[:, k % 4], source[:, k % 4]).then_inc(hi_done, 1)
                            if k == 1 and not none_before(b):
                                take_mod3(b - 1)
                            if k == 8 and not none_before(b):
                                add_residual(b - 1)

                    over_all(dve, batch)
                    take_mod3(B - 1)
                    add_residual(B - 1)

                @block.gpsimd
                def _(pool):
                    def batch(b):
                        for k in range(TILES):
                            n = TILES * b + k
                            pool.wait_ge(hi_done, n + 1)
                            source = act_out if k < SHT else gated
                            nc.gpsimd.tensor_tensor(hid_l[:, k % 4], source[:, k % 4], hid_h[:, k % 4].bitcast(F32),
                                                    ALU.subtract).then_inc(lo_done, 1)

                    over_all(pool, batch)


_INS = ["L0_attn_x", "L0_attn_Wq", "L0_attn_Wk", "L0_attn_Wv", "L0_attn_Wo", "L0_attn_bo", "L0_attn_q_scale",
        "L0_attn_k_scale", "L0_ffn_proj_w", "L0_ffn_proj_b", "L0_ffn_expert_bias", "L0_ffn_fc1_w", "L0_ffn_fc1_b",
        "L0_ffn_fc2_w", "L0_ffn_fc2_b", "L0_ffn_sh1_w", "L0_ffn_sh1_b", "L0_ffn_sh2_w", "L0_ffn_sh2_b", "L0_c",
        "L0_wmod"]


def kernel(**inputs):
    import numpy as np
    import concourse.bacc as bacc
    from concourse.bass_utils import run_bass_kernel_spmd

    nc = bacc.Bacc("TRN2", target_bir_lowering=False, num_devices=1)
    arrays, args = {}, []
    for name in _INS:
        a = np.ascontiguousarray(inputs[name])
        arrays[f"in_{name}"] = a
        args.append(nc.dram_tensor(f"in_{name}", a.shape, mybir.dt.from_np(a.dtype), kind="ExternalInput").ap())
    shape = arrays["in_L0_attn_x"].shape
    args.append(nc.dram_tensor("out_0", shape, F32, kind="ExternalOutput").ap())
    adaln_attention_moe(nc, *args)
    r = run_bass_kernel_spmd(nc, [arrays], core_ids=[0])
    return r.results[0]["out_0"]
```

```python
from contextlib import ExitStack

import concourse.bass as bass
from concourse import mybir

P = 128
ALU = mybir.AluOpType
ACT = mybir.ActivationFunctionType
AX = mybir.AxisListType
F32 = mybir.dt.float32
F32R = mybir.dt.float32r
I32 = mybir.dt.int32
U32 = mybir.dt.uint32

LN_EPS = 1e-5
NORM_EPS = 1e-12
CLIP = 1e-12
MIN_GATE = 0.25
EXPERTS_PER_TOKEN = 2
CAP_NUM, CAP_DEN = 5, 4
RSQRT_MAGIC = float(0x5F3759DF)

SA, CA, GA, SB, CB, GB, GA_BO, GB_B2 = range(8)

QL, KL, KH, QH = range(4)
ST_Q, ST_K, ST_KX = range(3)


def after(engine, semaphore, value):
    if not (isinstance(value, int) and value <= 0):
        engine.wait_ge(semaphore, value)


def rsqrt_guess(nc, out, half, x, done):
    nc.vector.tensor_scalar(half, x, -0.5, None, ALU.mult)
    nc.vector.tensor_scalar(out.bitcast(I32), x.bitcast(I32), -0.5, RSQRT_MAGIC, ALU.mult, ALU.add).then_inc(done, 1)


def rsqrt_newton(nc, pool, out, half, tmp, c15, step, done):
    for k in range(3):
        if k:
            pool.wait_ge(step, done + 4 * k)
        nc.gpsimd.tensor_tensor(tmp, out, out, ALU.mult).then_inc(step, 1)
        pool.wait_ge(step, done + 4 * k + 1)
        nc.gpsimd.tensor_tensor(tmp, tmp, half, ALU.mult).then_inc(step, 1)
        pool.wait_ge(step, done + 4 * k + 2)
        nc.gpsimd.tensor_tensor(tmp, tmp, c15, ALU.add).then_inc(step, 1)
        pool.wait_ge(step, done + 4 * k + 3)
        nc.gpsimd.tensor_tensor(out, out, tmp, ALU.mult).then_inc(step, 1)


NEWTON_OPS = 12



def adaln_attention_moe(nc, x, Wq, Wk, Wv, Wo, bo, q_scale, k_scale, proj_w, proj_b, expert_bias,
                        fc1_w, fc1_b, fc2_w, fc2_b, sh1_w, sh1_b, sh2_w, sh2_b, c, wmod, out):
    B, N, C = x.shape
    H, DH = q_scale.shape[0], q_scale.shape[2]
    E, EH = fc1_b.shape
    SH = sh1_b.shape[0]
    NT = N // P
    HP = H // 2
    TT = B * NT
    T = B * N
    CAP = -(-(-(-T * EXPERTS_PER_TOKEN // E)) * CAP_NUM // CAP_DEN)
    S_TILES = 2 * NT
    assert C == P and DH == 64 and N == 512 and HP % 4 == 0 and EH == 2 * P and SH % P == 0

    x_tok = x.rearrange("b (t p) c -> p (b t) c", p=P)
    out_tok = out.rearrange("b (t p) c -> b p t c", p=P)

    with ExitStack() as whole:
        whole.enter_context(nc.allow_non_contiguous_dma(reason="a few small vectors go on partitions"))

        def alloc(scope):
            def sb(name, shape, dt=F32):
                return scope.enter_context(nc.sbuf_tensor(name, shape, dt))

            def pb(name, shape=(P, 512)):
                return scope.enter_context(nc.psum_tensor(name, list(shape), F32))

            def sem(name):
                return scope.enter_context(nc.semaphore(name))
            return sb, pb, sem

        sb, pb, sem = alloc(whole)
        x1_all = sb("x1_all", [P, TT, C])
        h2_all = sb("h2_all", [P, T])
        z_all = sb("z_all", [P, TT, E])
        ident = sb("ident", [P, P])
        modT = sb("modT", [P, 8, B])
        projT = sb("projT", [P, E])
        projb_row = sb("projb_row", [P, E])
        sh2b_col = sb("sh2b_col", [P, 1])
        bank = [pb(f"bank{i}") for i in range(8)]

        with ExitStack() as scope:
            sb, pb, sem = alloc(scope)
            wqkv_h = sb("wqkv_h", [P, 3, H * DH], F32R)
            wqkv_l = sb("wqkv_l", [P, 3, H * DH], F32R)
            wo_h = sb("wo_h", [P, HP, C], F32R)
            wo_l = sb("wo_l", [P, HP, C], F32R)
            qk_scale = sb("qk_scale", [P, HP])

            with ExitStack() as scope0:
                sb, pb, sem = alloc(scope0)
                raw = sb("raw", [P, 3, HP, C])
                raw_o = sb("raw_o", [P, H * DH])
                wmod_sb = sb("wmod_sb", [P, 6 * C])
                cT = sb("cT", [P, B])
                eT = sb("eT", [P, B])
                siluT = sb("siluT", [P, B])
                mod_sb = sb("mod_sb", [P, 6 * B])
                clampT = sb("clampT", [P, 2, B])
                signT = sb("signT", [P, 2, B])
                bo_col = sb("bo_col", [P, 1])
                ks_col = sb("ks_col", [P, HP])
                qs_col = sb("qs_col", [P, HP])
                s_w = [sem(f"s_w{i}") for i in range(4)]
                s_mod_in = sem("s_mod_in")
                s_small = sem("s_small")
                s_ident = sem("s_ident")
                s_wt = sem("s_wt")
                s_wh = sem("s_wh")
                s_wl = sem("s_wl")
                s_exp = sem("s_exp")
                s_silu = sem("s_silu")
                s_mod = sem("s_mod")
                s_mc = sem("s_mc")
                s_x = sem("s_x")

                with nc.Block() as block:
                    @block.sync
                    def _(sp):
                        for n, w in enumerate((Wq, Wk, Wv)):
                            sp.dma_start(raw[:, n], w.rearrange("(r p) c -> p r c", p=P)).then_inc(s_w[n], 16)
                        sp.dma_start(raw_o[:], Wo).then_inc(s_w[3], 16)
                        sp.dma_start(x1_all[:], x_tok).then_inc(s_x, 16)
                        sp.wait_ge(s_x, 16)

                    @block.gpsimd
                    def _(pool):
                        nc.gpsimd.memset(ident[:], 0.0).then_inc(s_ident, 1)
                        pool.wait_ge(s_ident, 1)
                        nc.gpsimd.affine_select(out=ident[:], in_=ident[:], compare_op=ALU.not_equal, fill=1.0,
                                                base=0, pattern=[[-1, P]], channel_multiplier=1).then_inc(s_ident, 1)

                    @block.tensor
                    def _(pe):
                        pe.wait_ge(s_ident, 2)
                        for n in range(4):
                            pe.wait_ge(s_w[n], 16)
                            for half in range(2):
                                for r in range(4):
                                    chunk = 4 * half + r
                                    src = raw[:, n, chunk] if n < 3 else raw_o[:, chunk * P:(chunk + 1) * P]
                                    last = nc.tensor.transpose(bank[2 * n + half][:, r * P:(r + 1) * P], src, ident[:])
                                last.then_inc(s_wt, 1)
                        pe.wait_ge(s_silu, 3)
                        pe.wait_ge(s_wl, 1)
                        for v in range(6):
                            last = nc.tensor.matmul(bank[0][:, v * B:(v + 1) * B], wmod_sb[:, v * C:(v + 1) * C],
                                                    siluT[:], start=True, stop=True)
                        last.then_inc(s_mod, 1)

                    def weight_part(parts, n, half):
                        w = parts[0] if n < 3 else parts[1]
                        flat = w[:, n] if n < 3 else w[:].rearrange("p h c -> p (h c)")
                        return flat[:, half * 512:(half + 1) * 512]

                    @block.scalar
                    def _(act):
                        act.dma_start(cT[:], c.rearrange("b c -> c b")).then_inc(s_mod_in, 16)
                        act.dma_start(wmod_sb[:], wmod).then_inc(s_mod_in, 16)
                        act.dma_start(bo_col[:], bo.rearrange("(c o) -> c o", o=1)).then_inc(s_small, 16)
                        act.dma_start(sh2b_col[:], sh2_b.rearrange("(c o) -> c o", o=1)).then_inc(s_small, 16)
                        for h in range(2):
                            act.dma_start(qs_col[h * DH:(h + 1) * DH, :],
                                          q_scale.rearrange("(hp two) o d -> two d (hp o)", two=2)[h]).then_inc(s_small, 16)
                            act.dma_start(ks_col[h * DH:(h + 1) * DH, :],
                                          k_scale.rearrange("(hp two) o d -> two d (hp o)", two=2)[h]).then_inc(s_small, 16)
                        act.dma_start(projT[:], proj_w.rearrange("e c -> c e")).then_inc(s_small, 16)
                        act.dma_start(projb_row[:], proj_b.partition_broadcast(P)).then_inc(s_small, 16)
                        act.wait_ge(s_mod_in, 32)
                        nc.scalar.activation(eT[:], cT[:], ACT.Exp, scale=-1.0).then_inc(s_exp, 1)
                        for j in range(8):
                            act.wait_ge(s_wt, j + 1)
                            nc.scalar.activation(weight_part((wqkv_h, wo_h), j // 2, j % 2), bank[j][:],
                                                 ACT.Copy).then_inc(s_wh, 1)

                    @block.vector
                    def _(dve):
                        dve.wait_ge(s_exp, 1)
                        nc.vector.tensor_scalar(eT[:], eT[:], 1.0, None, ALU.add).then_inc(s_silu, 1)
                        dve.wait_ge(s_silu, 1)
                        nc.vector.reciprocal(eT[:], eT[:]).then_inc(s_silu, 1)
                        dve.wait_ge(s_silu, 2)
                        nc.vector.tensor_tensor(siluT[:], eT[:], cT[:], ALU.mult).then_inc(s_silu, 1)
                        for j in range(8):
                            dve.wait_ge(s_wh, j + 1)
                            nc.vector.tensor_tensor(weight_part((wqkv_l, wo_l), j // 2, j % 2), bank[j][:],
                                                    weight_part((wqkv_h, wo_h), j // 2, j % 2).bitcast(F32),
                                                    ALU.subtract).then_inc(s_wl, 1)
                        dve.wait_ge(s_small, 8 * 16)
                        nc.vector.scalar_tensor_tensor(out=qk_scale[:], in0=qs_col[:], scalar=float(DH) ** -0.5,
                                                       in1=ks_col[:], op0=ALU.mult, op1=ALU.mult)
                        dve.wait_ge(s_mod, 1)
                        nc.vector.tensor_copy(mod_sb[:], bank[0][:, 0:6 * B]).then_inc(s_mc, 1)
                        dve.wait_ge(s_mc, 1)
                        for v in (SA, SB):
                            nc.vector.tensor_copy(modT[:, v], mod_sb[:, v * B:(v + 1) * B])
                        for v in (CA, CB):
                            nc.vector.tensor_scalar(modT[:, v], mod_sb[:, v * B:(v + 1) * B], 1.0, None, ALU.add)
                        for k, v in enumerate((GA, GB)):
                            nc.vector.tensor_scalar(signT[:, k], mod_sb[:, v * B:(v + 1) * B], 0.0, 2.0,
                                                    ALU.is_ge, ALU.mult).then_inc(s_mc, 1)
                            nc.vector.scalar_tensor_tensor(out=clampT[:, k], in0=mod_sb[:, v * B:(v + 1) * B],
                                                           scalar=-1.0, in1=mod_sb[:, v * B:(v + 1) * B],
                                                           op0=ALU.mult, op1=ALU.max).then_inc(s_mc, 1)
                        dve.wait_ge(s_mc, 5)
                        nc.vector.tensor_scalar(clampT[:], clampT[:], MIN_GATE, None, ALU.max).then_inc(s_mc, 1)
                        dve.wait_ge(s_mc, 6)
                        for k, v in enumerate((GA, GB)):
                            nc.vector.scalar_tensor_tensor(out=modT[:, v], in0=signT[:, k], scalar=-1.0,
                                                           in1=clampT[:, k], op0=ALU.add, op1=ALU.mult).then_inc(s_mc, 1)
                        dve.wait_ge(s_mc, 8)
                        nc.vector.tensor_scalar(modT[:, GA_BO], modT[:, GA], bo_col[:], None, ALU.mult)
                        nc.vector.tensor_scalar(modT[:, GB_B2], modT[:, GB], sh2b_col[:], None, ALU.mult)

            sb, pb, sem = alloc(scope)
            hT_h = sb("hT_h", [P, N], F32R)
            hT_l = sb("hT_l", [P, N], F32R)
            qk_tok = sb("qk_tok", [P, 2, NT, 2 * P])
            v_tok = sb("v_tok", [P, 4, NT, P])
            sq = sb("sq", [P, NT, 2 * P])
            ss = sb("ss", [P, NT * 4])
            rn = sb("rn", [P, NT * 4])
            rn_t = sb("rn_t", [P, NT * 4])
            ss_half = sb("ss_half", [P, NT * 4])
            consts1 = sb("consts1", [P, 2])
            c15, c1 = consts1[:, 0:1], consts1[:, 1:2]
            var_half = sb("var_half", [P, NT])
            parts = sb("parts", [P, 4, N], F32R)
            stack = sb("stack", [P, 2, 2, 3, N], F32R)
            probs = sb("probs", [P, 4, N])
            probsT = sb("probsT", [P, 2, 2, NT, N])
            neg_max = sb("neg_max", [P, S_TILES])
            row_sum = sb("row_sum", [P, 2, S_TILES])
            inv_sum = sb("inv_sum", [P, 2, S_TILES])
            inv_wide = sb("inv_wide", [P, NT, 2, DH])
            inv_row = sb("inv_row", [P, N])
            oT = sb("oT", [P, N])
            oT_h = sb("oT_h", [P, HP, N], F32R)
            oT_l = sb("oT_l", [P, HP, N], F32R)
            m_out = sb("m_out", [P, N])
            h_ln = sb("h_ln", [P, NT, C])
            stats = sb("stats", [P, NT, 6])
            mean_var = sb("mean_var", [P, NT, 2])
            var_eps = sb("var_eps", [P, NT])
            rstd = sb("rstd", [P, NT])
            rstd_t = sb("rstd_t", [P, NT])
            mod1 = sb("mod1", [P, 2])
            mod2 = sb("mod2", [P, 4])

            S_BANK, T_BANK, O_BANK, PJ_BANK = bank[0:3], bank[3:5], bank[5], bank[6]
            XT_BANK = M_BANK = bank[7]

            hT_ready = sem("hT_ready")
            pj_ready = sem("pj_ready")
            pj_copied = sem("pj_copied")
            v_copied = sem("v_copied")
            sq_done = sem("sq_done")
            ss_done = sem("ss_done")
            ss_max = sem("ss_max")
            rn_guess = sem("rn_guess")
            ln_guess = sem("ln_guess")
            s_const = sem("s_const")
            rn_step = sem("rn_step")
            qn_done = sem("qn_done")
            qt_ready = sem("qt_ready")
            qh_done = sem("qh_done")
            ql_done = sem("ql_done")
            kt_ready = sem("kt_ready")
            kh_done = sem("kh_done")
            kl_done = sem("kl_done")
            stack_a = sem("stack_a")
            stack_b = sem("stack_b")
            s_ready = sem("s_ready")
            max_done = sem("max_done")
            p_done = sem("p_done")
            t_ready = sem("t_ready")
            t_dve = sem("t_dve")
            t_act = sem("t_act")
            inv_done = sem("inv_done")
            wide_done = sem("wide_done")
            r_ready = sem("r_ready")
            r_copied = sem("r_copied")
            av_done = sem("av_done")
            o_done = sem("o_done")
            oh_done = sem("oh_done")
            ol_done = sem("ol_done")
            mod1_done = sem("mod1_done")
            st1_done = sem("st1_done")
            ve_done = sem("ve_done")
            ln_step = sem("ln_step")
            hln_done = sem("hln_done")
            hlnT_ready = sem("hlnT_ready")
            h1_done = sem("h1_done")
            h1h_done = sem("h1h_done")
            y_ready = sem("y_ready")
            y_done = sem("y_done")
            yT_ready = sem("yT_ready")
            mod2_done = sem("mod2_done")
            x1_done = sem("x1_done")
            h2_done = sem("h2_done")
            h2_kept = sem("h2_kept")
            z_ready = sem("z_ready")
            z_done = sem("z_done")

            QT_AT, KT_AT = 1, 3
            Y_SLOT, Y_STEPS = 1, (5, 6)
            YT_AT, H2T_AT, Z_AT, H1T_AT = (2, 0), (3, 6), (4, 0), (4, 6)

            LAST = B - 1
            P_LAG = 3

            def over_batches(engine, batch):
                batch(0)
                with engine.Fori(1, LAST) as b:
                    batch(b)
                batch(LAST)

            def is_const(b, value):
                return isinstance(b, int) and b == value

            with nc.Block() as block:

                @block.sync
                def _(sp):
                    def stacks(u, hp):
                        sp.wait_ge(kl_done, u + 1)
                        for head in range(2):
                            own, other = (0, DH) if head == 0 else (DH, 0)
                            src = parts[own:own + DH]
                            dst = stack[:, hp % 2, head]
                            there = (stack_a, stack_b)[head]
                            sp.dma_start(dst[own:own + DH].bitcast(F32), src[:, QH:QL:-1].bitcast(F32)).then_inc(there, 16)
                            sp.dma_start(dst[other:other + DH].bitcast(F32), src[:, QL:QH].bitcast(F32)).then_inc(there, 16)

                    def batch(b):
                        for hp in range(HP):
                            stacks(HP * b + hp, hp)

                    over_batches(sp, batch)

                @block.tensor
                def _(pe):
                    def project(u, hp, wb, t):
                        if t == 0:
                            pe.wait_ge(hT_ready, wb + 1)
                            after(pe, r_copied, u - 3)
                            after(pe, v_copied, NT * u)
                        else:
                            pe.wait_ge(v_copied, NT * u + t)
                        o = PJ_BANK[:, 0:3 * P].rearrange("p (n c) -> p n c", n=3)
                        cols = slice(hp * P, (hp + 1) * P)
                        toks = slice(t * P, (t + 1) * P)
                        nc.tensor.matmul(o, hT_h[:, toks], wqkv_h[:, :, cols], start=True, stop=False)
                        nc.tensor.matmul(o, hT_h[:, toks], wqkv_l[:, :, cols], start=False, stop=False)
                        nc.tensor.matmul(o, hT_l[:, toks], wqkv_h[:, :, cols], start=False,
                                         stop=True).then_inc(pj_ready, 1)

                    def transpose_q(u, hp, *free):
                        pe.wait_ge(qn_done, u + 1)
                        for semaphore, value in free:
                            after(pe, semaphore, value)
                        for t in range(NT):
                            last = nc.tensor.transpose(XT_BANK[:, t * P:(t + 1) * P], qk_tok[:, hp % 2, t, 0:P], ident[:])
                        last.then_inc(qt_ready, 1)

                    def transpose_k(u, hp):
                        pe.wait_ge(ql_done, u + 1)
                        for t in range(NT):
                            last = nc.tensor.transpose(XT_BANK[:, t * P:(t + 1) * P], qk_tok[:, hp % 2, t, P:2 * P], ident[:])
                        last.then_inc(kt_ready, 1)

                    def scores(u, hp, i):
                        g = S_TILES * u + i
                        if i == 0:
                            pe.wait_ge(stack_a, 32 * (u + 1))
                        if i == NT:
                            pe.wait_ge(stack_b, 32 * (u + 1))
                        after(pe, p_done, g - (2 if i >= 3 else 4 if i == 2 else 1))
                        head, t = i // NT, i % NT
                        st = stack[:, hp % 2, head]
                        q = st[:, ST_Q, t * P:(t + 1) * P]
                        nc.tensor.matmul(S_BANK[i % 3][:], q, st[:, ST_K], start=True, stop=False)
                        nc.tensor.matmul(S_BANK[i % 3][:], q, st[:, ST_KX], start=False, stop=True).then_inc(s_ready, 1)

                    def transpose_probs(u, i):
                        pe.wait_ge(p_done, S_TILES * u + i + 1)
                        semaphore, count = {0: (t_dve, -1), 1: (t_dve, 0), 2: (t_dve, 1), 7: (t_dve, 2)}.get(i, (t_act, i - 2))
                        after(pe, semaphore, 4 * u + count)
                        for j in range(NT):
                            last = nc.tensor.transpose(T_BANK[i % 2][:, j * P:(j + 1) * P],
                                                       probs[:, i % 4, j * P:(j + 1) * P], ident[:])
                        last.then_inc(t_ready, 1)

                    def inverse_rows(u, hp, pj):
                        pe.wait_ge(wide_done, u + 1)
                        pe.wait_ge(v_copied, pj)
                        after(pe, r_copied, u)
                        for t in range(NT):
                            last = nc.tensor.transpose(PJ_BANK[:, t * P:(t + 1) * P],
                                                       inv_wide[:, t].rearrange("p h d -> p (h d)"), ident[:])
                        last.then_inc(r_ready, 1)

                    def weigh_values(u, hp, j):
                        if j == 0:
                            pe.wait_ge(t_dve, 4 * (u + 1))
                            pe.wait_ge(t_act, 4 * (u + 1))
                            after(pe, o_done, u)
                        for head in range(2):
                            rows = slice(head * DH, (head + 1) * DH)
                            last = nc.tensor.matmul(O_BANK[rows, :], v_tok[:, hp % 4, j, rows],
                                                    probsT[:, hp % 2, head, j], start=(j == 0), stop=(j == NT - 1),
                                                    skip_group_check=True)
                        if j == NT - 1:
                            last.then_inc(av_done, 1)

                    def project_out(b, u, half):
                        if half == 0:
                            pe.wait_ge(ol_done, HP * (b + 1))
                            after(pe, kl_done, u)
                        for hp in range(half * HP // 2, (half + 1) * HP // 2):
                            nc.tensor.matmul(M_BANK[:], wo_h[:, hp], oT_h[:, hp], start=(hp == 0), stop=False)
                            nc.tensor.matmul(M_BANK[:], wo_l[:, hp], oT_h[:, hp], start=False, stop=False)
                            last = nc.tensor.matmul(M_BANK[:], wo_h[:, hp], oT_l[:, hp], start=False, stop=(hp == HP - 1))
                        if half == 1:
                            last.then_inc(y_ready, 1)

                    def transpose_y(b):
                        pe.wait_ge(y_done, b + 1)
                        for t in range(NT):
                            last = nc.tensor.transpose(M_BANK[:, t * P:(t + 1) * P], m_out[:, t * P:(t + 1) * P], ident[:])
                        last.then_inc(yT_ready, 1)

                    def transpose_ln(count, *free):
                        pe.wait_ge(hln_done, count)
                        for semaphore, value in free:
                            after(pe, semaphore, value)
                        for t in range(NT):
                            last = nc.tensor.transpose(M_BANK[:, t * P:(t + 1) * P], h_ln[:, t], ident[:])
                        last.then_inc(hlnT_ready, 1)

                    def router(b, u):
                        pe.wait_ge(h2_done, b + 1)
                        after(pe, kl_done, u)
                        for t in range(NT):
                            last = nc.tensor.matmul(M_BANK[:, t * E:(t + 1) * E], m_out[:, t * P:(t + 1) * P], projT[:],
                                                    start=True, stop=True)
                        last.then_inc(z_ready, 1)

                    def slot(b, hp, main=True, tail=True):
                        u = HP * b + hp
                        front_a = main and not (is_const(b, LAST) and hp + 2 >= HP)
                        front_b = main and not (is_const(b, LAST) and hp + 1 >= HP)
                        for i in range(S_TILES):
                            if main:
                                scores(u, hp, i)
                            if tail and i < P_LAG:
                                transpose_probs(u - 1, S_TILES - P_LAG + i)
                            if main and i >= P_LAG:
                                transpose_probs(u, i - P_LAG)
                            if front_a and i < NT:
                                project(u + 2, (hp + 2) % HP, b + (hp + 2) // HP, i)
                            if not is_const(b, 0) and main:
                                if (hp, i) == YT_AT:
                                    transpose_y(b - 1)
                                if (hp, i) == Z_AT:
                                    router(b - 1, u + 1)
                            if front_b and i == QT_AT:
                                side = {2: (x1_done, b), 4: (z_done, b), 5: (h1_done, b + 2)}
                                if is_const(b, LAST):
                                    side.pop(5)
                                transpose_q(u + 1, hp + 1, side.get(hp, (kl_done, u + 1)), (kl_done, u + 1))
                            if front_b and i == KT_AT:
                                transpose_k(u + 1, hp + 1)
                            if tail and i in (4, 6):
                                weigh_values(u - 1, hp - 1, i - 4)
                                weigh_values(u - 1, hp - 1, i - 3)
                            if tail and i == 5:
                                pj = NT * (u + 3) if front_a else NT * HP * B
                                inverse_rows(u - 1, hp - 1, pj)
                            if not is_const(b, 0) and main:
                                if hp == Y_SLOT and i in Y_STEPS:
                                    project_out(b - 1, u + 2, Y_STEPS.index(i))
                                if (hp, i) == H2T_AT:
                                    transpose_ln(2 * b + 1, (kl_done, u + 2))
                            if not is_const(b, LAST) and (hp, i) == H1T_AT and main:
                                transpose_ln(2 * b + 2, (kl_done, u + 2))

                    def batch(b):
                        for hp in range(HP):
                            slot(b, hp, tail=not (is_const(b, 0) and hp == 0))

                    transpose_ln(1)
                    for hp in range(2):
                        for t in range(NT):
                            project(hp, hp, 0, t)
                    transpose_q(0, 0, (h1_done, 1))
                    transpose_k(0, 0)
                    over_batches(pe, batch)
                    slot(B, 0, main=False)
                    for half in range(2):
                        project_out(LAST, HP * B, half)
                    transpose_y(LAST)
                    transpose_ln(2 * B, (x1_done, B))
                    router(LAST, 0)

                @block.scalar
                def _(act):
                    def copy_projection(u, hp, t):
                        act.wait_ge(pj_ready, NT * u + t + 1)
                        if t == 0:
                            after(act, av_done, u - 3)
                        nc.scalar.activation(qk_tok[:, hp % 2, t], PJ_BANK[:, 0:2 * P], ACT.Copy).then_inc(pj_copied, 1)
                        nc.scalar.activation(v_tok[:, hp % 4, t], PJ_BANK[:, 2 * P:3 * P], ACT.Copy).then_inc(v_copied, 1)

                    def square_projection(u, hp, t):
                        act.wait_ge(pj_copied, NT * u + t + 1)
                        if t == 0:
                            after(act, ss_done, 2 * u)
                        nc.scalar.activation(sq[:, t], qk_tok[:, hp % 2, t], ACT.Square).then_inc(sq_done, 1)

                    def high_q(u, hp):
                        act.wait_ge(qt_ready, u + 1)
                        after(act, stack_a, 32 * u)
                        after(act, stack_b, 32 * u)
                        nc.scalar.activation(parts[:, QH], XT_BANK[:], ACT.Copy,
                                             scale=qk_scale[:, hp % HP:hp % HP + 1]).then_inc(qh_done, 1)

                    def high_k(u):
                        act.wait_ge(kt_ready, u + 1)
                        nc.scalar.activation(parts[:, KH], XT_BANK[:], ACT.Copy).then_inc(kh_done, 1)

                    def exponentials(u, hp, i):
                        g = S_TILES * u + i
                        act.wait_ge(max_done, g + 1)
                        after(act, t_ready, g - 3)
                        if i == 0:
                            after(act, inv_done, u - 1)
                        nc.scalar.activation(probs[:, i % 4], S_BANK[i % 3][:], ACT.Exp, bias=neg_max[:, i:i + 1],
                                             accum_out=row_sum[:, hp % 2, i:i + 1]).then_inc(p_done, 1)

                    def copy_transposed(u, hp, i):
                        act.wait_ge(t_ready, S_TILES * u + i + 1)
                        if i == 1:
                            after(act, av_done, u - 1)
                        head, t = i // NT, i % NT
                        nc.scalar.activation(probsT[:, hp % 2, head, :, t * P:(t + 1) * P],
                                             T_BANK[i % 2][:].rearrange("p (j q) -> p j q", j=NT),
                                             ACT.Copy).then_inc(t_act, 1)

                    def copy_inverse(u):
                        act.wait_ge(r_ready, u + 1)
                        after(act, o_done, u)
                        nc.scalar.activation(inv_row[:], PJ_BANK[:], ACT.Copy).then_inc(r_copied, 1)

                    def modulate1(b):
                        act.wait_ge(hlnT_ready, 2 * b if not isinstance(b, int) else max(2 * b, 1))
                        act.wait_ge(mod1_done, b + 1)
                        nc.scalar.activation(m_out[:], M_BANK[:], ACT.Identity, scale=mod1[:, 0:1],
                                             bias=mod1[:, 1:2]).then_inc(h1_done, 1)

                    def gate_y(b):
                        act.wait_ge(y_ready, b + 1)
                        act.wait_ge(mod2_done, b + 1)
                        act.wait_ge(hT_ready, b + 2 if not is_const(b, LAST) else LAST + 1)
                        nc.scalar.activation(m_out[:], M_BANK[:], ACT.Identity, scale=mod2[:, 0:1],
                                             bias=mod2[:, 1:2]).then_inc(y_done, 1)

                    def modulate2(b, count):
                        act.wait_ge(hlnT_ready, count)
                        nc.scalar.activation(m_out[:], M_BANK[:], ACT.Identity, scale=mod2[:, 2:3],
                                             bias=mod2[:, 3:4]).then_inc(h2_done, 1)

                    def keep_h2(b):
                        act.wait_ge(h2_done, b + 1)
                        nc.scalar.activation(h2_all[:, bass.ts(b, N)], m_out[:], ACT.Copy).then_inc(h2_kept, 1)

                    def slot(b, hp, main=True, tail=True):
                        u = HP * b + hp
                        front_a = main and not (is_const(b, LAST) and hp + 2 >= HP)
                        front_b = main and not (is_const(b, LAST) and hp + 1 >= HP)
                        for i in range(S_TILES):
                            if not is_const(b, 0) and main:
                                if (hp, i) == (Y_SLOT, Y_STEPS[-1] + 1):
                                    gate_y(b - 1)
                                if (hp, i) == (H2T_AT[0], H2T_AT[1] + 1):
                                    modulate2(b - 1, 2 * b + 1)
                            if front_a and i < NT:
                                copy_projection(u + 2, hp + 2, i)
                            if front_b and i == KT_AT + 1:
                                high_k(u + 1)
                            if main and i > P_LAG:
                                copy_transposed(u, hp, i - P_LAG)
                            if front_a and i < NT:
                                square_projection(u + 2, hp + 2, i)
                            if main:
                                exponentials(u, hp, i)
                            if front_b and i == QT_AT:
                                high_q(u + 1, hp + 1)
                            if tail and i == 6:
                                copy_inverse(u - 1)
                            if not is_const(b, 0) and main and (hp, i) == (H2T_AT[0], H2T_AT[1] + 1):
                                keep_h2(b - 1)
                            if not is_const(b, LAST) and (hp, i) == (H1T_AT[0], H1T_AT[1] + 1) and main:
                                modulate1(b + 1)

                    def batch(b):
                        for hp in range(HP):
                            slot(b, hp, tail=not (is_const(b, 0) and hp == 0))

                    modulate1(0)
                    for hp in range(2):
                        for t in range(NT):
                            copy_projection(hp, hp, t)
                            square_projection(hp, hp, t)
                    high_q(0, 0)
                    high_k(0)
                    over_batches(act, batch)
                    slot(B, 0, main=False)
                    gate_y(LAST)
                    modulate2(LAST, 2 * B)
                    keep_h2(LAST)

                @block.vector
                def _(dve):
                    def sum_squares(u, half):
                        dve.wait_ge(sq_done, NT * u + 2 * half + 2)
                        if half == 0:
                            after(dve, qn_done, u)
                        nc.vector.reduce_sum(ss[:, 8 * half:8 * half + 8],
                                             sq[:, 2 * half:2 * half + 2].rearrange("p t (n d) -> p (t n) d", d=DH),
                                             AX.X).then_inc(ss_done, 1)

                    def guard_squares(u):
                        dve.wait_ge(ss_done, 2 * u + 2)
                        nc.vector.tensor_scalar(ss[:], ss[:], NORM_EPS ** 2, None, ALU.max).then_inc(ss_max, 1)

                    def guess_norms(u):
                        dve.wait_ge(ss_max, u + 1)
                        rsqrt_guess(nc, rn[:], ss_half[:], ss[:], rn_guess)

                    def low_q(u, hp):
                        dve.wait_ge(qh_done, u + 1)
                        nc.vector.scalar_tensor_tensor(out=parts[:, QL], in0=XT_BANK[:],
                                                       scalar=qk_scale[:, hp % HP:hp % HP + 1],
                                                       in1=parts[:, QH].bitcast(F32), op0=ALU.mult,
                                                       op1=ALU.subtract).then_inc(ql_done, 1)

                    def low_k(u):
                        dve.wait_ge(kh_done, u + 1)
                        nc.vector.tensor_tensor(parts[:, KL], XT_BANK[:], parts[:, KH].bitcast(F32),
                                                ALU.subtract).then_inc(kl_done, 1)

                    def row_max(u, i):
                        dve.wait_ge(s_ready, S_TILES * u + i + 1)
                        nc.vector.reduce_max(neg_max[:, i:i + 1], S_BANK[i % 3][:], AX.X, negate=True).then_inc(max_done, 1)

                    def copy_transposed(u, hp, i):
                        dve.wait_ge(t_ready, S_TILES * u + i + 1)
                        if i == 0:
                            after(dve, av_done, u - 1)
                        head, t = i // NT, i % NT
                        nc.vector.tensor_copy(probsT[:, hp % 2, head, :, t * P:(t + 1) * P],
                                              T_BANK[i % 2][:].rearrange("p (j q) -> p j q", j=NT)).then_inc(t_dve, 1)

                    def invert_sums(u, hp):
                        dve.wait_ge(p_done, S_TILES * (u + 1))
                        after(dve, wide_done, u - 1)
                        nc.vector.reciprocal(inv_sum[:, hp % 2], row_sum[:, hp % 2]).then_inc(inv_done, 1)

                    def normalise(u):
                        dve.wait_ge(av_done, u + 1)
                        dve.wait_ge(r_copied, u + 1)
                        after(dve, ol_done, u)
                        nc.vector.tensor_tensor(oT[:], O_BANK[:], inv_row[:], ALU.mult).then_inc(o_done, 1)

                    def high_o(u, hp, b):
                        dve.wait_ge(o_done, u + 1)
                        after(dve, y_ready, b)
                        nc.vector.tensor_copy(oT_h[:, hp % HP], oT[:]).then_inc(oh_done, 1)

                    def tile_of(b, t):
                        return x1_all[:, bass.ds(b * NT + t, 1)].rearrange("p o c -> p (o c)")

                    def tile_stats(b, count):
                        for t in range(NT):
                            nc.vector.bn_stats(stats[:, t], tile_of(b, t)).then_inc(st1_done, 1)

                    def stats_there(count):
                        dve.wait_ge(st1_done, (2 * NT) * count + NT)
                        after(dve, hln_done, count)

                    def aggregate(count):
                        for t in range(NT):
                            nc.vector.bn_aggr(mean_var[:, t], stats[:, t]).then_inc(st1_done, 1)
                        dve.wait_ge(st1_done, (2 * NT) * (count + 1))
                        after(dve, ln_step, NEWTON_OPS * count)
                        nc.vector.tensor_scalar(var_eps[:], mean_var[:, :, 1], LN_EPS, None, ALU.add).then_inc(ve_done, 1)

                    def guess_std(count):
                        dve.wait_ge(ve_done, count + 1)
                        rsqrt_guess(nc, rstd[:], var_half[:], var_eps[:], ln_guess)

                    def ln_rows(b, count):
                        dve.wait_ge(ln_step, NEWTON_OPS * (count + 1))
                        after(dve, hlnT_ready, count)
                        for t in range(NT):
                            last = nc.vector.tensor_scalar(
                                h_ln[:, t], tile_of(b, t),
                                mean_var[:, t, 0:1], rstd[:, t:t + 1], ALU.subtract, ALU.mult)
                        last.then_inc(hln_done, 1)

                    def take_mod(dst, cols, b, done, free):
                        after(dve, *free)
                        for k, v in enumerate(cols):
                            last = nc.vector.tensor_copy(dst[:, k:k + 1], modT[:, v, bass.ts(b, 1)])
                        last.then_inc(done, 1)

                    def high_h1(b):
                        dve.wait_ge(h1_done, b + 1)
                        after(dve, pj_ready, NT * HP * b)
                        nc.vector.tensor_copy(hT_h[:], m_out[:]).then_inc(h1h_done, 1)

                    def low_h1(b):
                        dve.wait_ge(h1h_done, b + 1)
                        nc.vector.tensor_tensor(hT_l[:], m_out[:], hT_h[:].bitcast(F32), ALU.subtract).then_inc(hT_ready, 1)

                    def residual(b):
                        dve.wait_ge(yT_ready, b + 1)
                        rows = x1_all[:, bass.ts(b, NT)]
                        nc.vector.tensor_tensor(rows, M_BANK[:].rearrange("p (t c) -> p t c", t=NT), rows,
                                                ALU.add).then_inc(x1_done, 1)

                    def logits(b):
                        dve.wait_ge(z_ready, b + 1)
                        rows = z_all[:, bass.ts(b, NT)]
                        nc.vector.tensor_tensor(rows, M_BANK[:, 0:NT * E].rearrange("p (t e) -> p t e", t=NT),
                                                projb_row[:].unsqueeze(1).to_broadcast([P, NT, E]), ALU.add).then_inc(z_done, 1)

                    def slot(b, hp, main=True, tail=True):
                        u = HP * b + hp
                        front_a = main and not (is_const(b, LAST) and hp + 2 >= HP)
                        front_b = main and not (is_const(b, LAST) and hp + 1 >= HP)
                        for i in range(S_TILES):
                            if main and not is_const(b, 0) and (hp, i) == (2, 5):
                                dve.wait_ge(x1_done, b)
                            if main and not is_const(b, 0) and (hp, i) == (2, 6):
                                stats_there(2 * b)
                            if main and not is_const(b, LAST) and (hp, i) == (3, 7):
                                stats_there(2 * b + 1)
                            if main:
                                row_max(u, i)
                            if tail and i < P_LAG:
                                copy_transposed(u - 1, hp - 1, S_TILES - P_LAG + i)
                            if tail and i == 1:
                                invert_sums(u - 1, hp - 1)
                            if main and i == P_LAG:
                                copy_transposed(u, hp, 0)
                            if front_b and i == QT_AT + 1:
                                low_q(u + 1, hp + 1)
                            if front_b and i == KT_AT + 1:
                                low_k(u + 1)
                            if front_a and i in (3, 4):
                                sum_squares(u + 2, i - 3)
                            if front_a and i == 5:
                                guard_squares(u + 2)
                                guess_norms(u + 2)
                            if tail and i == 7:
                                normalise(u - 1)
                                high_o(u - 1, hp - 1, b if hp > 0 else b - 1)
                            if not is_const(b, 0) and main:
                                if (hp, i) == (0, 5):
                                    take_mod(mod2, (GA, GA_BO, CB, SB), b - 1, mod2_done, (h2_done, b - 1))
                                if (hp, i) == YT_AT:
                                    residual(b - 1)
                                if (hp, i) == (2, 5):
                                    tile_stats(b - 1, 2 * b)
                                if (hp, i) == (2, 6):
                                    aggregate(2 * b)
                                if (hp, i) == (2, 7):
                                    guess_std(2 * b)
                                if (hp, i) == (3, 5):
                                    ln_rows(b - 1, 2 * b)
                                if (hp, i) == Z_AT:
                                    logits(b - 1)
                            if not is_const(b, LAST) and main:
                                nth = 2 * b + 1
                                if (hp, i) == (3, 6):
                                    tile_stats(b + 1, nth)
                                    take_mod(mod1, (CA, SA), b + 1, mod1_done, (h1_done, b + 1))
                                if (hp, i) == (3, 7):
                                    aggregate(nth)
                                if (hp, i) == (4, 0):
                                    guess_std(nth)
                                if (hp, i) == (4, 5):
                                    ln_rows(b + 1, nth)
                                if (hp, i) == (5, 5):
                                    high_h1(b + 1)
                                if (hp, i) == (5, 6):
                                    low_h1(b + 1)

                    def batch(b):
                        for hp in range(HP):
                            slot(b, hp, tail=not (is_const(b, 0) and hp == 0))

                    take_mod(mod1, (CA, SA), 0, mod1_done, (h1_done, 0))
                    tile_stats(0, 0)
                    stats_there(0)
                    aggregate(0)
                    guess_std(0)
                    ln_rows(0, 0)
                    high_h1(0)
                    low_h1(0)
                    for u in range(2):
                        sum_squares(u, 0)
                        sum_squares(u, 1)
                        guard_squares(u)
                        guess_norms(u)
                    low_q(0, 0)
                    low_k(0)
                    over_batches(dve, batch)
                    slot(B, 0, main=False)
                    take_mod(mod2, (GA, GA_BO, CB, SB), LAST, mod2_done, (h2_done, LAST))
                    residual(LAST)
                    dve.wait_ge(x1_done, B)
                    tile_stats(LAST, 2 * B - 1)
                    stats_there(2 * B - 1)
                    aggregate(2 * B - 1)
                    guess_std(2 * B - 1)
                    ln_rows(LAST, 2 * B - 1)
                    logits(LAST)

                @block.gpsimd
                def _(pool):
                    def normalise_qk(u, hp):
                        pool.wait_ge(rn_guess, u + 1)
                        rsqrt_newton(nc, pool, rn[:], ss_half[:], rn_t[:], c15.to_broadcast([P, NT * 4]), rn_step, NEWTON_OPS * u)
                        pool.wait_ge(rn_step, NEWTON_OPS * (u + 1))
                        qk = qk_tok[:, hp % 2].rearrange("p t (n d) -> p (t n) d", d=DH)
                        nc.gpsimd.tensor_tensor(qk, qk, rn[:].unsqueeze(2).to_broadcast([P, NT * 4, DH]),
                                                ALU.mult).then_inc(qn_done, 1)

                    def widen(u, hp):
                        pool.wait_ge(inv_done, u + 1)
                        after(pool, r_ready, u)
                        src = inv_sum[:, hp % 2].rearrange("p (h t) -> p t h", h=2)
                        nc.gpsimd.tensor_tensor(inv_wide[:], src.unsqueeze(3).to_broadcast([P, NT, 2, DH]),
                                                c1.unsqueeze(2).unsqueeze(3).to_broadcast([P, NT, 2, DH]),
                                                ALU.mult).then_inc(wide_done, 1)

                    def low_o(u, hp):
                        pool.wait_ge(oh_done, u + 1)
                        nc.gpsimd.tensor_tensor(oT_l[:, hp % HP], oT[:], oT_h[:, hp % HP].bitcast(F32),
                                                ALU.subtract).then_inc(ol_done, 1)

                    def inverse_std(count):
                        pool.wait_ge(ln_guess, count + 1)
                        rsqrt_newton(nc, pool, rstd[:], var_half[:], rstd_t[:], c15.to_broadcast([P, NT]), ln_step, NEWTON_OPS * count)

                    def slot(b, hp, main=True, tail=True):
                        u = HP * b + hp
                        front_a = main and not (is_const(b, LAST) and hp + 2 >= HP)
                        if tail:
                            widen(u - 1, hp - 1)
                        if not is_const(b, 0) and main and hp == 3:
                            inverse_std(2 * b)
                        if not is_const(b, LAST) and main and hp == 4:
                            inverse_std(2 * b + 1)
                        if front_a:
                            normalise_qk(u + 2, hp + 2)
                        if tail:
                            low_o(u - 1, hp - 1)

                    def batch(b):
                        for hp in range(HP):
                            slot(b, hp, tail=not (is_const(b, 0) and hp == 0))

                    nc.gpsimd.memset(c15, 1.5).then_inc(s_const, 1)
                    nc.gpsimd.memset(c1, 1.0).then_inc(s_const, 1)
                    pool.wait_ge(s_const, 2)
                    inverse_std(0)
                    for u in range(2):
                        normalise_qk(u, u)
                    over_batches(pool, batch)
                    slot(B, 0, main=False)
                    inverse_std(2 * B - 1)

        TILES = SH // P + E * (EH // P)
        SHT = SH // P
        with ExitStack() as scope:
            sb, pb, sem = alloc(scope)
            up_h = sb("up_h", [P, TILES, P], F32R)
            up_l = sb("up_l", [P, TILES, P], F32R)
            down_h = sb("down_h", [P, TILES, P], F32R)
            down_l = sb("down_l", [P, TILES, P], F32R)
            up_bias = sb("up_bias", [P, TILES])
            b2_pad = sb("b2_pad", [P, C])
            h2_h = sb("h2_h", [P, T], F32R)
            h2_l = sb("h2_l", [P, T], F32R)
            gates = sb("gates", [P, TT, E])
            gatesT = sb("gatesT", [P, TT * E // P, P])
            gate_cols = sb("gate_cols", [P, T])
            shared = sb("shared", [P, T])
            act_out = sb("act_out", [P, 4, N])
            hid_h = sb("hid_h", [P, 4, N], F32R)
            hid_l = sb("hid_l", [P, 4, N], F32R)
            gate_scratch = nc.dram_tensor("gate_scratch", [TT * E, P], F32).ap()
            scratch_rows = gate_scratch.rearrange("(t e) k -> e t k", e=E)

            with ExitStack() as scope2:
                sb, pb, sem = alloc(scope2)
                raw_up = sb("raw_up", [P, TILES, P])
                raw_down = sb("raw_down", [P, TILES, P])
                ebias_row = sb("ebias_row", [P, E])
                s_shared = sem("s_shared")
                s_up = sem("s_up")
                s_down = sem("s_down")
                s_bias = sem("s_bias")
                s_zero = sem("s_zero")
                s_wt = sem("s_wt2")
                s_wh = sem("s_wh2")
                s_wl = sem("s_wl2")
                s_h2h = sem("s_h2h")
                s_h2l = sem("s_h2l")
                s_sig = sem("s_sig")
                rt = sem("rt")
                consts = sem("consts")
                count_in = sem("count_in")
                count_out = sem("count_out")
                thr = sem("thr")
                fin_in = sem("fin_in")
                fin_out = sem("fin_out")
                gates_done = sem("gates_done")
                gT2_ready = sem("gT2_ready")
                gT2_copied = sem("gT2_copied")
                gT2_out = sem("gT2_out")
                gT2_in = sem("gT2_in")
                up2_ready = sem("up2_ready")
                gelu2_done = sem("gelu2_done")
                hi2_done = sem("hi2_done")
                lo2_done = sem("lo2_done")
                down2_done = sem("down2_done")
                shared_kept = sem("shared_kept")

                def rt_tile(name, shape=(P, TT, E), dt=F32):
                    return sb(name, list(shape), dt)

                prob = rt_tile("prob")
                t1 = rt_tile("t1")
                t2 = rt_tile("t2")
                top1 = rt_tile("top1")
                top2 = rt_tile("top2")
                m1 = rt_tile("m1", (P, TT))
                m2 = rt_tile("m2", (P, TT))
                den = rt_tile("den", (P, TT))
                w1 = rt_tile("w1", (P, TT))
                w2 = rt_tile("w2", (P, TT))
                ranked = rt_tile("ranked", (P, E, TT))
                above = rt_tile("above", (P, E, TT))
                equal = rt_tile("equal", (P, E, TT))
                before = rt_tile("before", (P, E, TT))
                not_first = rt_tile("not_first", (P, E, TT))
                rev = rt_tile("rev", (P, E))
                rev_i = rt_tile("rev_i", (P, E), I32)
                ones = rt_tile("ones", (P, P))
                earlier = rt_tile("earlier", (P, P))
                thr_u = rt_tile("thr_u", (P, E), U32)
                cand_u = rt_tile("cand_u", (P, E), U32)
                bit_f = rt_tile("bit_f", (P, E))
                next_f = rt_tile("next_f", (P, E))
                bit_u = rt_tile("bit_u", (P, E), U32)
                less_u = rt_tile("less_u", (P, E), U32)
                inc_u = rt_tile("inc_u", (P, E), U32)
                part_count = rt_tile("part_count", (P, E))
                room = rt_tile("room", (P, E))
                BITS = 30

                def by_expert(tile):
                    return tile[:].rearrange("p t e -> p e t")

                wfull = sb("wfull", [P, 2, 4 * P])

                def weight_group(j):
                    low, high, raw = (up_l, up_h, raw_up) if j % 2 == 0 else (down_l, down_h, raw_down)
                    k = 4 * (j // 2)
                    flat = [w[:, k:k + 4].rearrange("p r c -> p (r c)") for w in (low, high)]
                    return flat[0], flat[1], wfull[:, j % 2], raw[:, k:k + 4]

                GROUPS = 2 * TILES // 4
                LAG2 = 2
                SEARCH_LESS = SHT * B - BITS
                FIN_BANKS, COUNT_BANK = bank[4:7], bank[7]
                H2_BANK, Y2_BANK = bank[0:2], bank[2]

                def chunks(engine, chunk):
                    chunk(0)
                    with engine.Fori(1, B) as c:
                        chunk(c)

                def first_chunk(c):
                    return isinstance(c, int) and c == 0

                with nc.Block() as block:
                    @block.sync
                    def _(sp):
                        sp.dma_start(ebias_row[:], expert_bias.partition_broadcast(P)).then_inc(s_bias, 16)
                        sp.dma_start(raw_up[:, 0:SHT], sh1_w.rearrange("(r p) c -> p r c", p=P)).then_inc(s_shared, 16)
                        sp.dma_start(raw_down[:, 0:SHT], sh2_w.rearrange("c (r h) -> c r h", h=P)).then_inc(s_shared, 16)
                        sp.dma_start(raw_up[:, SHT:], fc1_w.rearrange("e (r p) c -> p (e r) c", p=P)).then_inc(s_up, 16)
                        sp.dma_start(raw_down[:, SHT:].rearrange("p (e r) h -> p e (r h)", e=E),
                                     fc2_w.rearrange("e c h -> c e h")).then_inc(s_down, 16)
                        sp.dma_start(up_bias[:, 0:SHT], sh1_b.rearrange("(r p) -> p r", p=P)).then_inc(s_bias, 16)
                        sp.dma_start(up_bias[:, SHT:], fc1_b.rearrange("e (r p) -> p (e r)", p=P)).then_inc(s_bias, 16)
                        sp.wait_ge(s_zero, 2)
                        sp.dma_start(b2_pad[0:E, :], fc2_b).then_inc(s_bias, 16)
                        sp.wait_ge(s_bias, 64)
                        sp.wait_ge(gT2_copied, 1)
                        sp.dma_start(gate_scratch.rearrange("(h p) k -> p h k", p=P), gatesT[:]).then_inc(gT2_out, 16)
                        sp.wait_ge(gT2_out, 16)
                        sp.dma_start(gate_cols[0:E].rearrange("e (t k) -> e t k", k=P), scratch_rows).then_inc(gT2_in, 16)
                        sp.wait_ge(gT2_in, 16)

                    @block.gpsimd
                    def _(pool):
                        nc.gpsimd.memset(b2_pad[:], 0.0).then_inc(s_zero, 1)
                        nc.gpsimd.memset(gate_cols[:], 0.0).then_inc(s_zero, 1)
                        nc.gpsimd.iota(rev_i[:], pattern=[[-1, E]], base=E, channel_multiplier=0).then_inc(consts, 1)
                        nc.gpsimd.memset(ones[:], 1.0).then_inc(consts, 1)
                        pool.wait_ge(consts, 2)
                        nc.gpsimd.affine_select(out=earlier[:], in_=ones[:], compare_op=ALU.is_gt, fill=0.0,
                                                base=0, pattern=[[1, P]], channel_multiplier=-1).then_inc(consts, 1)
                        def split_group(j):
                            pool.wait_ge(s_wh, 2 * j + 2)
                            dst, hi, full, _ = weight_group(j)
                            nc.gpsimd.tensor_tensor(dst, full, hi.bitcast(F32), ALU.subtract).then_inc(s_wl, 1)

                        def split_h2(q):
                            pool.wait_ge(s_h2h, q + 1)
                            cols = slice(q * N, (q + 1) * N)
                            nc.gpsimd.tensor_tensor(h2_l[:, cols], h2_all[:, cols], h2_h[:, cols].bitcast(F32),
                                                    ALU.subtract).then_inc(s_h2l, 1)

                        def chunk(c):
                            for k in range(SHT):
                                n = SHT * c + k
                                pool.wait_ge(hi2_done, n + 1)
                                nc.gpsimd.tensor_tensor(hid_l[:, k], act_out[:, k], hid_h[:, k].bitcast(F32),
                                                        ALU.subtract).then_inc(lo2_done, 1)

                        for j in range(max(GROUPS, B)):
                            if j < GROUPS:
                                split_group(j)
                            if j < B:
                                split_h2(j)
                        chunks(pool, chunk)

                    @block.tensor
                    def _(pe):
                        def transpose_weights(j):
                            if j == 0:
                                pe.wait_ge(s_shared, 32)
                            if j == 2:
                                pe.wait_ge(s_up, 16)
                                pe.wait_ge(s_down, 16)
                            after(pe, s_wh, 2 * (j - 3))
                            raw = weight_group(j)[3]
                            for r in range(4):
                                last = nc.tensor.transpose(bank[j % 4][:, r * P:(r + 1) * P], raw[:, r], ident[:])
                            last.then_inc(s_wt, 1)

                        def count(m):
                            pe.wait_ge(count_in, m + 1)
                            nc.tensor.matmul(COUNT_BANK[:, 0:E], ones[:], part_count[:], start=True,
                                             stop=True).then_inc(count_out, 1)

                        def up(c, k):
                            after(pe, gelu2_done, SHT * c + k - 1)
                            if k == 0:
                                pe.wait_ge(s_h2l, c + 1)
                            cols = bass.ts(c, N)
                            nc.tensor.matmul(H2_BANK[k % 2][:], up_h[:, k], h2_h[:, cols], start=True, stop=False)
                            nc.tensor.matmul(H2_BANK[k % 2][:], up_l[:, k], h2_h[:, cols], start=False, stop=False)
                            nc.tensor.matmul(H2_BANK[k % 2][:], up_h[:, k], h2_l[:, cols], start=False,
                                             stop=True).then_inc(up2_ready, 1)

                        def down(c, k):
                            if k == 0:
                                after(pe, shared_kept, c)
                            pe.wait_ge(lo2_done, SHT * c + k + 1)
                            nc.tensor.matmul(Y2_BANK[:], down_h[:, k], hid_h[:, k], start=(k == 0), stop=False)
                            nc.tensor.matmul(Y2_BANK[:], down_l[:, k], hid_h[:, k], start=False, stop=False)
                            nc.tensor.matmul(Y2_BANK[:], down_h[:, k], hid_l[:, k], start=False,
                                             stop=(k == SHT - 1)).then_inc(down2_done, 1)

                        def chunk(c):
                            for k in range(SHT):
                                if not first_chunk(c):
                                    count(SHT * c + k - SEARCH_LESS)
                                elif k < SHT - SEARCH_LESS:
                                    count(k)
                                up(c, k)
                                if k >= LAG2:
                                    down(c, k - LAG2)
                                elif not first_chunk(c):
                                    down(c - 1, SHT + k - LAG2)

                        for j in range(GROUPS):
                            transpose_weights(j)
                        pe.wait_ge(s_wh, 2 * GROUPS)
                        pe.wait_ge(s_wl, GROUPS)
                        pe.wait_ge(consts, 3)
                        chunks(pe, chunk)
                        for k in range(SHT - LAG2, SHT):
                            down(B - 1, k)
                        pe.wait_ge(fin_in, 1)
                        nc.tensor.matmul(FIN_BANKS[2][:, 0:E], ones[:], part_count[:], start=True, stop=True).then_inc(fin_out, 1)
                        nc.tensor.matmul(FIN_BANKS[1][:, 0:E * TT], ones[:], equal[:].rearrange("p e t -> p (e t)"),
                                         start=True, stop=True).then_inc(fin_out, 1)
                        nc.tensor.matmul(FIN_BANKS[0][:, 0:E * TT], earlier[:], equal[:].rearrange("p e t -> p (e t)"),
                                         start=True, stop=True).then_inc(fin_out, 1)
                        pe.wait_ge(gates_done, 1)
                        for h in range(TT * E // P):
                            last = nc.tensor.transpose(COUNT_BANK[:, h * P:(h + 1) * P],
                                                       gates[:].rearrange("p t e -> p (t e)")[:, h * P:(h + 1) * P], ident[:])
                        last.then_inc(gT2_ready, 1)

                    @block.scalar
                    def _(act):
                        nc.scalar.activation(t1[:], z_all[:], ACT.Exp, scale=-1.0).then_inc(s_sig, 1)
                        def high_group(j):
                            act.wait_ge(s_wt, j + 1)
                            after(act, s_wl, j - 1)
                            _, hi, full, _ = weight_group(j)
                            nc.scalar.activation(full, bank[j % 4][:], ACT.Copy).then_inc(s_wh, 1)
                            nc.scalar.activation(hi, bank[j % 4][:], ACT.Copy).then_inc(s_wh, 1)

                        def high_h2(q):
                            cols = slice(q * N, (q + 1) * N)
                            nc.scalar.activation(h2_h[:, cols], h2_all[:, cols], ACT.Copy).then_inc(s_h2h, 1)

                        def keep(c):
                            act.wait_ge(down2_done, SHT * (c + 1))
                            nc.scalar.activation(shared[:, bass.ts(c, N)], Y2_BANK[:], ACT.Copy).then_inc(shared_kept, 1)

                        def chunk(c):
                            for k in range(SHT):
                                n = SHT * c + k
                                if k == LAG2 and not first_chunk(c):
                                    keep(c - 1)
                                act.wait_ge(up2_ready, n + 1)
                                after(act, lo2_done, n - 3)
                                nc.scalar.activation(act_out[:, k], H2_BANK[k % 2][:], ACT.Gelu,
                                                     bias=up_bias[:, k:k + 1]).then_inc(gelu2_done, 1)
                                act.wait_ge(gelu2_done, n + 1)
                                after(act, down2_done, n - 3)
                                nc.scalar.activation(hid_h[:, k], act_out[:, k], ACT.Copy).then_inc(hi2_done, 1)

                        for j in range(max(GROUPS, B)):
                            if j < GROUPS:
                                high_group(j)
                            if j < B:
                                high_h2(j)
                        act.wait_ge(s_bias, 64)
                        chunks(act, chunk)
                        keep(B - 1)
                        act.wait_ge(gT2_ready, 1)
                        nc.scalar.activation(gatesT[:].rearrange("p h k -> p (h k)"), COUNT_BANK[:, 0:TT * E],
                                             ACT.Copy).then_inc(gT2_copied, 1)

                    @block.vector
                    def _(dve):
                        steps = [0]

                        def link(instruction):
                            steps[0] += 1
                            instruction.then_inc(rt, 1)
                            dve.wait_ge(rt, steps[0])

                        def spread(row):
                            return row[:].unsqueeze(2).to_broadcast([P, TT, E])

                        dve.wait_ge(consts, 3)
                        link(nc.vector.tensor_copy(rev[:], rev_i[:]))
                        rev_all = rev[:].unsqueeze(1).to_broadcast([P, TT, E])
                        dve.wait_ge(s_sig, 1)
                        dve.wait_ge(s_bias, 64)
                        link(nc.vector.tensor_scalar(t1[:], t1[:], 1.0, None, ALU.add))
                        link(nc.vector.reciprocal(t1[:], t1[:]))
                        link(nc.vector.tensor_tensor(t1[:], t1[:], ebias_row[:].unsqueeze(1).to_broadcast([P, TT, E]), ALU.add))
                        link(nc.vector.tensor_scalar(t1[:], t1[:], CLIP, None, ALU.max))
                        link(nc.vector.reduce_max(m1[:], t1[:], AX.X))
                        link(nc.vector.reciprocal(m1[:], m1[:]))
                        link(nc.vector.tensor_tensor(t1[:], t1[:], spread(m1), ALU.mult))
                        link(nc.vector.reduce_sum(m1[:], t1[:], AX.X))
                        link(nc.vector.reciprocal(m1[:], m1[:]))
                        link(nc.vector.tensor_tensor(prob[:], t1[:], spread(m1), ALU.mult))

                        def first_max(values, best, choice):
                            link(nc.vector.reduce_max(best[:], values[:], AX.X))
                            link(nc.vector.tensor_tensor(t2[:], values[:], spread(best), ALU.is_equal))
                            link(nc.vector.tensor_tensor(t2[:], t2[:], rev_all, ALU.mult))
                            link(nc.vector.reduce_max(den[:], t2[:], AX.X))
                            link(nc.vector.tensor_tensor(choice[:], rev_all, spread(den), ALU.is_equal))

                        first_max(prob, m1, top1)
                        link(nc.vector.scalar_tensor_tensor(out=t1[:], in0=top1[:], scalar=-2.0, in1=prob[:],
                                                            op0=ALU.mult, op1=ALU.add))
                        first_max(t1, m2, top2)
                        link(nc.vector.tensor_tensor(den[:], m1[:], m2[:], ALU.add))
                        link(nc.vector.tensor_scalar(den[:], den[:], CLIP, None, ALU.max))
                        link(nc.vector.reciprocal(den[:], den[:]))
                        link(nc.vector.tensor_tensor(w1[:], m1[:], den[:], ALU.mult))
                        link(nc.vector.tensor_tensor(w2[:], m2[:], den[:], ALU.mult))
                        link(nc.vector.tensor_tensor(t1[:], top1[:], spread(w1), ALU.mult))
                        link(nc.vector.tensor_tensor(t2[:], top2[:], spread(w2), ALU.mult))
                        link(nc.vector.tensor_tensor(prob[:], t1[:], t2[:], ALU.add))
                        link(nc.vector.tensor_tensor(t1[:], top1[:], top2[:], ALU.add))
                        link(nc.vector.scalar_tensor_tensor(out=ranked[:], in0=by_expert(t1), scalar=-1.0,
                                                            in1=by_expert(prob), op0=ALU.add, op1=ALU.add))

                        link(nc.vector.memset(thr_u[:], 0))
                        link(nc.vector.memset(bit_f[:], float(2 ** (BITS - 1))))
                        link(nc.vector.tensor_copy(cand_u[:], bit_f[:]))
                        def search(m):
                            nc.vector.tensor_tensor(above[:], ranked[:],
                                                    cand_u[:].bitcast(F32).unsqueeze(2).to_broadcast([P, E, TT]),
                                                    ALU.is_ge).then_inc(thr, 1)
                            dve.wait_ge(thr, 7 * m + 1)
                            nc.vector.reduce_sum(part_count[:], above[:], AX.X).then_inc(count_in, 1)
                            nc.vector.tensor_scalar(next_f[:], bit_f[:], 0.5, None, ALU.mult).then_inc(thr, 1)
                            dve.wait_ge(thr, 7 * m + 2)
                            nc.vector.tensor_copy(bit_u[:], next_f[:]).then_inc(thr, 1)
                            dve.wait_ge(thr, 7 * m + 3)
                            nc.vector.tensor_tensor(less_u[:], thr_u[:], bit_u[:], ALU.bitwise_or).then_inc(thr, 1)
                            dve.wait_ge(count_out, m + 1)
                            nc.vector.scalar_tensor_tensor(out=inc_u[:], in0=COUNT_BANK[:, 0:E], scalar=float(CAP),
                                                           in1=bit_f[:], op0=ALU.is_ge, op1=ALU.mult).then_inc(thr, 1)
                            dve.wait_ge(thr, 7 * m + 5)
                            nc.vector.tensor_tensor(cand_u[:], less_u[:], inc_u[:], ALU.bitwise_or).then_inc(thr, 1)
                            nc.vector.tensor_tensor(thr_u[:], thr_u[:], inc_u[:], ALU.bitwise_or)
                            nc.vector.tensor_scalar(bit_f[:], bit_f[:], 0.5, None, ALU.mult).then_inc(thr, 1)
                            dve.wait_ge(thr, 7 * m + 7)

                        for m in range(BITS - SHT * (B - 1)):
                            search(m)
                        with dve.Fori(1, B) as c:
                            for k in range(SHT):
                                search(SHT * c + k - SEARCH_LESS)

                        thr_all = thr_u[:].bitcast(F32).unsqueeze(2).to_broadcast([P, E, TT])
                        link(nc.vector.tensor_tensor(above[:], ranked[:], thr_all, ALU.is_gt))
                        link(nc.vector.tensor_tensor(equal[:], ranked[:], thr_all, ALU.is_equal))
                        link(nc.vector.memset(not_first[:], 1.0))
                        link(nc.vector.memset(not_first[:, :, 0:1], 0.0))
                        nc.vector.reduce_sum(part_count[:], above[:], AX.X).then_inc(fin_in, 1)
                        dve.wait_ge(fin_out, 3)
                        link(nc.vector.tensor_scalar(room[:], FIN_BANKS[2][:, 0:E], -1.0, float(CAP), ALU.mult, ALU.add))
                        link(nc.vector.tensor_copy(before[:], FIN_BANKS[1][:, 0:E * TT].rearrange("p (e t) -> p e t", e=E)))
                        link(nc.vector.tensor_tensor_scan(t1[:].rearrange("p t e -> p (t e)"),
                                                          not_first[:].rearrange("p e t -> p (e t)"),
                                                          before[:].rearrange("p e t -> p (e t)"), 0.0, ALU.mult, ALU.add))
                        flat1 = t1[:].rearrange("p t e -> p (t e)").rearrange("p (e t) -> p e t", e=E)
                        link(nc.vector.tensor_tensor(before[:], flat1, before[:], ALU.subtract))
                        link(nc.vector.tensor_tensor(before[:], FIN_BANKS[0][:, 0:E * TT].rearrange("p (e t) -> p e t", e=E),
                                                     before[:], ALU.add))
                        link(nc.vector.tensor_tensor(before[:], before[:], room[:].unsqueeze(2).to_broadcast([P, E, TT]), ALU.is_lt))
                        link(nc.vector.tensor_tensor(before[:], before[:], equal[:], ALU.mult))
                        link(nc.vector.tensor_tensor(above[:], above[:], before[:], ALU.add))
                        nc.vector.tensor_tensor(by_expert(gates), above[:], by_expert(prob), ALU.mult).then_inc(gates_done, 1)

            sb, pb, sem = alloc(scope)
            ET = TILES - SHT
            LAG = 4
            gated = sb("gated", [P, 4, N])
            gate_rows = sb("gate_rows", [P, E, N])
            y_sum = sb("y_sum", [P, N])
            yT = sb("yT", [P, N])
            mod3 = sb("mod3", [P, 2])
            H_BANK, Y_BANK, Z_BANK = bank[0:4], bank[4], bank[6]
            rows_in = [sem(f"rows_in{e}") for e in range(E)]
            ysum_done = sem("ysum_done")
            up_ready = sem("up_ready")
            gelu_done = sem("gelu_done")
            gated_done = sem("gated_done")
            hi_done = sem("hi_done")
            lo_even = sem("lo_even")
            lo_odd = sem("lo_odd")
            down_done = sem("down_done")
            mod3_done = sem("mod3_done")
            yc_done = sem("yc_done")
            z3_ready = sem("z3_ready")
            out_done = sem("out_done")
            stored = sem("stored")

            def over_all(engine, batch):
                batch(0)
                with engine.Fori(1, B) as b:
                    batch(b)

            def none_before(b):
                return isinstance(b, int) and b == 0

            with nc.Block() as block:
                @block.sync
                def _(sp):
                    def store(b):
                        sp.wait_ge(out_done, b + 1)
                        sp.dma_start(out_tok[bass.ds(b, 1)].rearrange("o p t c -> p (o t) c"),
                                     x1_all[:, bass.ts(b, NT)]).then_inc(stored, 16)

                    def load_gates(b, e):
                        after(sp, gated_done, ET * (b - 1) + 2 * (e + 1))
                        sp.dma_start(gate_rows[:, e].rearrange("p (t k) -> p t k", t=NT),
                                     scratch_rows[e, bass.ts(b, NT)].partition_broadcast(P)).then_inc(rows_in[e], 16)

                    def batch(b, store_too=True):
                        for e in range(E):
                            if e == E // 2 and store_too:
                                store(b - 2)
                            load_gates(b, e)

                    batch(0, False)
                    batch(1, False)
                    with sp.Fori(2, B) as b:
                        batch(b)
                    store(B - 2)
                    store(B - 1)
                    sp.wait_ge(stored, 16 * B)

                @block.tensor
                def _(pe):
                    def up(b, k):
                        after(pe, gelu_done, ET * b + k - 3)
                        cols = bass.ts(b, N)
                        o, w = H_BANK[k % 4][:], SHT + k
                        nc.tensor.matmul(o, up_h[:, w], h2_h[:, cols], start=True, stop=False)
                        nc.tensor.matmul(o, up_l[:, w], h2_h[:, cols], start=False, stop=False)
                        nc.tensor.matmul(o, up_h[:, w], h2_l[:, cols], start=False, stop=True).then_inc(up_ready, 1)

                    def down(b, k):
                        if k == 0:
                            after(pe, ysum_done, b)
                            nc.tensor.matmul(Y_BANK[:], b2_pad[:], gate_cols[:, bass.ts(b, N)], start=True, stop=False)
                        pe.wait_ge((lo_even, lo_odd)[k % 2], ET // 2 * b + k // 2 + 1)
                        w = SHT + k
                        nc.tensor.matmul(Y_BANK[:], down_h[:, w], hid_h[:, k % 4], start=False, stop=False)
                        nc.tensor.matmul(Y_BANK[:], down_l[:, w], hid_h[:, k % 4], start=False, stop=False)
                        nc.tensor.matmul(Y_BANK[:], down_h[:, w], hid_l[:, k % 4], start=False,
                                         stop=(k == ET - 1)).then_inc(down_done, 1)

                    def back_to_tokens(b):
                        pe.wait_ge(yc_done, b + 1)
                        after(pe, out_done, b)
                        for t in range(NT):
                            last = nc.tensor.transpose(Z_BANK[:, t * P:(t + 1) * P], yT[:, t * P:(t + 1) * P], ident[:])
                        last.then_inc(z3_ready, 1)

                    def batch(b):
                        for k in range(ET):
                            if k == LAG - 1 and not none_before(b):
                                down(b - 1, ET - 1)
                            up(b, k)
                            if k >= LAG:
                                down(b, k - LAG)
                            elif k < LAG - 1 and not none_before(b):
                                down(b - 1, ET + k - LAG)
                            if k == 8 and not none_before(b):
                                back_to_tokens(b - 1)

                    over_all(pe, batch)
                    for k in range(ET - LAG, ET):
                        down(B - 1, k)
                    back_to_tokens(B - 1)

                @block.scalar
                def _(act):
                    def high(b, k):
                        n = ET * b + k
                        act.wait_ge(gated_done, n + 1)
                        after(act, down_done, n - 3)
                        nc.scalar.activation(hid_h[:, k % 4], gated[:, k % 4], ACT.Copy).then_inc(hi_done, 1)

                    def take_sum(b):
                        act.wait_ge(ysum_done, b + 1)
                        act.wait_ge(mod3_done, b + 1)
                        after(act, z3_ready, b)
                        nc.scalar.activation(yT[:], y_sum[:], ACT.Identity, scale=mod3[:, 0:1],
                                             bias=mod3[:, 1:2]).then_inc(yc_done, 1)

                    def batch(b):
                        for k in range(ET):
                            n = ET * b + k
                            act.wait_ge(up_ready, n + 1)
                            after(act, gated_done, n - 3)
                            nc.scalar.activation(act_out[:, k % 4], H_BANK[k % 4][:], ACT.Gelu,
                                                 bias=up_bias[:, SHT + k:SHT + k + 1]).then_inc(gelu_done, 1)
                            if k >= 1:
                                high(b, k - 1)
                            elif not none_before(b):
                                high(b - 1, ET - 1)
                            if k == 6 and not none_before(b):
                                take_sum(b - 1)

                    over_all(act, batch)
                    high(B - 1, ET - 1)
                    take_sum(B - 1)

                @block.vector
                def _(dve):
                    def low(b, k):
                        dve.wait_ge(hi_done, ET * b + k + 1)
                        nc.vector.tensor_tensor(hid_l[:, k % 4], gated[:, k % 4], hid_h[:, k % 4].bitcast(F32),
                                                ALU.subtract).then_inc(lo_odd, 1)

                    def add_shared(b):
                        dve.wait_ge(down_done, ET * (b + 1))
                        after(dve, yc_done, b)
                        nc.vector.tensor_tensor(y_sum[:], Y_BANK[:], shared[:, bass.ts(b, N)], ALU.add).then_inc(ysum_done, 1)

                    def take_mod3(b):
                        after(dve, yc_done, b)
                        for j, v in enumerate((GB, GB_B2)):
                            last = nc.vector.tensor_copy(mod3[:, j:j + 1], modT[:, v, bass.ts(b, 1)])
                        last.then_inc(mod3_done, 1)

                    def add_residual(b):
                        dve.wait_ge(z3_ready, b + 1)
                        rows = x1_all[:, bass.ts(b, NT)]
                        nc.vector.tensor_tensor(rows, Z_BANK[:].rearrange("p (t c) -> p t c", t=NT), rows,
                                                ALU.add).then_inc(out_done, 1)

                    def batch(b):
                        for k in range(ET):
                            n = ET * b + k
                            if k % 2 == 0:
                                dve.wait_ge(rows_in[k // 2], 16 * (b + 1))
                            if k == LAG - 1 and not none_before(b):
                                add_shared(b - 1)
                            dve.wait_ge(gelu_done, n + 1)
                            after(dve, (lo_even, lo_odd)[k % 2], ET // 2 * b + k // 2 - 1)
                            nc.vector.tensor_tensor(gated[:, k % 4], gate_rows[:, k // 2], act_out[:, k % 4],
                                                    ALU.mult).then_inc(gated_done, 1)
                            if k % 2 == 0 and k > 0:
                                low(b, k - 1)
                            elif k == 0 and not none_before(b):
                                low(b - 1, ET - 1)
                            if k == LAG and not none_before(b):
                                take_mod3(b - 1)
                            if k == 10 and not none_before(b):
                                add_residual(b - 1)

                    over_all(dve, batch)
                    low(B - 1, ET - 1)
                    add_shared(B - 1)
                    take_mod3(B - 1)
                    add_residual(B - 1)

                @block.gpsimd
                def _(pool):
                    def batch(b):
                        for k in range(0, ET, 2):
                            pool.wait_ge(hi_done, ET * b + k + 1)
                            nc.gpsimd.tensor_tensor(hid_l[:, k % 4], gated[:, k % 4], hid_h[:, k % 4].bitcast(F32),
                                                    ALU.subtract).then_inc(lo_even, 1)

                    over_all(pool, batch)


_INS = ["L0_attn_x", "L0_attn_Wq", "L0_attn_Wk", "L0_attn_Wv", "L0_attn_Wo", "L0_attn_bo", "L0_attn_q_scale",
        "L0_attn_k_scale", "L0_ffn_proj_w", "L0_ffn_proj_b", "L0_ffn_expert_bias", "L0_ffn_fc1_w", "L0_ffn_fc1_b",
        "L0_ffn_fc2_w", "L0_ffn_fc2_b", "L0_ffn_sh1_w", "L0_ffn_sh1_b", "L0_ffn_sh2_w", "L0_ffn_sh2_b", "L0_c",
        "L0_wmod"]


def kernel(**inputs):
    import numpy as np
    import concourse.bacc as bacc
    from concourse.bass_utils import run_bass_kernel_spmd

    nc = bacc.Bacc("TRN2", target_bir_lowering=False, num_devices=1)
    arrays, args = {}, []
    for name in _INS:
        a = np.ascontiguousarray(inputs[name])
        arrays[f"in_{name}"] = a
        args.append(nc.dram_tensor(f"in_{name}", a.shape, mybir.dt.from_np(a.dtype), kind="ExternalInput").ap())
    shape = arrays["in_L0_attn_x"].shape
    args.append(nc.dram_tensor("out_0", shape, F32, kind="ExternalOutput").ap())
    adaln_attention_moe(nc, *args)
    r = run_bass_kernel_spmd(nc, [arrays], core_ids=[0])
    return r.results[0]["out_0"]
```

```python
from contextlib import ExitStack

import concourse.bass as bass
from concourse import mybir

P = 128
ALU = mybir.AluOpType
ACT = mybir.ActivationFunctionType
AX = mybir.AxisListType
F32 = mybir.dt.float32
F32R = mybir.dt.float32r
I32 = mybir.dt.int32
U32 = mybir.dt.uint32

LN_EPS = 1e-5
NORM_EPS = 1e-12
CLIP = 1e-12
MIN_GATE = 0.25
EXPERTS_PER_TOKEN = 2
CAP_NUM, CAP_DEN = 5, 4
RSQRT_MAGIC = float(0x5F3759DF)

SA, CA, GA, SB, CB, GB, GA_BO, GB_B2 = range(8)

QL, KL, KH, QH = range(4)
ST_Q, ST_K, ST_KX = range(3)


def after(engine, semaphore, value):
    if not (isinstance(value, int) and value <= 0):
        engine.wait_ge(semaphore, value)


def rsqrt_guess(nc, out, half, x, done):
    nc.vector.tensor_scalar(half, x, -0.5, None, ALU.mult)
    nc.vector.tensor_scalar(out.bitcast(I32), x.bitcast(I32), -0.5, RSQRT_MAGIC, ALU.mult, ALU.add).then_inc(done, 1)


def rsqrt_newton(nc, pool, out, half, tmp, c15, step, done):
    for k in range(3):
        if k:
            pool.wait_ge(step, done + 4 * k)
        nc.gpsimd.tensor_tensor(tmp, out, out, ALU.mult).then_inc(step, 1)
        pool.wait_ge(step, done + 4 * k + 1)
        nc.gpsimd.tensor_tensor(tmp, tmp, half, ALU.mult).then_inc(step, 1)
        pool.wait_ge(step, done + 4 * k + 2)
        nc.gpsimd.tensor_tensor(tmp, tmp, c15, ALU.add).then_inc(step, 1)
        pool.wait_ge(step, done + 4 * k + 3)
        nc.gpsimd.tensor_tensor(out, out, tmp, ALU.mult).then_inc(step, 1)


NEWTON_OPS = 12


def adaln_attention_moe(nc, x, Wq, Wk, Wv, Wo, bo, q_scale, k_scale, proj_w, proj_b, expert_bias,
                        fc1_w, fc1_b, fc2_w, fc2_b, sh1_w, sh1_b, sh2_w, sh2_b, c, wmod, out):
    B, N, C = x.shape
    H, DH = q_scale.shape[0], q_scale.shape[2]
    E, EH = fc1_b.shape
    SH = sh1_b.shape[0]
    NT = N // P
    HP = H // 2
    TT = B * NT
    T = B * N
    CAP = -(-(-(-T * EXPERTS_PER_TOKEN // E)) * CAP_NUM // CAP_DEN)
    S_TILES = 2 * NT
    assert C == P and DH == 64 and N == 512 and HP % 4 == 0 and EH == 2 * P and SH % P == 0

    x_tok = x.rearrange("b (t p) c -> p (b t) c", p=P)
    out_tok = out.rearrange("b (t p) c -> b p t c", p=P)

    with ExitStack() as whole:
        whole.enter_context(nc.allow_non_contiguous_dma(reason="a few small vectors go on partitions"))

        def alloc(scope):
            def sb(name, shape, dt=F32):
                return scope.enter_context(nc.sbuf_tensor(name, shape, dt))

            def pb(name, shape=(P, 512)):
                return scope.enter_context(nc.psum_tensor(name, list(shape), F32))

            def sem(name):
                return scope.enter_context(nc.semaphore(name))
            return sb, pb, sem

        sb, pb, sem = alloc(whole)
        x1_all = sb("x1_all", [P, TT, C])
        h2_all = sb("h2_all", [P, T])
        z_all = sb("z_all", [P, TT, E])
        ident = sb("ident", [P, P])
        modT = sb("modT", [P, 8, B])
        projT = sb("projT", [P, E])
        projb_row = sb("projb_row", [P, E])
        sh2b_col = sb("sh2b_col", [P, 1])
        ebias_row = sb("ebias_row", [P, E])
        bank = [pb(f"bank{i}") for i in range(8)]

        operands = sb("operands", [P, 16 * N], F32R)
        stack = operands[:, 0:12 * N].rearrange("p (a h s n) -> p a h s n", a=2, h=2, s=3)
        parts = operands[:, 12 * N:].rearrange("p (k n) -> p k n", k=4)
        h2_h, h2_l = operands[:, 0:T], operands[:, T:2 * T]
        probsT = sb("probsT", [P, 2, 2, NT, N])
        TILES = SH // P + E * (EH // P)
        SHT = SH // P
        free = probsT[:].rearrange("p a h j q -> p (a h j q)")
        raw_up, raw_down = (free[:, k * TILES * P:(k + 1) * TILES * P].rearrange("p (r c) -> p r c", c=P)
                            for k in range(2))
        beyond_raw = free[:, 2 * TILES * P:]
        gate_rows = free[:, 0:E * N].rearrange("p (e n) -> p e n", e=E)
        y_sum, yT = free[:, E * N:(E + 1) * N], free[:, (E + 1) * N:(E + 2) * N]
        assert 2 * T <= 16 * N and 2 * TILES * P <= 4 * NT * N and (E + 2) * N <= 4 * NT * N
        s_shared = sem("s_shared")
        s_up = sem("s_up")
        s_down = sem("s_down")
        s_h2h = sem("s_h2h")
        s_h2l = sem("s_h2l")

        def high_h2(q):
            cols = slice(q * N, (q + 1) * N)
            nc.scalar.activation(h2_h[:, cols], h2_all[:, cols], ACT.Copy).then_inc(s_h2h, 1)

        def low_h2(pool, q):
            pool.wait_ge(s_h2h, q + 1)
            cols = slice(q * N, (q + 1) * N)
            nc.gpsimd.tensor_tensor(h2_l[:, cols], h2_all[:, cols], h2_h[:, cols].bitcast(F32),
                                    ALU.subtract).then_inc(s_h2l, 1)

        with ExitStack() as scope:
            sb, pb, sem = alloc(scope)
            wqkv_h = sb("wqkv_h", [P, 3, H * DH], F32R)
            wqkv_l = sb("wqkv_l", [P, 3, H * DH], F32R)
            wo_h = sb("wo_h", [P, HP, C], F32R)
            wo_l = sb("wo_l", [P, HP, C], F32R)
            qk_scale = sb("qk_scale", [P, HP])
            consts1 = sb("consts1", [P, 2])
            c15, c1 = consts1[:, 0:1], consts1[:, 1:2]
            h_ln = sb("h_ln", [P, NT, C])
            stats = sb("stats", [P, NT, 6])
            mean_var = sb("mean_var", [P, NT, 2])
            var_eps = sb("var_eps", [P, NT])
            var_half = sb("var_half", [P, NT])
            rstd = sb("rstd", [P, NT])
            rstd_t = sb("rstd_t", [P, NT])
            st1_done = sem("st1_done")
            ve_done = sem("ve_done")
            ln_guess = sem("ln_guess")
            ln_step = sem("ln_step")
            hln_done = sem("hln_done")
            hlnT_ready = sem("hlnT_ready")
            s_const = sem("s_const")
            x0_in = sem("x0_in")
            x_in = sem("x_in")

            def tile_of(b, t):
                return x1_all[:, bass.ds(b * NT + t, 1)].rearrange("p o c -> p (o c)")

            def tile_stats(b):
                for t in range(NT):
                    nc.vector.bn_stats(stats[:, t], tile_of(b, t)).then_inc(st1_done, 1)

            def stats_there(dve, count):
                dve.wait_ge(st1_done, (2 * NT) * count + NT)
                after(dve, hln_done, count)

            def aggregate(dve, count):
                for t in range(NT):
                    nc.vector.bn_aggr(mean_var[:, t], stats[:, t]).then_inc(st1_done, 1)
                dve.wait_ge(st1_done, (2 * NT) * (count + 1))
                after(dve, ln_step, NEWTON_OPS * count)
                nc.vector.tensor_scalar(var_eps[:], mean_var[:, :, 1], LN_EPS, None, ALU.add).then_inc(ve_done, 1)

            def guess_std(dve, count):
                dve.wait_ge(ve_done, count + 1)
                rsqrt_guess(nc, rstd[:], var_half[:], var_eps[:], ln_guess)

            def inverse_std(pool, count):
                pool.wait_ge(ln_guess, count + 1)
                rsqrt_newton(nc, pool, rstd[:], var_half[:], rstd_t[:], c15.to_broadcast([P, NT]), ln_step, NEWTON_OPS * count)

            def ln_rows(dve, b, count):
                dve.wait_ge(ln_step, NEWTON_OPS * (count + 1))
                after(dve, hlnT_ready, count)
                for t in range(NT):
                    last = nc.vector.tensor_scalar(h_ln[:, t], tile_of(b, t), mean_var[:, t, 0:1], rstd[:, t:t + 1],
                                                   ALU.subtract, ALU.mult)
                last.then_inc(hln_done, 1)

            with ExitStack() as scope0:
                sb, pb, sem = alloc(scope0)
                raw = sb("raw", [P, 3, HP, C])
                raw_o = sb("raw_o", [P, H * DH])
                wmod_sb = sb("wmod_sb", [P, 6 * C])
                cT = sb("cT", [P, B])
                eT = sb("eT", [P, B])
                siluT = sb("siluT", [P, B])
                mod_sb = sb("mod_sb", [P, 6 * B])
                clampT = sb("clampT", [P, 2, B])
                signT = sb("signT", [P, 2, B])
                bo_col = sb("bo_col", [P, 1])
                ks_col = sb("ks_col", [P, HP])
                qs_col = sb("qs_col", [P, HP])
                s_w = [sem(f"s_w{i}") for i in range(4)]
                s_mod_in = sem("s_mod_in")
                s_small = sem("s_small")
                s_ident = sem("s_ident")
                s_wt = sem("s_wt")
                s_wh = sem("s_wh")
                s_wl = sem("s_wl")
                s_exp = sem("s_exp")
                s_silu = sem("s_silu")
                s_mod = sem("s_mod")
                s_mc = sem("s_mc")

                with nc.Block() as block:
                    @block.sync
                    def _(sp):
                        for n, w in enumerate((Wq, Wk, Wv)):
                            sp.dma_start(raw[:, n], w.rearrange("(r p) c -> p r c", p=P)).then_inc(s_w[n], 16)
                            if n == 0:
                                sp.dma_start(x1_all[:, 0:NT], x_tok[:, 0:NT]).then_inc(x0_in, 16)
                        sp.dma_start(raw_o[:], Wo).then_inc(s_w[3], 16)
                        sp.dma_start(bo_col[:], bo.rearrange("(c o) -> c o", o=1)).then_inc(s_small, 16)
                        sp.dma_start(sh2b_col[:], sh2_b.rearrange("(c o) -> c o", o=1)).then_inc(s_small, 16)
                        for h in range(2):
                            sp.dma_start(qs_col[h * DH:(h + 1) * DH, :],
                                          q_scale.rearrange("(hp two) o d -> two d (hp o)", two=2)[h]).then_inc(s_small, 16)
                            sp.dma_start(ks_col[h * DH:(h + 1) * DH, :],
                                          k_scale.rearrange("(hp two) o d -> two d (hp o)", two=2)[h]).then_inc(s_small, 16)
                        sp.dma_start(projT[:], proj_w.rearrange("e c -> c e")).then_inc(s_small, 16)
                        sp.dma_start(projb_row[:], proj_b.partition_broadcast(P)).then_inc(s_small, 16)
                        sp.dma_start(ebias_row[:], expert_bias.partition_broadcast(P)).then_inc(s_small, 16)
                        sp.wait_ge(s_small, 9 * 16)
                        sp.dma_start(x1_all[:, NT:], x_tok[:, NT:]).then_inc(x_in, 16)

                    @block.gpsimd
                    def _(pool):
                        nc.gpsimd.memset(ident[:], 0.0).then_inc(s_ident, 1)
                        pool.wait_ge(s_ident, 1)
                        nc.gpsimd.affine_select(out=ident[:], in_=ident[:], compare_op=ALU.not_equal, fill=1.0,
                                                base=0, pattern=[[-1, P]], channel_multiplier=1).then_inc(s_ident, 1)
                        nc.gpsimd.memset(c15, 1.5).then_inc(s_const, 1)
                        nc.gpsimd.memset(c1, 1.0).then_inc(s_const, 1)
                        pool.wait_ge(s_const, 2)
                        inverse_std(pool, 0)

                    @block.tensor
                    def _(pe):
                        pe.wait_ge(s_ident, 2)
                        for n in range(4):
                            pe.wait_ge(s_w[n], 16)
                            for half in range(2):
                                for r in range(4):
                                    chunk = 4 * half + r
                                    src = raw[:, n, chunk] if n < 3 else raw_o[:, chunk * P:(chunk + 1) * P]
                                    last = nc.tensor.transpose(bank[2 * n + half][:, r * P:(r + 1) * P], src, ident[:])
                                last.then_inc(s_wt, 1)
                        pe.wait_ge(s_silu, 3)
                        pe.wait_ge(s_wl, 1)
                        for v in range(6):
                            last = nc.tensor.matmul(bank[0][:, v * B:(v + 1) * B], wmod_sb[:, v * C:(v + 1) * C],
                                                    siluT[:], start=True, stop=True)
                        last.then_inc(s_mod, 1)

                    def weight_part(parts, n, half):
                        w = parts[0] if n < 3 else parts[1]
                        flat = w[:, n] if n < 3 else w[:].rearrange("p h c -> p (h c)")
                        return flat[:, half * 512:(half + 1) * 512]

                    @block.scalar
                    def _(act):
                        act.dma_start(cT[:], c.rearrange("b c -> c b")).then_inc(s_mod_in, 16)
                        act.dma_start(wmod_sb[:], wmod).then_inc(s_mod_in, 16)
                        act.wait_ge(s_mod_in, 32)
                        nc.scalar.activation(eT[:], cT[:], ACT.Exp, scale=-1.0).then_inc(s_exp, 1)
                        for j in range(8):
                            act.wait_ge(s_wt, j + 1)
                            nc.scalar.activation(weight_part((wqkv_h, wo_h), j // 2, j % 2), bank[j][:],
                                                 ACT.Copy).then_inc(s_wh, 1)

                    @block.vector
                    def _(dve):
                        dve.wait_ge(s_exp, 1)
                        nc.vector.tensor_scalar(eT[:], eT[:], 1.0, None, ALU.add).then_inc(s_silu, 1)
                        dve.wait_ge(s_silu, 1)
                        nc.vector.reciprocal(eT[:], eT[:]).then_inc(s_silu, 1)
                        dve.wait_ge(s_silu, 2)
                        nc.vector.tensor_tensor(siluT[:], eT[:], cT[:], ALU.mult).then_inc(s_silu, 1)
                        dve.wait_ge(x0_in, 16)
                        tile_stats(0)
                        stats_there(dve, 0)
                        aggregate(dve, 0)
                        guess_std(dve, 0)
                        for j in range(8):
                            dve.wait_ge(s_wh, j + 1)
                            nc.vector.tensor_tensor(weight_part((wqkv_l, wo_l), j // 2, j % 2), bank[j][:],
                                                    weight_part((wqkv_h, wo_h), j // 2, j % 2).bitcast(F32),
                                                    ALU.subtract).then_inc(s_wl, 1)
                            if j == 5:
                                ln_rows(dve, 0, 0)
                        dve.wait_ge(s_small, 9 * 16)
                        nc.vector.scalar_tensor_tensor(out=qk_scale[:], in0=qs_col[:], scalar=float(DH) ** -0.5,
                                                       in1=ks_col[:], op0=ALU.mult, op1=ALU.mult)
                        dve.wait_ge(s_mod, 1)
                        nc.vector.tensor_copy(mod_sb[:], bank[0][:, 0:6 * B]).then_inc(s_mc, 1)
                        dve.wait_ge(s_mc, 1)
                        for v in (SA, SB):
                            nc.vector.tensor_copy(modT[:, v], mod_sb[:, v * B:(v + 1) * B])
                        for v in (CA, CB):
                            nc.vector.tensor_scalar(modT[:, v], mod_sb[:, v * B:(v + 1) * B], 1.0, None, ALU.add)
                        for k, v in enumerate((GA, GB)):
                            nc.vector.tensor_scalar(signT[:, k], mod_sb[:, v * B:(v + 1) * B], 0.0, 2.0,
                                                    ALU.is_ge, ALU.mult).then_inc(s_mc, 1)
                            nc.vector.scalar_tensor_tensor(out=clampT[:, k], in0=mod_sb[:, v * B:(v + 1) * B],
                                                           scalar=-1.0, in1=mod_sb[:, v * B:(v + 1) * B],
                                                           op0=ALU.mult, op1=ALU.max).then_inc(s_mc, 1)
                        dve.wait_ge(s_mc, 5)
                        nc.vector.tensor_scalar(clampT[:], clampT[:], MIN_GATE, None, ALU.max).then_inc(s_mc, 1)
                        dve.wait_ge(s_mc, 6)
                        for k, v in enumerate((GA, GB)):
                            nc.vector.scalar_tensor_tensor(out=modT[:, v], in0=signT[:, k], scalar=-1.0,
                                                           in1=clampT[:, k], op0=ALU.add, op1=ALU.mult).then_inc(s_mc, 1)
                        dve.wait_ge(s_mc, 8)
                        nc.vector.tensor_scalar(modT[:, GA_BO], modT[:, GA], bo_col[:], None, ALU.mult)
                        nc.vector.tensor_scalar(modT[:, GB_B2], modT[:, GB], sh2b_col[:], None, ALU.mult)

            sb, pb, sem = alloc(scope)
            hT_h = sb("hT_h", [P, N], F32R)
            hT_l = sb("hT_l", [P, N], F32R)
            qk_tok = sb("qk_tok", [P, 2, NT, 2 * P])
            v_tok = sb("v_tok", [P, 4, NT, P])
            sq = sb("sq", [P, NT, 2 * P])
            ss = sb("ss", [P, NT * 4])
            rn = sb("rn", [P, NT * 4])
            rn_t = sb("rn_t", [P, NT * 4])
            ss_half = sb("ss_half", [P, NT * 4])
            probs = sb("probs", [P, 4, N])
            neg_max = sb("neg_max", [P, S_TILES])
            row_sum = sb("row_sum", [P, 2, S_TILES])
            inv_sum = sb("inv_sum", [P, 2, S_TILES])
            inv_wide = sb("inv_wide", [P, NT, 2, DH])
            inv_row = sb("inv_row", [P, N])
            oT = sb("oT", [P, N])
            oT_h = sb("oT_h", [P, HP, N], F32R)
            oT_l = sb("oT_l", [P, HP, N], F32R)
            m_out = sb("m_out", [P, N])
            mod1 = sb("mod1", [P, 2])
            mod2 = sb("mod2", [P, 4])

            S_BANK, T_BANK, O_BANK, PJ_BANK = bank[0:3], bank[3:5], bank[5], bank[6]
            FRONT_BANKS = bank[0:7] + bank[0:1]
            XT_BANK = M_BANK = bank[7]

            hT_ready = sem("hT_ready")
            pj_ready = sem("pj_ready")
            pj_copied = sem("pj_copied")
            v_copied = sem("v_copied")
            sq_done = sem("sq_done")
            ss_done = sem("ss_done")
            ss_max = sem("ss_max")
            rn_guess = sem("rn_guess")
            rn_step = sem("rn_step")
            qn_done = sem("qn_done")
            qt_ready = sem("qt_ready")
            qh_done = sem("qh_done")
            ql_done = sem("ql_done")
            kt_ready = sem("kt_ready")
            kh_done = sem("kh_done")
            kl_done = sem("kl_done")
            stack_a = sem("stack_a")
            stack_b = sem("stack_b")
            s_ready = sem("s_ready")
            max_done = sem("max_done")
            p_done = sem("p_done")
            t_ready = sem("t_ready")
            t_dve = sem("t_dve")
            t_act = sem("t_act")
            inv_done = sem("inv_done")
            wide_done = sem("wide_done")
            r_ready = sem("r_ready")
            r_copied = sem("r_copied")
            av_done = sem("av_done")
            o_done = sem("o_done")
            oh_done = sem("oh_done")
            ol_done = sem("ol_done")
            mod1_done = sem("mod1_done")
            h1_done = sem("h1_done")
            h1h_done = sem("h1h_done")
            y_ready = sem("y_ready")
            y_done = sem("y_done")
            yT_ready = sem("yT_ready")
            mod2_done = sem("mod2_done")
            x1_done = sem("x1_done")
            h2_done = sem("h2_done")
            h2_kept = sem("h2_kept")
            z_ready = sem("z_ready")
            z_done = sem("z_done")

            QT_AT, KT_AT = 1, 3
            Y_SLOT, Y_STEPS = 1, (5, 6)
            YT_AT, H2T_AT, Z_AT, H1T_AT = (2, 0), (3, 6), (4, 0), (4, 6)

            LAST = B - 1
            H2_EARLY, H2_MID = 1, 4
            P_LAG = 3

            def over_batches(engine, batch):
                batch(0)
                with engine.Fori(1, LAST) as b:
                    batch(b)
                batch(LAST)

            def is_const(b, value):
                return isinstance(b, int) and b == value

            with nc.Block() as block:

                @block.sync
                def _(sp):
                    def stacks(u, hp):
                        sp.wait_ge(kl_done, u + 1)
                        for head in range(2):
                            own, other = (0, DH) if head == 0 else (DH, 0)
                            src = parts[own:own + DH]
                            dst = stack[:, hp % 2, head]
                            there = (stack_a, stack_b)[head]
                            sp.dma_start(dst[own:own + DH].bitcast(F32), src[:, QH:QL:-1].bitcast(F32)).then_inc(there, 16)
                            sp.dma_start(dst[other:other + DH].bitcast(F32), src[:, QL:QH].bitcast(F32)).then_inc(there, 16)

                    def batch(b):
                        for hp in range(HP):
                            stacks(HP * b + hp, hp)

                    over_batches(sp, batch)
                    sp.wait_ge(av_done, HP * B)
                    sp.dma_start(raw_up[:, 0:SHT], sh1_w.rearrange("(r p) c -> p r c", p=P)).then_inc(s_shared, 16)
                    sp.dma_start(raw_down[:, 0:SHT], sh2_w.rearrange("c (r h) -> c r h", h=P)).then_inc(s_shared, 16)
                    sp.dma_start(raw_up[:, SHT:], fc1_w.rearrange("e (r p) c -> p (e r) c", p=P)).then_inc(s_up, 16)
                    sp.dma_start(raw_down[:, SHT:].rearrange("p (e r) h -> p e (r h)", e=E),
                                 fc2_w.rearrange("e c h -> c e h")).then_inc(s_down, 16)

                @block.tensor
                def _(pe):
                    def project(u, hp, wb, t, front=None):
                        if front is not None:
                            pe.wait_ge(hT_ready, 1)
                            after(pe, v_copied, front + 1 - 7)
                        elif t == 0:
                            pe.wait_ge(hT_ready, wb + 1)
                            after(pe, r_copied, u - 3)
                            after(pe, v_copied, NT * u)
                        else:
                            pe.wait_ge(v_copied, NT * u + t)
                        o = (PJ_BANK if front is None else FRONT_BANKS[front])[:, 0:3 * P].rearrange("p (n c) -> p n c", n=3)
                        cols = slice(hp * P, (hp + 1) * P)
                        toks = slice(t * P, (t + 1) * P)
                        nc.tensor.matmul(o, hT_h[:, toks], wqkv_h[:, :, cols], start=True, stop=False)
                        nc.tensor.matmul(o, hT_h[:, toks], wqkv_l[:, :, cols], start=False, stop=False)
                        nc.tensor.matmul(o, hT_l[:, toks], wqkv_h[:, :, cols], start=False,
                                         stop=True).then_inc(pj_ready, 1)

                    def transpose_q(u, hp, *free):
                        pe.wait_ge(qn_done, u + 1)
                        for semaphore, value in free:
                            after(pe, semaphore, value)
                        for t in range(NT):
                            last = nc.tensor.transpose(XT_BANK[:, t * P:(t + 1) * P], qk_tok[:, hp % 2, t, 0:P], ident[:])
                        last.then_inc(qt_ready, 1)

                    def transpose_k(u, hp):
                        pe.wait_ge(ql_done, u + 1)
                        for t in range(NT):
                            last = nc.tensor.transpose(XT_BANK[:, t * P:(t + 1) * P], qk_tok[:, hp % 2, t, P:2 * P], ident[:])
                        last.then_inc(kt_ready, 1)

                    def scores(u, hp, i):
                        g = S_TILES * u + i
                        if i == 0:
                            pe.wait_ge(stack_a, 32 * (u + 1))
                        if i == NT:
                            pe.wait_ge(stack_b, 32 * (u + 1))
                        after(pe, p_done, g - (2 if i >= 3 else 4 if i == 2 else 1))
                        head, t = i // NT, i % NT
                        st = stack[:, hp % 2, head]
                        q = st[:, ST_Q, t * P:(t + 1) * P]
                        nc.tensor.matmul(S_BANK[i % 3][:], q, st[:, ST_K], start=True, stop=False)
                        nc.tensor.matmul(S_BANK[i % 3][:], q, st[:, ST_KX], start=False, stop=True).then_inc(s_ready, 1)

                    def transpose_probs(u, i):
                        pe.wait_ge(p_done, S_TILES * u + i + 1)
                        semaphore, count = {0: (t_dve, -1), 1: (t_dve, 0), 2: (t_dve, 1), 7: (t_dve, 2)}.get(i, (t_act, i - 2))
                        after(pe, semaphore, 4 * u + count)
                        for j in range(NT):
                            last = nc.tensor.transpose(T_BANK[i % 2][:, j * P:(j + 1) * P],
                                                       probs[:, i % 4, j * P:(j + 1) * P], ident[:])
                        last.then_inc(t_ready, 1)

                    def inverse_rows(u, hp, pj):
                        pe.wait_ge(wide_done, u + 1)
                        pe.wait_ge(v_copied, pj)
                        after(pe, r_copied, u)
                        for t in range(NT):
                            last = nc.tensor.transpose(PJ_BANK[:, t * P:(t + 1) * P],
                                                       inv_wide[:, t].rearrange("p h d -> p (h d)"), ident[:])
                        last.then_inc(r_ready, 1)

                    def weigh_values(u, hp, j):
                        if j == 0:
                            pe.wait_ge(t_dve, 4 * (u + 1))
                            pe.wait_ge(t_act, 4 * (u + 1))
                            after(pe, o_done, u)
                        for head in range(2):
                            rows = slice(head * DH, (head + 1) * DH)
                            last = nc.tensor.matmul(O_BANK[rows, :], v_tok[:, hp % 4, j, rows],
                                                    probsT[:, hp % 2, head, j], start=(j == 0), stop=(j == NT - 1),
                                                    skip_group_check=True)
                        if j == NT - 1:
                            last.then_inc(av_done, 1)

                    def project_out(b, u, pairs):
                        pe.wait_ge(ol_done, HP * b + pairs[-1] + 1)
                        if pairs[0] == 0:
                            after(pe, kl_done, u)
                        for hp in pairs:
                            nc.tensor.matmul(M_BANK[:], wo_h[:, hp], oT_h[:, hp], start=(hp == 0), stop=False)
                            nc.tensor.matmul(M_BANK[:], wo_l[:, hp], oT_h[:, hp], start=False, stop=False)
                            last = nc.tensor.matmul(M_BANK[:], wo_h[:, hp], oT_l[:, hp], start=False, stop=(hp == HP - 1))
                        if pairs[-1] == HP - 1:
                            last.then_inc(y_ready, 1)

                    def transpose_y(b):
                        pe.wait_ge(y_done, b + 1)
                        for t in range(NT):
                            last = nc.tensor.transpose(M_BANK[:, t * P:(t + 1) * P], m_out[:, t * P:(t + 1) * P], ident[:])
                        last.then_inc(yT_ready, 1)

                    def transpose_ln(count, *free):
                        pe.wait_ge(hln_done, count)
                        for semaphore, value in free:
                            after(pe, semaphore, value)
                        for t in range(NT):
                            last = nc.tensor.transpose(M_BANK[:, t * P:(t + 1) * P], h_ln[:, t], ident[:])
                        last.then_inc(hlnT_ready, 1)

                    def router(b, u):
                        pe.wait_ge(h2_done, b + 1)
                        after(pe, kl_done, u)
                        for t in range(NT):
                            last = nc.tensor.matmul(M_BANK[:, t * E:(t + 1) * E], m_out[:, t * P:(t + 1) * P], projT[:],
                                                    start=True, stop=True)
                        last.then_inc(z_ready, 1)

                    def slot(b, hp, main=True, tail=True):
                        u = HP * b + hp
                        front_a = main and not (is_const(b, LAST) and hp + 2 >= HP)
                        front_b = main and not (is_const(b, LAST) and hp + 1 >= HP)
                        for i in range(S_TILES):
                            if main:
                                scores(u, hp, i)
                            if tail and i >= S_TILES - NT:
                                weigh_values(u - 1, hp - 1, i - (S_TILES - NT))
                            if tail and i < P_LAG:
                                transpose_probs(u - 1, S_TILES - P_LAG + i)
                            if main and i >= P_LAG:
                                transpose_probs(u, i - P_LAG)
                            if front_a and i < NT:
                                project(u + 2, (hp + 2) % HP, b + (hp + 2) // HP, i)
                            if not is_const(b, 0) and main:
                                if (hp, i) == YT_AT:
                                    transpose_y(b - 1)
                                if (hp, i) == Z_AT:
                                    router(b - 1, u + 1)
                            if front_b and i == QT_AT:
                                side = {2: (x1_done, b), 4: (z_done, b), 5: (h1_done, b + 2)}
                                if is_const(b, LAST):
                                    side.pop(5)
                                transpose_q(u + 1, hp + 1, side.get(hp, (kl_done, u + 1)), (kl_done, u + 1))
                            if front_b and i == KT_AT:
                                transpose_k(u + 1, hp + 1)
                            if tail and i == 5:
                                pj = NT * (u + 3) if front_a else NT * HP * B
                                inverse_rows(u - 1, hp - 1, pj)
                            if not is_const(b, 0) and main:
                                if hp == Y_SLOT and i in Y_STEPS:
                                    half = Y_STEPS.index(i)
                                    project_out(b - 1, u + 2, range(half * HP // 2, (half + 1) * HP // 2))
                                if (hp, i) == H2T_AT:
                                    transpose_ln(2 * b + 1, (kl_done, u + 2))
                            if not is_const(b, LAST) and (hp, i) == H1T_AT and main:
                                transpose_ln(2 * b + 2, (kl_done, u + 2))

                    def batch(b):
                        for hp in range(HP):
                            slot(b, hp, tail=not (is_const(b, 0) and hp == 0))

                    transpose_ln(1)
                    for w in range(2):
                        for t in range(NT):
                            project(w, w, 0, t, front=NT * w + t)
                    transpose_q(0, 0, (h1_done, 1))
                    transpose_k(0, 0)
                    over_batches(pe, batch)
                    slot(B, 0, main=False)
                    project_out(LAST, HP * B, range(HP - 1))
                    project_out(LAST, HP * B, [HP - 1])
                    transpose_y(LAST)
                    transpose_ln(2 * B, (x1_done, B))
                    router(LAST, 0)

                @block.scalar
                def _(act):
                    def copy_projection(u, hp, t, bank=PJ_BANK):
                        act.wait_ge(pj_ready, NT * u + t + 1)
                        if t == 0:
                            after(act, av_done, u - 3)
                        nc.scalar.activation(qk_tok[:, hp % 2, t], bank[:, 0:2 * P], ACT.Copy).then_inc(pj_copied, 1)
                        nc.scalar.activation(v_tok[:, hp % 4, t], bank[:, 2 * P:3 * P], ACT.Copy).then_inc(v_copied, 1)

                    def square_projection(u, hp, t):
                        act.wait_ge(pj_copied, NT * u + t + 1)
                        if t == 0:
                            after(act, ss_done, 2 * u)
                        nc.scalar.activation(sq[:, t], qk_tok[:, hp % 2, t], ACT.Square).then_inc(sq_done, 1)

                    def high_q(u, hp):
                        act.wait_ge(qt_ready, u + 1)
                        after(act, stack_a, 32 * u)
                        after(act, stack_b, 32 * u)
                        nc.scalar.activation(parts[:, QH], XT_BANK[:], ACT.Copy,
                                             scale=qk_scale[:, hp % HP:hp % HP + 1]).then_inc(qh_done, 1)

                    def high_k(u):
                        act.wait_ge(kt_ready, u + 1)
                        nc.scalar.activation(parts[:, KH], XT_BANK[:], ACT.Copy).then_inc(kh_done, 1)

                    def exponentials(u, hp, i):
                        g = S_TILES * u + i
                        act.wait_ge(max_done, g + 1)
                        after(act, t_ready, g - 3)
                        if i == 0:
                            after(act, inv_done, u - 1)
                        nc.scalar.activation(probs[:, i % 4], S_BANK[i % 3][:], ACT.Exp, bias=neg_max[:, i:i + 1],
                                             accum_out=row_sum[:, hp % 2, i:i + 1]).then_inc(p_done, 1)

                    def copy_transposed(u, hp, i):
                        act.wait_ge(t_ready, S_TILES * u + i + 1)
                        if i == 1:
                            after(act, av_done, u - 1)
                        head, t = i // NT, i % NT
                        nc.scalar.activation(probsT[:, hp % 2, head, :, t * P:(t + 1) * P],
                                             T_BANK[i % 2][:].rearrange("p (j q) -> p j q", j=NT),
                                             ACT.Copy).then_inc(t_act, 1)

                    def copy_inverse(u):
                        act.wait_ge(r_ready, u + 1)
                        after(act, o_done, u)
                        nc.scalar.activation(inv_row[:], PJ_BANK[:], ACT.Copy).then_inc(r_copied, 1)

                    def modulate1(b):
                        act.wait_ge(hlnT_ready, 2 * b if not isinstance(b, int) else max(2 * b, 1))
                        act.wait_ge(mod1_done, b + 1)
                        nc.scalar.activation(m_out[:], M_BANK[:], ACT.Identity, scale=mod1[:, 0:1],
                                             bias=mod1[:, 1:2]).then_inc(h1_done, 1)

                    def gate_y(b):
                        act.wait_ge(y_ready, b + 1)
                        act.wait_ge(mod2_done, b + 1)
                        act.wait_ge(hT_ready, b + 2 if not is_const(b, LAST) else LAST + 1)
                        nc.scalar.activation(m_out[:], M_BANK[:], ACT.Identity, scale=mod2[:, 0:1],
                                             bias=mod2[:, 1:2]).then_inc(y_done, 1)

                    def modulate2(b, count):
                        act.wait_ge(hlnT_ready, count)
                        nc.scalar.activation(m_out[:], M_BANK[:], ACT.Identity, scale=mod2[:, 2:3],
                                             bias=mod2[:, 3:4]).then_inc(h2_done, 1)

                    def keep_h2(b):
                        act.wait_ge(h2_done, b + 1)
                        nc.scalar.activation(h2_all[:, bass.ts(b, N)], m_out[:], ACT.Copy).then_inc(h2_kept, 1)

                    def slot(b, hp, main=True, tail=True):
                        u = HP * b + hp
                        front_a = main and not (is_const(b, LAST) and hp + 2 >= HP)
                        front_b = main and not (is_const(b, LAST) and hp + 1 >= HP)
                        for i in range(S_TILES):
                            if not is_const(b, 0) and main:
                                if (hp, i) == (Y_SLOT, Y_STEPS[-1] + 1):
                                    gate_y(b - 1)
                                if (hp, i) == (H2T_AT[0], H2T_AT[1] + 1):
                                    modulate2(b - 1, 2 * b + 1)
                            if front_a and i < NT:
                                copy_projection(u + 2, hp + 2, i)
                            if front_b and i == KT_AT + 1:
                                high_k(u + 1)
                            if not is_const(b, LAST) and (hp, i) == (H1T_AT[0], H1T_AT[1] + 1) and main:
                                modulate1(b + 1)
                            if front_a and i < NT:
                                square_projection(u + 2, hp + 2, i)
                            if main:
                                exponentials(u, hp, i)
                            if main and i > P_LAG:
                                copy_transposed(u, hp, i - P_LAG)
                            if front_b and i == QT_AT:
                                high_q(u + 1, hp + 1)
                            if tail and i == 6:
                                copy_inverse(u - 1)
                            if not is_const(b, 0) and main and (hp, i) == (H2T_AT[0], H2T_AT[1] + 1):
                                keep_h2(b - 1)

                    def batch(b):
                        for hp in range(HP):
                            slot(b, hp, tail=not (is_const(b, 0) and hp == 0))

                    modulate1(0)
                    for w in range(2):
                        for t in range(NT):
                            copy_projection(w, w, t, FRONT_BANKS[NT * w + t])
                            square_projection(w, w, t)
                    high_q(0, 0)
                    high_k(0)
                    over_batches(act, batch)
                    act.wait_ge(s_ready, S_TILES * HP * B)
                    act.wait_ge(h2_kept, B - 1)
                    for q in range(H2_EARLY):
                        high_h2(q)
                    slot(B, 0, main=False)
                    for q in range(H2_EARLY, B - 1):
                        high_h2(q)
                    gate_y(LAST)
                    modulate2(LAST, 2 * B)
                    keep_h2(LAST)

                @block.vector
                def _(dve):
                    def sum_squares(u, half):
                        dve.wait_ge(sq_done, NT * u + 2 * half + 2)
                        if half == 0:
                            after(dve, qn_done, u)
                        nc.vector.reduce_sum(ss[:, 8 * half:8 * half + 8],
                                             sq[:, 2 * half:2 * half + 2].rearrange("p t (n d) -> p (t n) d", d=DH),
                                             AX.X).then_inc(ss_done, 1)

                    def guard_squares(u):
                        dve.wait_ge(ss_done, 2 * u + 2)
                        nc.vector.tensor_scalar(ss[:], ss[:], NORM_EPS ** 2, None, ALU.max).then_inc(ss_max, 1)

                    def guess_norms(u):
                        dve.wait_ge(ss_max, u + 1)
                        rsqrt_guess(nc, rn[:], ss_half[:], ss[:], rn_guess)

                    def low_q(u, hp):
                        dve.wait_ge(qh_done, u + 1)
                        nc.vector.scalar_tensor_tensor(out=parts[:, QL], in0=XT_BANK[:],
                                                       scalar=qk_scale[:, hp % HP:hp % HP + 1],
                                                       in1=parts[:, QH].bitcast(F32), op0=ALU.mult,
                                                       op1=ALU.subtract).then_inc(ql_done, 1)

                    def low_k(u):
                        dve.wait_ge(kh_done, u + 1)
                        nc.vector.tensor_tensor(parts[:, KL], XT_BANK[:], parts[:, KH].bitcast(F32),
                                                ALU.subtract).then_inc(kl_done, 1)

                    def row_max(u, i):
                        dve.wait_ge(s_ready, S_TILES * u + i + 1)
                        nc.vector.reduce_max(neg_max[:, i:i + 1], S_BANK[i % 3][:], AX.X, negate=True).then_inc(max_done, 1)

                    def copy_transposed(u, hp, i):
                        dve.wait_ge(t_ready, S_TILES * u + i + 1)
                        if i == 0:
                            after(dve, av_done, u - 1)
                        head, t = i // NT, i % NT
                        nc.vector.tensor_copy(probsT[:, hp % 2, head, :, t * P:(t + 1) * P],
                                              T_BANK[i % 2][:].rearrange("p (j q) -> p j q", j=NT)).then_inc(t_dve, 1)

                    def invert_sums(u, hp):
                        dve.wait_ge(p_done, S_TILES * (u + 1))
                        after(dve, wide_done, u - 1)
                        nc.vector.reciprocal(inv_sum[:, hp % 2], row_sum[:, hp % 2]).then_inc(inv_done, 1)

                    def normalise(u):
                        dve.wait_ge(av_done, u + 1)
                        dve.wait_ge(r_copied, u + 1)
                        after(dve, ol_done, u)
                        nc.vector.tensor_tensor(oT[:], O_BANK[:], inv_row[:], ALU.mult).then_inc(o_done, 1)

                    def high_o(u, hp, b):
                        dve.wait_ge(o_done, u + 1)
                        after(dve, y_ready, b)
                        nc.vector.tensor_copy(oT_h[:, hp % HP], oT[:]).then_inc(oh_done, 1)

                    def take_mod(dst, cols, b, done, free):
                        after(dve, *free)
                        for k, v in enumerate(cols):
                            last = nc.vector.tensor_copy(dst[:, k:k + 1], modT[:, v, bass.ts(b, 1)])
                        last.then_inc(done, 1)

                    def high_h1(b):
                        dve.wait_ge(h1_done, b + 1)
                        after(dve, pj_ready, NT * HP * b)
                        nc.vector.tensor_copy(hT_h[:], m_out[:]).then_inc(h1h_done, 1)

                    def low_h1(b):
                        dve.wait_ge(h1h_done, b + 1)
                        nc.vector.tensor_tensor(hT_l[:], m_out[:], hT_h[:].bitcast(F32), ALU.subtract).then_inc(hT_ready, 1)

                    def residual(b):
                        dve.wait_ge(yT_ready, b + 1)
                        rows = x1_all[:, bass.ts(b, NT)]
                        nc.vector.tensor_tensor(rows, M_BANK[:].rearrange("p (t c) -> p t c", t=NT), rows,
                                                ALU.add).then_inc(x1_done, 1)

                    def logits(b):
                        dve.wait_ge(z_ready, b + 1)
                        rows = z_all[:, bass.ts(b, NT)]
                        nc.vector.tensor_tensor(rows, M_BANK[:, 0:NT * E].rearrange("p (t e) -> p t e", t=NT),
                                                projb_row[:].unsqueeze(1).to_broadcast([P, NT, E]), ALU.add).then_inc(z_done, 1)

                    def slot(b, hp, main=True, tail=True):
                        u = HP * b + hp
                        front_a = main and not (is_const(b, LAST) and hp + 2 >= HP)
                        front_b = main and not (is_const(b, LAST) and hp + 1 >= HP)
                        for i in range(S_TILES):
                            if main and not is_const(b, 0) and (hp, i) == (2, 5):
                                dve.wait_ge(x1_done, b)
                            if main and not is_const(b, 0) and (hp, i) == (2, 6):
                                stats_there(dve, 2 * b)
                            if main and not is_const(b, LAST) and (hp, i) == (3, 7):
                                stats_there(dve, 2 * b + 1)
                            if main:
                                row_max(u, i)
                            if tail and i < P_LAG:
                                copy_transposed(u - 1, hp - 1, S_TILES - P_LAG + i)
                            if tail and i == 1:
                                invert_sums(u - 1, hp - 1)
                            if main and i == P_LAG:
                                copy_transposed(u, hp, 0)
                            if front_b and i == QT_AT + 1:
                                low_q(u + 1, hp + 1)
                            if front_b and i == KT_AT + 1:
                                low_k(u + 1)
                            if front_a and i in (3, 4):
                                sum_squares(u + 2, i - 3)
                            if front_a and i == 5:
                                guard_squares(u + 2)
                                guess_norms(u + 2)
                            if tail and i == 7:
                                normalise(u - 1)
                                high_o(u - 1, hp - 1, b if hp > 0 else b - 1)
                            if not is_const(b, 0) and main:
                                if (hp, i) == (0, 5):
                                    take_mod(mod2, (GA, GA_BO, CB, SB), b - 1, mod2_done, (h2_done, b - 1))
                                if (hp, i) == YT_AT:
                                    residual(b - 1)
                                if (hp, i) == (2, 5):
                                    tile_stats(b - 1)
                                if (hp, i) == (2, 6):
                                    aggregate(dve, 2 * b)
                                if (hp, i) == (2, 7):
                                    guess_std(dve, 2 * b)
                                if (hp, i) == (3, 5):
                                    ln_rows(dve, b - 1, 2 * b)
                                if (hp, i) == Z_AT:
                                    logits(b - 1)
                            if not is_const(b, LAST) and main:
                                nth = 2 * b + 1
                                if (hp, i) == (3, 6):
                                    tile_stats(b + 1)
                                    take_mod(mod1, (CA, SA), b + 1, mod1_done, (h1_done, b + 1))
                                if (hp, i) == (3, 7):
                                    aggregate(dve, nth)
                                if (hp, i) == (4, 0):
                                    guess_std(dve, nth)
                                if (hp, i) == (4, 5):
                                    ln_rows(dve, b + 1, nth)
                                if (hp, i) == (5, 5):
                                    high_h1(b + 1)
                                if (hp, i) == (5, 6):
                                    low_h1(b + 1)

                    def batch(b):
                        for hp in range(HP):
                            slot(b, hp, tail=not (is_const(b, 0) and hp == 0))

                    take_mod(mod1, (CA, SA), 0, mod1_done, (h1_done, 0))
                    high_h1(0)
                    low_h1(0)
                    for u in range(2):
                        sum_squares(u, 0)
                        sum_squares(u, 1)
                        guard_squares(u)
                        guess_norms(u)
                    low_q(0, 0)
                    low_k(0)
                    dve.wait_ge(x_in, 16)
                    over_batches(dve, batch)
                    slot(B, 0, main=False)
                    take_mod(mod2, (GA, GA_BO, CB, SB), LAST, mod2_done, (h2_done, LAST))
                    residual(LAST)
                    dve.wait_ge(x1_done, B)
                    tile_stats(LAST)
                    stats_there(dve, 2 * B - 1)
                    aggregate(dve, 2 * B - 1)
                    guess_std(dve, 2 * B - 1)
                    ln_rows(dve, LAST, 2 * B - 1)
                    logits(LAST)

                @block.gpsimd
                def _(pool):
                    def normalise_qk(u, hp):
                        pool.wait_ge(rn_guess, u + 1)
                        rsqrt_newton(nc, pool, rn[:], ss_half[:], rn_t[:], c15.to_broadcast([P, NT * 4]), rn_step, NEWTON_OPS * u)
                        pool.wait_ge(rn_step, NEWTON_OPS * (u + 1))
                        qk = qk_tok[:, hp % 2].rearrange("p t (n d) -> p (t n) d", d=DH)
                        nc.gpsimd.tensor_tensor(qk, qk, rn[:].unsqueeze(2).to_broadcast([P, NT * 4, DH]),
                                                ALU.mult).then_inc(qn_done, 1)

                    def widen(u, hp):
                        pool.wait_ge(inv_done, u + 1)
                        after(pool, r_ready, u)
                        src = inv_sum[:, hp % 2].rearrange("p (h t) -> p t h", h=2)
                        nc.gpsimd.tensor_tensor(inv_wide[:], src.unsqueeze(3).to_broadcast([P, NT, 2, DH]),
                                                c1.unsqueeze(2).unsqueeze(3).to_broadcast([P, NT, 2, DH]),
                                                ALU.mult).then_inc(wide_done, 1)

                    def low_o(u, hp):
                        pool.wait_ge(oh_done, u + 1)
                        nc.gpsimd.tensor_tensor(oT_l[:, hp % HP], oT[:], oT_h[:, hp % HP].bitcast(F32),
                                                ALU.subtract).then_inc(ol_done, 1)

                    def slot(b, hp, main=True, tail=True):
                        u = HP * b + hp
                        front_a = main and not (is_const(b, LAST) and hp + 2 >= HP)
                        if tail:
                            widen(u - 1, hp - 1)
                        if not is_const(b, 0) and main and hp == 3:
                            inverse_std(pool, 2 * b)
                        if not is_const(b, LAST) and main and hp == 4:
                            inverse_std(pool, 2 * b + 1)
                        if front_a:
                            normalise_qk(u + 2, hp + 2)
                        if tail:
                            low_o(u - 1, hp - 1)

                    def batch(b):
                        for hp in range(HP):
                            slot(b, hp, tail=not (is_const(b, 0) and hp == 0))

                    for u in range(2):
                        normalise_qk(u, u)
                    over_batches(pool, batch)
                    for q in range(H2_EARLY):
                        low_h2(pool, q)
                    slot(B, 0, main=False)
                    for q in range(H2_EARLY, H2_MID):
                        low_h2(pool, q)
                    inverse_std(pool, 2 * B - 1)
                    for q in range(H2_MID, B - 1):
                        low_h2(pool, q)

        with ExitStack() as scope:
            sb, pb, sem = alloc(scope)
            up_h = sb("up_h", [P, TILES, P], F32R)
            up_l = sb("up_l", [P, TILES, P], F32R)
            down_h = sb("down_h", [P, TILES, P], F32R)
            down_l = sb("down_l", [P, TILES, P], F32R)
            up_bias = sb("up_bias", [P, TILES])
            b2_pad = sb("b2_pad", [P, C])
            gates = sb("gates", [P, TT, E])
            gatesT = sb("gatesT", [P, TT * E // P, P])
            gate_cols = sb("gate_cols", [P, T])
            shared = sb("shared", [P, T])
            act_out = sb("act_out", [P, 4, N])
            hid_h = sb("hid_h", [P, 4, N], F32R)
            hid_l = sb("hid_l", [P, 4, N], F32R)
            gT2_copied = sem("gT2_copied")
            cols_zero = sem("cols_zero")
            gate_scratch = nc.dram_tensor("gate_scratch", [TT * E, P], F32).ap()
            scratch_rows = gate_scratch.rearrange("(t e) k -> e t k", e=E)

            with ExitStack() as scope2:
                sb, pb, sem = alloc(scope2)
                s_bias = sem("s_bias")
                s_zero = sem("s_zero")
                s_wt = sem("s_wt2")
                s_wh = sem("s_wh2")
                s_wl = sem("s_wl2")
                s_sig = sem("s_sig")
                rt = sem("rt")
                consts = sem("consts")
                count_in = sem("count_in")
                count_out = sem("count_out")
                thr = sem("thr")
                fin_in = sem("fin_in")
                fin_out = sem("fin_out")
                gates_done = sem("gates_done")
                gT2_ready = sem("gT2_ready")
                up2_ready = sem("up2_ready")
                gelu2_done = sem("gelu2_done")
                hi2_done = sem("hi2_done")
                lo2_done = sem("lo2_done")
                down2_done = sem("down2_done")
                shared_kept = sem("shared_kept")

                def rt_tile(name, shape=(P, TT, E), dt=F32):
                    return sb(name, list(shape), dt)

                prob = rt_tile("prob")
                t1 = rt_tile("t1")
                t2 = rt_tile("t2")
                top1 = rt_tile("top1")
                top2 = rt_tile("top2")
                m1 = rt_tile("m1", (P, TT))
                m2 = rt_tile("m2", (P, TT))
                den = rt_tile("den", (P, TT))
                w1 = rt_tile("w1", (P, TT))
                w2 = rt_tile("w2", (P, TT))
                ranked = rt_tile("ranked", (P, E, TT))
                above = rt_tile("above", (P, E, TT))
                equal = rt_tile("equal", (P, E, TT))
                before = beyond_raw[:, 3 * E * TT:4 * E * TT].rearrange("p (e t) -> p e t", e=E)
                not_first = t2[:].rearrange("p t e -> p (t e)").rearrange("p (e t) -> p e t", e=E)
                gelu_warm = sb("gelu_warm", [P, 1])
                rev = rt_tile("rev", (P, E))
                rev_i = rt_tile("rev_i", (P, E), I32)
                ones = rt_tile("ones", (P, P))
                earlier = rt_tile("earlier", (P, P))
                thr_u = rt_tile("thr_u", (P, E), U32)
                digit = rt_tile("digit", (P, 3, E))
                next_digit = rt_tile("next_digit", (P, 3, E))
                digit_u = rt_tile("digit_u", (P, 3, E), U32)
                less_u = rt_tile("less_u", (P, 3, E), U32)
                cand_u = rt_tile("cand_u", (P, 3, E), U32)
                at_least = beyond_raw[:, 0:3 * E * TT].rearrange("p (j e t) -> p j e t", j=3, e=E)
                enough = rt_tile("enough", (P, 3, E))
                inc_u = rt_tile("inc_u", (P, E), U32)
                part_count = rt_tile("part_count", (P, 3, E))
                room = rt_tile("room", (P, E))
                BITS = 30
                SEARCHES = BITS // 2
                assert SHT % 2 == 0 and SHT * (B - 1) // 2 <= SEARCHES <= SHT * B // 2

                def by_expert(tile):
                    return tile[:].rearrange("p t e -> p e t")

                def weight_group(j):
                    low, high, raw = (up_l, up_h, raw_up) if j % 2 == 0 else (down_l, down_h, raw_down)
                    k = 4 * (j // 2)
                    flat = [w[:, k:k + 4].rearrange("p r c -> p (r c)") for w in (low, high)]
                    return flat[0], flat[1], act_out[:, j % 2], raw[:, k:k + 4]

                GROUPS = 2 * TILES // 4
                LAG2 = 2
                FIN_BANKS, COUNT_BANK = bank[4:7], bank[7]
                H2_BANK, Y2_BANK = bank[0:2], bank[2]

                def chunks(engine, chunk):
                    chunk(0)
                    with engine.Fori(1, B) as c:
                        chunk(c)

                def first_chunk(c):
                    return isinstance(c, int) and c == 0

                with nc.Block() as block:
                    @block.sync
                    def _(sp):
                        sp.dma_start(up_bias[:, 0:SHT], sh1_b.rearrange("(r p) -> p r", p=P)).then_inc(s_bias, 16)
                        sp.dma_start(up_bias[:, SHT:], fc1_b.rearrange("e (r p) -> p (e r)", p=P)).then_inc(s_bias, 16)
                        sp.wait_ge(s_zero, 1)
                        sp.dma_start(b2_pad[0:E, :], fc2_b).then_inc(s_bias, 16)
                        sp.wait_ge(s_bias, 48)

                    @block.gpsimd
                    def _(pool):
                        nc.gpsimd.memset(b2_pad[:], 0.0).then_inc(s_zero, 1)
                        nc.gpsimd.iota(rev_i[:], pattern=[[-1, E]], base=E, channel_multiplier=0).then_inc(consts, 1)
                        nc.gpsimd.memset(ones[:], 1.0).then_inc(consts, 1)
                        pool.wait_ge(consts, 2)
                        nc.gpsimd.affine_select(out=earlier[:], in_=ones[:], compare_op=ALU.is_gt, fill=0.0,
                                                base=0, pattern=[[1, P]], channel_multiplier=-1).then_inc(consts, 1)
                        def split_group(j):
                            pool.wait_ge(s_wh, 2 * j + 2)
                            dst, hi, full, _ = weight_group(j)
                            nc.gpsimd.tensor_tensor(dst, full, hi.bitcast(F32), ALU.subtract).then_inc(s_wl, 1)

                        def chunk(c):
                            for k in range(SHT):
                                n = SHT * c + k
                                pool.wait_ge(hi2_done, n + 1)
                                nc.gpsimd.tensor_tensor(hid_l[:, k], act_out[:, k], hid_h[:, k].bitcast(F32),
                                                        ALU.subtract).then_inc(lo2_done, 1)

                        low_h2(pool, B - 1)
                        for j in range(GROUPS):
                            split_group(j)
                        nc.gpsimd.memset(gate_cols[:], 0.0).then_inc(cols_zero, 1)
                        chunks(pool, chunk)

                    @block.tensor
                    def _(pe):
                        def transpose_weights(j):
                            if j == 0:
                                pe.wait_ge(s_shared, 32)
                            if j == 2:
                                pe.wait_ge(s_up, 16)
                                pe.wait_ge(s_down, 16)
                            after(pe, s_wh, 2 * (j - 3))
                            raw = weight_group(j)[3]
                            for r in range(4):
                                last = nc.tensor.transpose(bank[j % 4][:, r * P:(r + 1) * P], raw[:, r], ident[:])
                            last.then_inc(s_wt, 1)

                        def count(m):
                            pe.wait_ge(count_in, m + 1)
                            nc.tensor.matmul(COUNT_BANK[:, 0:3 * E], ones[:], part_count[:].rearrange("p j e -> p (j e)"),
                                             start=True, stop=True).then_inc(count_out, 1)

                        def up(c, k):
                            after(pe, gelu2_done, SHT * c + k - 1)
                            if k == 0:
                                pe.wait_ge(s_h2l, c + 1)
                            cols = bass.ts(c, N)
                            nc.tensor.matmul(H2_BANK[k % 2][:], up_h[:, k], h2_h[:, cols], start=True, stop=False)
                            nc.tensor.matmul(H2_BANK[k % 2][:], up_l[:, k], h2_h[:, cols], start=False, stop=False)
                            nc.tensor.matmul(H2_BANK[k % 2][:], up_h[:, k], h2_l[:, cols], start=False,
                                             stop=True).then_inc(up2_ready, 1)

                        def down(c, k):
                            if k == 0:
                                after(pe, shared_kept, c)
                            pe.wait_ge(lo2_done, SHT * c + k + 1)
                            nc.tensor.matmul(Y2_BANK[:], down_h[:, k], hid_h[:, k], start=(k == 0), stop=False)
                            nc.tensor.matmul(Y2_BANK[:], down_l[:, k], hid_h[:, k], start=False, stop=False)
                            nc.tensor.matmul(Y2_BANK[:], down_h[:, k], hid_l[:, k], start=False,
                                             stop=(k == SHT - 1)).then_inc(down2_done, 1)

                        def chunk(c):
                            for k in range(SHT):
                                if k % 2 == 0 and not (isinstance(c, int) and SHT * c // 2 + k // 2 >= SEARCHES):
                                    count(SHT // 2 * c + k // 2)
                                up(c, k)
                                if k >= LAG2:
                                    down(c, k - LAG2)
                                elif not first_chunk(c):
                                    down(c - 1, SHT + k - LAG2)

                        for j in range(GROUPS):
                            transpose_weights(j)
                        pe.wait_ge(s_wh, 2 * GROUPS)
                        pe.wait_ge(s_wl, GROUPS)
                        pe.wait_ge(consts, 3)
                        chunk(0)
                        with pe.Fori(1, B - 1) as c:
                            chunk(c)
                        chunk(B - 1)
                        pe.wait_ge(fin_in, 1)
                        nc.tensor.matmul(FIN_BANKS[2][:, 0:E], ones[:], part_count[:, 0], start=True, stop=True).then_inc(fin_out, 1)
                        nc.tensor.matmul(FIN_BANKS[1][:, 0:E * TT], ones[:], equal[:].rearrange("p e t -> p (e t)"),
                                         start=True, stop=True).then_inc(fin_out, 1)
                        nc.tensor.matmul(FIN_BANKS[0][:, 0:E * TT], earlier[:], equal[:].rearrange("p e t -> p (e t)"),
                                         start=True, stop=True).then_inc(fin_out, 1)
                        for k in range(SHT - LAG2, SHT):
                            down(B - 1, k)
                        pe.wait_ge(gates_done, 1)
                        for h in range(TT * E // P):
                            last = nc.tensor.transpose(COUNT_BANK[:, h * P:(h + 1) * P],
                                                       gates[:].rearrange("p t e -> p (t e)")[:, h * P:(h + 1) * P], ident[:])
                        last.then_inc(gT2_ready, 1)

                    @block.scalar
                    def _(act):
                        nc.scalar.activation(t1[:], z_all[:], ACT.Exp, scale=-1.0).then_inc(s_sig, 1)
                        def high_group(j):
                            act.wait_ge(s_wt, j + 1)
                            after(act, s_wl, j - 1)
                            _, hi, full, _ = weight_group(j)
                            nc.scalar.activation(full, bank[j % 4][:], ACT.Copy).then_inc(s_wh, 1)
                            nc.scalar.activation(hi, bank[j % 4][:], ACT.Copy).then_inc(s_wh, 1)

                        def keep(c):
                            act.wait_ge(down2_done, SHT * (c + 1))
                            nc.scalar.activation(shared[:, bass.ts(c, N)], Y2_BANK[:], ACT.Copy).then_inc(shared_kept, 1)

                        def chunk(c):
                            for k in range(SHT):
                                n = SHT * c + k
                                if k == LAG2 and not first_chunk(c):
                                    keep(c - 1)
                                act.wait_ge(up2_ready, n + 1)
                                after(act, lo2_done, n - 3)
                                nc.scalar.activation(act_out[:, k], H2_BANK[k % 2][:], ACT.Gelu,
                                                     bias=up_bias[:, k:k + 1]).then_inc(gelu2_done, 1)
                                act.wait_ge(gelu2_done, n + 1)
                                after(act, down2_done, n - 3)
                                nc.scalar.activation(hid_h[:, k], act_out[:, k], ACT.Copy).then_inc(hi2_done, 1)

                        high_h2(B - 1)
                        for j in range(GROUPS):
                            high_group(j)
                        act.wait_ge(s_bias, 48)
                        nc.scalar.activation(gelu_warm[:], up_bias[:, 0:1], ACT.Gelu)
                        chunks(act, chunk)
                        keep(B - 1)
                        act.wait_ge(gT2_ready, 1)
                        nc.scalar.activation(gatesT[:].rearrange("p h k -> p (h k)"), COUNT_BANK[:, 0:TT * E],
                                             ACT.Copy).then_inc(gT2_copied, 1)

                    @block.vector
                    def _(dve):
                        steps = [0]

                        def link(instruction, wait=True):
                            steps[0] += 1
                            instruction.then_inc(rt, 1)
                            if wait:
                                dve.wait_ge(rt, steps[0])

                        def spread(row):
                            return row[:].unsqueeze(2).to_broadcast([P, TT, E])

                        link(nc.vector.memset(thr_u[:], 0))
                        for j in range(3):
                            link(nc.vector.memset(digit[:, j], float((j + 1) * 2 ** (BITS - 2))))
                        link(nc.vector.tensor_copy(cand_u[:], digit[:]))
                        dve.wait_ge(consts, 3)
                        link(nc.vector.tensor_copy(rev[:], rev_i[:]))
                        rev_all = rev[:].unsqueeze(1).to_broadcast([P, TT, E])
                        dve.wait_ge(s_sig, 1)
                        link(nc.vector.tensor_scalar(t1[:], t1[:], 1.0, None, ALU.add))
                        link(nc.vector.reciprocal(t1[:], t1[:]))
                        link(nc.vector.tensor_tensor(t1[:], t1[:], ebias_row[:].unsqueeze(1).to_broadcast([P, TT, E]), ALU.add))
                        link(nc.vector.tensor_scalar(t1[:], t1[:], CLIP, None, ALU.max))
                        link(nc.vector.reduce_max(m1[:], t1[:], AX.X))
                        link(nc.vector.reciprocal(m1[:], m1[:]))
                        link(nc.vector.tensor_tensor(t1[:], t1[:], spread(m1), ALU.mult))
                        link(nc.vector.reduce_sum(m1[:], t1[:], AX.X))
                        link(nc.vector.reciprocal(m1[:], m1[:]))
                        link(nc.vector.tensor_tensor(prob[:], t1[:], spread(m1), ALU.mult))

                        def first_max(values, best, choice):
                            link(nc.vector.reduce_max(best[:], values[:], AX.X))
                            link(nc.vector.tensor_tensor(t2[:], values[:], spread(best), ALU.is_equal))
                            link(nc.vector.tensor_tensor(t2[:], t2[:], rev_all, ALU.mult))
                            link(nc.vector.reduce_max(den[:], t2[:], AX.X))
                            link(nc.vector.tensor_tensor(choice[:], rev_all, spread(den), ALU.is_equal))

                        first_max(prob, m1, top1)
                        link(nc.vector.scalar_tensor_tensor(out=t1[:], in0=top1[:], scalar=-2.0, in1=prob[:],
                                                            op0=ALU.mult, op1=ALU.add))
                        first_max(t1, m2, top2)
                        link(nc.vector.tensor_tensor(den[:], m1[:], m2[:], ALU.add))
                        link(nc.vector.tensor_scalar(den[:], den[:], CLIP, None, ALU.max))
                        link(nc.vector.reciprocal(den[:], den[:]))
                        link(nc.vector.tensor_tensor(w1[:], m1[:], den[:], ALU.mult), wait=False)
                        link(nc.vector.tensor_tensor(w2[:], m2[:], den[:], ALU.mult))
                        link(nc.vector.tensor_tensor(t1[:], top1[:], spread(w1), ALU.mult), wait=False)
                        link(nc.vector.tensor_tensor(t2[:], top2[:], spread(w2), ALU.mult))
                        link(nc.vector.tensor_tensor(prob[:], t1[:], t2[:], ALU.add))
                        link(nc.vector.tensor_tensor(t1[:], top1[:], top2[:], ALU.add))
                        link(nc.vector.scalar_tensor_tensor(out=ranked[:], in0=by_expert(t1), scalar=-1.0,
                                                            in1=by_expert(prob), op0=ALU.add, op1=ALU.add))

                        def search(m):
                            nc.vector.tensor_tensor(at_least, ranked[:].unsqueeze(1).to_broadcast([P, 3, E, TT]),
                                                    cand_u[:].bitcast(F32).unsqueeze(3).to_broadcast([P, 3, E, TT]),
                                                    ALU.is_ge).then_inc(thr, 1)
                            dve.wait_ge(thr, 8 * m + 1)
                            nc.vector.reduce_sum(part_count[:], at_least, AX.X).then_inc(count_in, 1)
                            nc.vector.tensor_scalar(next_digit[:], digit[:], 0.25, None, ALU.mult).then_inc(thr, 1)
                            dve.wait_ge(thr, 8 * m + 2)
                            nc.vector.tensor_copy(digit_u[:], next_digit[:]).then_inc(thr, 1)
                            dve.wait_ge(thr, 8 * m + 3)
                            nc.vector.tensor_tensor(less_u[:], thr_u[:].unsqueeze(1).to_broadcast([P, 3, E]), digit_u[:],
                                                    ALU.bitwise_or).then_inc(thr, 1)
                            dve.wait_ge(count_out, m + 1)
                            nc.vector.scalar_tensor_tensor(out=enough[:],
                                                           in0=COUNT_BANK[:, 0:3 * E].rearrange("p (j e) -> p j e", j=3),
                                                           scalar=float(CAP), in1=digit[:],
                                                           op0=ALU.is_ge, op1=ALU.mult).then_inc(thr, 1)
                            dve.wait_ge(thr, 8 * m + 5)
                            nc.vector.reduce_max(inc_u[:], enough[:].rearrange("p j e -> p e j"), AX.X).then_inc(thr, 1)
                            dve.wait_ge(thr, 8 * m + 6)
                            nc.vector.tensor_tensor(cand_u[:], less_u[:], inc_u[:].unsqueeze(1).to_broadcast([P, 3, E]),
                                                    ALU.bitwise_or).then_inc(thr, 1)
                            nc.vector.tensor_tensor(thr_u[:], thr_u[:], inc_u[:], ALU.bitwise_or)
                            nc.vector.tensor_scalar(digit[:], digit[:], 0.25, None, ALU.mult).then_inc(thr, 1)
                            dve.wait_ge(thr, 8 * m + 8)

                        for m in range(SHT // 2):
                            search(m)
                        with dve.Fori(1, B - 1) as c:
                            for k in range(SHT // 2):
                                search(SHT // 2 * c + k)
                        for m in range(SHT * (B - 1) // 2, SEARCHES):
                            search(m)

                        thr_all = thr_u[:].bitcast(F32).unsqueeze(2).to_broadcast([P, E, TT])
                        link(nc.vector.tensor_tensor(above[:], ranked[:], thr_all, ALU.is_gt), wait=False)
                        link(nc.vector.tensor_tensor(equal[:], ranked[:], thr_all, ALU.is_equal))
                        link(nc.vector.memset(not_first, 1.0))
                        link(nc.vector.memset(not_first[:, :, 0:1], 0.0))
                        nc.vector.reduce_sum(part_count[:, 0], above[:], AX.X).then_inc(fin_in, 1)
                        dve.wait_ge(fin_out, 3)
                        link(nc.vector.tensor_scalar(room[:], FIN_BANKS[2][:, 0:E], -1.0, float(CAP), ALU.mult, ALU.add), wait=False)
                        link(nc.vector.tensor_copy(before, FIN_BANKS[1][:, 0:E * TT].rearrange("p (e t) -> p e t", e=E)))
                        link(nc.vector.tensor_tensor_scan(t1[:].rearrange("p t e -> p (t e)"),
                                                          not_first.rearrange("p e t -> p (e t)"),
                                                          before.rearrange("p e t -> p (e t)"), 0.0, ALU.mult, ALU.add))
                        flat1 = t1[:].rearrange("p t e -> p (t e)").rearrange("p (e t) -> p e t", e=E)
                        link(nc.vector.tensor_tensor(before, flat1, before, ALU.subtract))
                        link(nc.vector.tensor_tensor(before, FIN_BANKS[0][:, 0:E * TT].rearrange("p (e t) -> p e t", e=E),
                                                     before, ALU.add))
                        link(nc.vector.tensor_tensor(before, before, room[:].unsqueeze(2).to_broadcast([P, E, TT]), ALU.is_lt))
                        link(nc.vector.tensor_tensor(before, before, equal[:], ALU.mult))
                        link(nc.vector.tensor_tensor(above[:], above[:], before, ALU.add))
                        nc.vector.tensor_tensor(by_expert(gates), above[:], by_expert(prob), ALU.mult).then_inc(gates_done, 1)

            sb, pb, sem = alloc(scope)
            ET = TILES - SHT
            LAG = 4
            gated = sb("gated", [P, 4, N])
            mod3 = sb("mod3", [P, 2])
            H_BANK, Y_BANK, Z_BANK = bank[0:4], bank[4], bank[6]
            gT2_out = sem("gT2_out")
            gT2_in = sem("gT2_in")
            rows_in = [sem(f"rows_in{e}") for e in range(E)]
            ysum_done = sem("ysum_done")
            up_ready = sem("up_ready")
            gelu_done = sem("gelu_done")
            gated_done = sem("gated_done")
            hi_done = sem("hi_done")
            lo_even = sem("lo_even")
            lo_odd = sem("lo_odd")
            down_done = sem("down_done")
            mod3_done = sem("mod3_done")
            yc_done = sem("yc_done")
            z3_ready = sem("z3_ready")
            out_done = sem("out_done")
            stored = sem("stored")

            def over_all(engine, batch):
                batch(0)
                with engine.Fori(1, B) as b:
                    batch(b)

            def none_before(b):
                return isinstance(b, int) and b == 0

            with nc.Block() as block:
                @block.sync
                def _(sp):
                    def store(b):
                        sp.wait_ge(out_done, b + 1)
                        sp.dma_start(out_tok[bass.ds(b, 1)].rearrange("o p t c -> p (o t) c"),
                                     x1_all[:, bass.ts(b, NT)]).then_inc(stored, 16)

                    def load_gates(b, e):
                        after(sp, gated_done, ET * (b - 1) + 2 * (e + 1))
                        sp.dma_start(gate_rows[:, e].rearrange("p (t k) -> p t k", t=NT),
                                     scratch_rows[e, bass.ts(b, NT)].partition_broadcast(P)).then_inc(rows_in[e], 16)

                    def batch(b, store_too=True):
                        for e in range(E):
                            if e == E // 2 and store_too:
                                store(b - 2)
                            load_gates(b, e)

                    sp.wait_ge(gT2_copied, 1)
                    sp.dma_start(gate_scratch.rearrange("(h p) k -> p h k", p=P), gatesT[:]).then_inc(gT2_out, 16)
                    sp.wait_ge(gT2_out, 16)
                    load_gates(0, 0)
                    sp.wait_ge(cols_zero, 1)
                    sp.dma_start(gate_cols[0:E].rearrange("e (t k) -> e t k", k=P), scratch_rows).then_inc(gT2_in, 16)
                    for e in range(1, E):
                        load_gates(0, e)
                    batch(1, False)
                    with sp.Fori(2, B) as b:
                        batch(b)
                    store(B - 2)
                    store(B - 1)
                    sp.wait_ge(stored, 16 * B)

                @block.tensor
                def _(pe):
                    def up(b, k):
                        after(pe, gelu_done, ET * b + k - 3)
                        cols = bass.ts(b, N)
                        o, w = H_BANK[k % 4][:], SHT + k
                        nc.tensor.matmul(o, up_h[:, w], h2_h[:, cols], start=True, stop=False)
                        nc.tensor.matmul(o, up_l[:, w], h2_h[:, cols], start=False, stop=False)
                        nc.tensor.matmul(o, up_h[:, w], h2_l[:, cols], start=False, stop=True).then_inc(up_ready, 1)

                    def down(b, k):
                        if k == 0:
                            after(pe, ysum_done, b)
                            if none_before(b):
                                pe.wait_ge(gT2_in, 16)
                            nc.tensor.matmul(Y_BANK[:], b2_pad[:], gate_cols[:, bass.ts(b, N)], start=True, stop=False)
                        pe.wait_ge((lo_even, lo_odd)[k % 2], ET // 2 * b + k // 2 + 1)
                        w = SHT + k
                        nc.tensor.matmul(Y_BANK[:], down_h[:, w], hid_h[:, k % 4], start=False, stop=False)
                        nc.tensor.matmul(Y_BANK[:], down_l[:, w], hid_h[:, k % 4], start=False, stop=False)
                        nc.tensor.matmul(Y_BANK[:], down_h[:, w], hid_l[:, k % 4], start=False,
                                         stop=(k == ET - 1)).then_inc(down_done, 1)

                    def back_to_tokens(b):
                        pe.wait_ge(yc_done, b + 1)
                        after(pe, out_done, b)
                        for t in range(NT):
                            last = nc.tensor.transpose(Z_BANK[:, t * P:(t + 1) * P], yT[:, t * P:(t + 1) * P], ident[:])
                        last.then_inc(z3_ready, 1)

                    def batch(b):
                        for k in range(ET):
                            if k == LAG - 1 and not none_before(b):
                                down(b - 1, ET - 1)
                            up(b, k)
                            if k >= LAG:
                                down(b, k - LAG)
                            elif k < LAG - 1 and not none_before(b):
                                down(b - 1, ET + k - LAG)
                            if k == 8 and not none_before(b):
                                back_to_tokens(b - 1)

                    over_all(pe, batch)
                    for k in range(ET - LAG, ET):
                        down(B - 1, k)
                    back_to_tokens(B - 1)

                @block.scalar
                def _(act):
                    def high(b, k):
                        n = ET * b + k
                        act.wait_ge(gated_done, n + 1)
                        after(act, down_done, n - 3)
                        nc.scalar.activation(hid_h[:, k % 4], gated[:, k % 4], ACT.Copy).then_inc(hi_done, 1)

                    def take_sum(b):
                        act.wait_ge(ysum_done, b + 1)
                        act.wait_ge(mod3_done, b + 1)
                        after(act, z3_ready, b)
                        nc.scalar.activation(yT[:], y_sum[:], ACT.Identity, scale=mod3[:, 0:1],
                                             bias=mod3[:, 1:2]).then_inc(yc_done, 1)

                    def batch(b):
                        for k in range(ET):
                            n = ET * b + k
                            act.wait_ge(up_ready, n + 1)
                            after(act, gated_done, n - 3)
                            nc.scalar.activation(act_out[:, k % 4], H_BANK[k % 4][:], ACT.Gelu,
                                                 bias=up_bias[:, SHT + k:SHT + k + 1]).then_inc(gelu_done, 1)
                            if k >= 1:
                                high(b, k - 1)
                            elif not none_before(b):
                                high(b - 1, ET - 1)
                            if k == 6 and not none_before(b):
                                take_sum(b - 1)

                    over_all(act, batch)
                    high(B - 1, ET - 1)
                    take_sum(B - 1)

                @block.vector
                def _(dve):
                    def low(b, k):
                        dve.wait_ge(hi_done, ET * b + k + 1)
                        nc.vector.tensor_tensor(hid_l[:, k % 4], gated[:, k % 4], hid_h[:, k % 4].bitcast(F32),
                                                ALU.subtract).then_inc(lo_odd, 1)

                    def add_shared(b):
                        dve.wait_ge(down_done, ET * (b + 1))
                        after(dve, yc_done, b)
                        nc.vector.tensor_tensor(y_sum[:], Y_BANK[:], shared[:, bass.ts(b, N)], ALU.add).then_inc(ysum_done, 1)

                    def take_mod3(b):
                        after(dve, yc_done, b)
                        for j, v in enumerate((GB, GB_B2)):
                            last = nc.vector.tensor_copy(mod3[:, j:j + 1], modT[:, v, bass.ts(b, 1)])
                        last.then_inc(mod3_done, 1)

                    def add_residual(b):
                        dve.wait_ge(z3_ready, b + 1)
                        rows = x1_all[:, bass.ts(b, NT)]
                        nc.vector.tensor_tensor(rows, Z_BANK[:].rearrange("p (t c) -> p t c", t=NT), rows,
                                                ALU.add).then_inc(out_done, 1)

                    def batch(b):
                        for k in range(ET):
                            n = ET * b + k
                            if k % 2 == 0:
                                dve.wait_ge(rows_in[k // 2], 16 * (b + 1))
                            if k == LAG - 1 and not none_before(b):
                                add_shared(b - 1)
                            dve.wait_ge(gelu_done, n + 1)
                            after(dve, (lo_even, lo_odd)[k % 2], ET // 2 * b + k // 2 - 1)
                            nc.vector.tensor_tensor(gated[:, k % 4], gate_rows[:, k // 2], act_out[:, k % 4],
                                                    ALU.mult).then_inc(gated_done, 1)
                            if k % 2 == 0 and k > 0:
                                low(b, k - 1)
                            elif k == 0 and not none_before(b):
                                low(b - 1, ET - 1)
                            if k == LAG and not none_before(b):
                                take_mod3(b - 1)
                            if k == 10 and not none_before(b):
                                add_residual(b - 1)

                    over_all(dve, batch)
                    low(B - 1, ET - 1)
                    add_shared(B - 1)
                    take_mod3(B - 1)
                    add_residual(B - 1)

                @block.gpsimd
                def _(pool):
                    def batch(b):
                        for k in range(0, ET, 2):
                            pool.wait_ge(hi_done, ET * b + k + 1)
                            nc.gpsimd.tensor_tensor(hid_l[:, k % 4], gated[:, k % 4], hid_h[:, k % 4].bitcast(F32),
                                                    ALU.subtract).then_inc(lo_even, 1)

                    over_all(pool, batch)


_INS = ["L0_attn_x", "L0_attn_Wq", "L0_attn_Wk", "L0_attn_Wv", "L0_attn_Wo", "L0_attn_bo", "L0_attn_q_scale",
        "L0_attn_k_scale", "L0_ffn_proj_w", "L0_ffn_proj_b", "L0_ffn_expert_bias", "L0_ffn_fc1_w", "L0_ffn_fc1_b",
        "L0_ffn_fc2_w", "L0_ffn_fc2_b", "L0_ffn_sh1_w", "L0_ffn_sh1_b", "L0_ffn_sh2_w", "L0_ffn_sh2_b", "L0_c",
        "L0_wmod"]


def kernel(**inputs):
    import numpy as np
    import concourse.bacc as bacc
    from concourse.bass_utils import run_bass_kernel_spmd

    nc = bacc.Bacc("TRN2", target_bir_lowering=False, num_devices=1)
    arrays, args = {}, []
    for name in _INS:
        a = np.ascontiguousarray(inputs[name])
        arrays[f"in_{name}"] = a
        args.append(nc.dram_tensor(f"in_{name}", a.shape, mybir.dt.from_np(a.dtype), kind="ExternalInput").ap())
    shape = arrays["in_L0_attn_x"].shape
    args.append(nc.dram_tensor("out_0", shape, F32, kind="ExternalOutput").ap())
    adaln_attention_moe(nc, *args)
    r = run_bass_kernel_spmd(nc, [arrays], core_ids=[0])
    return r.results[0]["out_0"]
```
